# Optimizing a Trainium2 kernel written in Bass

```python
import numpy as np
import jax
import jax.numpy as jnp

def _softmax(x, axis=-1):
    return jax.nn.softmax(x, axis=axis)

def _gelu(x):
    return jax.nn.gelu(x, approximate=True)

def _silu(x):
    return jax.nn.silu(x)

def _sigmoid(x):
    return jax.nn.sigmoid(x)

def _layernorm(x, axis=-1, eps=1e-05):
    m = jnp.mean(x, axis=axis, keepdims=True)
    v = jnp.var(x, axis=axis, keepdims=True)
    return (x - m) / jnp.sqrt(v + eps)

def _scatter_add(tgt, idx, src, axis=0):
    return tgt.at[idx].add(src)

def _segment_sum(src, seg, n):
    return jax.ops.segment_sum(src, seg, n)
kernel_name = 'mk_adaln_d1_jaxref_r8_8ffec9'

def setup_inputs(seed: int=0):
    np.random.seed(seed)
    _w = jnp.asarray

    def _L0_attn_setup():
        import jax, jax.numpy as jnp
        import numpy as np
        B, S, HID = (1, 256, 256)
        H, KVH, HD = (32, 8, 64)
        THETA = 10000.0

        def _rotate_half(x):
            x1, x2 = jnp.split(x, 2, axis=-1)
            return jnp.concatenate([-x2, x1], axis=-1)

        def _rope_cos_sin(seq_len, head_dim, theta, dtype):
            inv_freq = 1.0 / theta ** (jnp.arange(0, head_dim, 2, dtype=jnp.float32) / head_dim)
            pos = jnp.arange(seq_len, dtype=jnp.float32)
            freqs = pos[:, None] * inv_freq[None, :]
            emb = jnp.concatenate([freqs, freqs], axis=-1)
            return (jnp.cos(emb).astype(dtype), jnp.sin(emb).astype(dtype))
        key = jax.random.key(seed)
        k0, k1, k2, k3, k4 = jax.random.split(key, 5)
        w = lambda k, shape: jax.random.normal(k, shape, dtype=jnp.float32) * 0.02
        return {'hidden_states': jax.random.normal(k0, (B, S, HID), dtype=jnp.float32), 'Wq': w(k1, (H * HD, HID)), 'Wk': w(k2, (KVH * HD, HID)), 'Wv': w(k3, (KVH * HD, HID)), 'Wo': w(k4, (HID, H * HD))}
    _L0_attn_in = _L0_attn_setup()

    def _L0_ffn_setup():
        import jax, jax.numpy as jnp
        import numpy as np
        TOP_K = 2
        LORA_SCALE = 32.0 / 16.0
        key = jax.random.key(seed)
        ks = jax.random.split(key, 11)
        B, S, D, F, E, R = (4, 128, 256, 704, 8, 16)
        sd, sf = (1.0 / np.sqrt(D), 1.0 / np.sqrt(F))
        return {'x': jax.random.normal(ks[0], (B, S, D), jnp.float32), 'gate_w': jax.random.normal(ks[1], (E, D), jnp.float32) * 0.02, 'w1': jax.random.normal(ks[2], (F, D), jnp.float32) * sd, 'w3': jax.random.normal(ks[3], (F, D), jnp.float32) * sd, 'w2': jax.random.normal(ks[4], (D, F), jnp.float32) * sf, 'a1': jax.random.normal(ks[5], (E, R, D), jnp.float32) * sd, 'b1': jax.random.normal(ks[6], (E, F, R), jnp.float32) * 0.01, 'a3': jax.random.normal(ks[7], (E, R, D), jnp.float32) * sd, 'b3': jax.random.normal(ks[8], (E, F, R), jnp.float32) * 0.01, 'a2': jax.random.normal(ks[9], (E, R, F), jnp.float32) * sf, 'b2': jax.random.normal(ks[10], (E, D, R), jnp.float32) * 0.01}
    _L0_ffn_in = _L0_ffn_setup()
    _L0_c = _w((lambda *s: np.random.randn(*s).astype(np.float32) * 0.05)(2, 256))
    _L0_wmod = _w((lambda *s: np.random.randn(*s).astype(np.float32) * 0.05)(256, 6 * 256) * 256 ** (-0.5))
    _d = {'L0_attn_hidden_states': _L0_attn_in['hidden_states'], 'L0_attn_Wq': _L0_attn_in['Wq'], 'L0_attn_Wk': _L0_attn_in['Wk'], 'L0_attn_Wv': _L0_attn_in['Wv'], 'L0_attn_Wo': _L0_attn_in['Wo'], 'L0_ffn_gate_w': _L0_ffn_in['gate_w'], 'L0_ffn_w1': _L0_ffn_in['w1'], 'L0_ffn_w3': _L0_ffn_in['w3'], 'L0_ffn_w2': _L0_ffn_in['w2'], 'L0_ffn_a1': _L0_ffn_in['a1'], 'L0_ffn_b1': _L0_ffn_in['b1'], 'L0_ffn_a3': _L0_ffn_in['a3'], 'L0_ffn_b3': _L0_ffn_in['b3'], 'L0_ffn_a2': _L0_ffn_in['a2'], 'L0_ffn_b2': _L0_ffn_in['b2'], 'L0_c': _L0_c, 'L0_wmod': _L0_wmod}
    _x0 = _d['L0_attn_hidden_states']
    _d['L0_attn_hidden_states'] = jax.random.normal(jax.random.fold_in(jax.random.key(seed), 1), (2, 512, 256), dtype=_x0.dtype)
    del _x0
    return _d

def reference(L0_attn_hidden_states, L0_attn_Wq, L0_attn_Wk, L0_attn_Wv, L0_attn_Wo, L0_ffn_gate_w, L0_ffn_w1, L0_ffn_w3, L0_ffn_w2, L0_ffn_a1, L0_ffn_b1, L0_ffn_a3, L0_ffn_b3, L0_ffn_a2, L0_ffn_b2, L0_c, L0_wmod):

    def _L0_attn_ref(hidden_states, Wq, Wk, Wv, Wo):
        import jax, jax.numpy as jnp
        import numpy as np
        B, S, HID = (1, 256, 256)
        H, KVH, HD = (32, 8, 64)
        THETA = 10000.0

        def _rotate_half(x):
            x1, x2 = jnp.split(x, 2, axis=-1)
            return jnp.concatenate([-x2, x1], axis=-1)

        def _rope_cos_sin(seq_len, head_dim, theta, dtype):
            inv_freq = 1.0 / theta ** (jnp.arange(0, head_dim, 2, dtype=jnp.float32) / head_dim)
            pos = jnp.arange(seq_len, dtype=jnp.float32)
            freqs = pos[:, None] * inv_freq[None, :]
            emb = jnp.concatenate([freqs, freqs], axis=-1)
            return (jnp.cos(emb).astype(dtype), jnp.sin(emb).astype(dtype))
        b, s, _ = hidden_states.shape
        dtype = hidden_states.dtype
        q = (hidden_states @ Wq.T).reshape(b, s, H, HD).transpose(0, 2, 1, 3)
        k = (hidden_states @ Wk.T).reshape(b, s, KVH, HD).transpose(0, 2, 1, 3)
        v = (hidden_states @ Wv.T).reshape(b, s, KVH, HD).transpose(0, 2, 1, 3)
        cos, sin = _rope_cos_sin(s, HD, THETA, dtype)
        apply_rope = lambda x: x * cos + _rotate_half(x) * sin
        q = apply_rope(q)
        k = apply_rope(k)
        groups = H // KVH
        k = jnp.repeat(k, groups, axis=1)
        v = jnp.repeat(v, groups, axis=1)
        scale = 1.0 / jnp.sqrt(jnp.asarray(HD, dtype=dtype))
        logits = jnp.einsum('bhqd,bhkd->bhqk', q, k) * scale
        causal = jnp.tril(jnp.ones((s, s), dtype=bool))
        logits = jnp.where(causal, logits, jnp.finfo(dtype).min)
        attn = jax.nn.softmax(logits, axis=-1)
        out = jnp.einsum('bhqk,bhkd->bhqd', attn, v)
        out = out.transpose(0, 2, 1, 3).reshape(b, s, H * HD)
        return out @ Wo.T

    def _L0_ffn_ref(x, gate_w, w1, w3, w2, a1, b1, a3, b3, a2, b2):
        import jax, jax.numpy as jnp
        import numpy as np
        TOP_K = 2
        LORA_SCALE = 32.0 / 16.0
        B, S, D = x.shape
        E = gate_w.shape[0]
        xf = x.reshape(B * S, D)
        N = xf.shape[0]
        logits = xf @ gate_w.T
        top_w, top_i = jax.lax.top_k(logits, TOP_K)
        routing = jax.nn.softmax(top_w, axis=-1)
        w_full = jnp.zeros((N, E), x.dtype).at[jnp.arange(N)[:, None], top_i].add(routing)
        base1 = xf @ w1.T
        base3 = xf @ w3.T

        def expert_step(acc, p):
            A1, B1, A3, B3, A2, B2, we = p
            h1 = base1 + xf @ A1.T @ B1.T * LORA_SCALE
            h3 = base3 + xf @ A3.T @ B3.T * LORA_SCALE
            act = jax.nn.silu(h1) * h3
            out = act @ w2.T + act @ A2.T @ B2.T * LORA_SCALE
            return (acc + we[:, None] * out, None)
        init = jnp.zeros((N, D), x.dtype)
        out, _ = jax.lax.scan(expert_step, init, (a1, b1, a3, b3, a2, b2, w_full.T))
        return out.reshape(B, S, D)
    x = L0_attn_hidden_states
    mod = (_silu(L0_c) @ L0_wmod).reshape(L0_c.shape[0], 6, 1, -1)
    sa, ca, ga, sb, cb, gb = (mod[:, 0], mod[:, 1], mod[:, 2], mod[:, 3], mod[:, 4], mod[:, 5])
    ga = (2 * (ga >= 0) - 1) * jnp.maximum(jnp.abs(ga), 0.25)
    gb = (2 * (gb >= 0) - 1) * jnp.maximum(jnp.abs(gb), 0.25)
    h = _layernorm(x, axis=-1) * (1 + ca) + sa
    x = x + ga * _L0_attn_ref(h, L0_attn_Wq, L0_attn_Wk, L0_attn_Wv, L0_attn_Wo)
    h = _layernorm(x, axis=-1) * (1 + cb) + sb
    x = x + gb * _L0_ffn_ref(h, L0_ffn_gate_w, L0_ffn_w1, L0_ffn_w3, L0_ffn_w2, L0_ffn_a1, L0_ffn_b1, L0_ffn_a3, L0_ffn_b3, L0_ffn_a2, L0_ffn_b2)
    return x

_drawn_inputs = setup_inputs


def setup_inputs(seed=0):
    import zlib

    import numpy as np

    out = dict(_drawn_inputs(seed))
    spreads = {}
    factors = {'L0_attn_Wq': 8.0,
     'L0_attn_Wk': 8.0,
     'L0_attn_Wv': 6.683,
     'L0_attn_Wo': 6.551,
     'L0_ffn_gate_w': 4.434,
     'L0_ffn_a1': 6.479,
     'L0_ffn_b1': 6.477,
     'L0_ffn_a3': 6.693,
     'L0_ffn_b3': 6.772,
     'L0_ffn_a2': 6.681,
     'L0_ffn_b2': 6.727}
    for name, (base, spread) in spreads.items():
        noise = np.random.default_rng([zlib.crc32(name.encode()), seed]).standard_normal(out[name].shape)
        drawn = base * np.exp(spread * noise) if base else spread * noise
        out[name] = jnp.asarray(drawn.astype(out[name].dtype))
    for name, factor in factors.items():
        out[name] = (out[name] * factor).astype(out[name].dtype)
    return out
```

```python
from contextlib import ExitStack

import numpy as np

import concourse.bass as bass
from concourse import mybir

F32 = mybir.dt.float32
F16 = mybir.dt.float16
ALU = mybir.AluOpType
ACT = mybir.ActivationFunctionType
AX = mybir.AxisListType

P = 128
B, S, D = 2, 512, 256
H, KVH, HD = 32, 8, 64
F, E, R = 704, 8, 16
T = S // P
DK = D // P
G = H // KVH
GROUPS = B * KVH
HEADS = B * H
QKV = (G + 2) * HD
ROT = (G + 1) * HD
FT = -(-F // P)
EPS = 1e-5
SHIFT_UNIT = 64.0
SHIFT_BIAS = 4.0 * HD ** 0.5 / SHIFT_UNIT
MASKED = -1.0e30
KEY_OFF = [0, 512, 896, 1152]
PROBS = 1280
LORA_SCALE = 2.0


def wait(eng, sem, value):
    if isinstance(value, int) and value < 1:
        return
    eng.wait_ge(sem, value)


def wait_apart(eng, sem, value, passed):
    wait(eng, sem, value)
    eng.sem_inc(passed, 1)


def block_kernel(nc, x, wqkv, wo, cos, sin, cT, wmod, w1T, w3T, w2T, gateT, a1T, a3T, b1T, b3T, a2T, b2T, out):
    ctx = ExitStack()
    with ctx:
        def sb(name, shape, dt=F32):
            return ctx.enter_context(nc.sbuf_tensor(name, shape, dt))

        def sem(name):
            return ctx.enter_context(nc.semaphore(name))

        ps = ctx.enter_context(nc.psum_tensor("ps", [P, 8, 512], F32))
        S1_BANK, ST_BANK, T_BANK, PV_BANK, MISC_BANK = 0, 2, 4, 5, 6

        xs = sb("xs", [P, B * T, D])
        wq_sb = sb("wq_sb", [P, KVH, DK, QKV])
        wo_sb = sb("wo_sb", [P, H // 2, D])
        cos_sb = sb("cos_sb", [P, T, QKV])
        sin_sb = sb("sin_sb", [P, T, ROT])
        hT = sb("hT", [P, B, DK, S])
        acc = sb("acc", [P, B * T, D])
        w1_sb = sb("w1_sb", [P, DK, F])
        w3_sb = sb("w3_sb", [P, DK, F])
        w2_sb = sb("w2_sb", [P, FT, D])
        gate_sb = sb("gate_sb", [P, DK, E])
        a1_sb = sb("a1_sb", [P, DK, P])
        a3_sb = sb("a3_sb", [P, DK, P])
        b1_sb = sb("b1_sb", [P, F])
        b3_sb = sb("b3_sb", [P, F])
        a2_sb = sb("a2_sb", [P, FT, P])
        b2_sb = sb("b2_sb", [P, D])
        ident = sb("ident", [P, P])
        ident16 = sb("ident16", [P, P], F16)
        causal = sb("causal", [P, S])
        gates = sb("gates", [P, 2 * B, D])
        modT = sb("modT", [P, 12, B])
        c_sb = sb("c_sb", [P, DK, B])
        c_e = sb("c_e", [P, DK, B])
        c_s = sb("c_s", [P, DK, B])
        stats = sb("stats", [P, B * T, 6])
        mv = sb("mv", [P, B * T, 2])
        ve = sb("ve", [P, B * T])
        sd = sb("sd", [P, B * T])
        rstd = sb("rstd", [P, B * T])
        nrt = sb("nrt", [P, B * T])
        g_sign = sb("g_sign", [P, 4, B])
        g_abs = sb("g_abs", [P, 4, B])

        ra = sb("ra", [P, T, QKV])
        rb = sb("rb", [P, T, ROT])
        rot = sb("rot", [P, T, G + 1, HD])
        src = sb("src", [P, 2, G + 1, T, 2, P], F16)
        qT = sb("qT", [P, 2, 2, S], F16)
        kT = sb("kT", [P, 2, 2, S], F16)
        vh = sb("vh", [P, 2, T, HD + 1], F16)
        vl = sb("vl", [P, 2, T, HD], F16)
        prob = sb("prob", [P, 2, PROBS])
        ph = sb("ph", [P, 2, PROBS], F16)
        pl = sb("pl", [P, 2, PROBS], F16)
        mx = sb("mx", [P, 2, T])
        rsum = sb("rsum", [P, T])
        on = sb("on", [P, 2, T, 2 * HD])
        oT = sb("oT", [P, 2, S])
        junk = sb("junk", [P, PROBS], F16)

        def over(t, shape):
            flat = t[tuple([slice(None)] * len(t.shape))]
            names = " ".join("abcdefg"[:len(t.shape) - 1])
            flat = flat.rearrange(f"p {names} -> p ({names})") if len(t.shape) > 2 else flat
            if t.dtype != F32:
                flat = flat.bitcast(F32)
            n = int(np.prod(shape[1:]))
            flat = flat[:, 0:n]
            if len(shape) == 3:
                flat = flat.rearrange("p (a b) -> p a b", a=shape[1])
            if len(shape) == 4:
                flat = flat.rearrange("p (a b c) -> p a b c", a=shape[1], b=shape[2])
            return flat

        wmod_sb = over(prob, [P, DK, 1024])
        wmod_gb = over(ph, [P, DK, 512])
        xn = over(ra, [P, T, D])
        xn2 = over(rb, [P, T, D])
        gwide = over(pl, [P, 4, P])
        gwide2 = over(oT, [P, 4, P])

        ld_x, ld_c, ld_mod, ld_rope, ld_wo, ld_ffn = (sem(f"ld_{k}") for k in ("x", "c", "mod", "rope", "wo", "ffn"))
        ld_w = sem("ld_w")
        s_const = sem("s_const")
        c_exp, c_one, c_rec, c_silu = (sem(f"c_{k}") for k in ("exp", "one", "rec", "silu"))
        mod_mm, mod_sb = sem("mod_mm"), sem("mod_sb")
        mod_add = sem("mod_add")
        ln_stat, ln_aggr, ln_eps, ln_sqrt, ln_rec = (sem(f"ln_{k}") for k in ("stat", "aggr", "eps", "sqrt", "rec"))
        ln_n1, ln_n2, ln_rstd, xn_ready, xnT_mm, hT_ready = (
            sem(k) for k in ("ln_n1", "ln_n2", "ln_rstd", "xn_ready", "xnT_mm", "hT_ready"))
        g_s, g_a, g_m, g_wide, g_mm, g_ready = (sem(f"g_{k}") for k in ("s", "a", "m", "wide", "mm", "ready"))
        proj_done, rope_done, rot_half, rot_ready = (sem(k) for k in ("proj_done", "rope_done", "rot_half", "rot_ready"))
        kh_ready, kl_ready, qh_ready, ql_ready = (sem(k) for k in ("kh_ready", "kl_ready", "qh_ready", "ql_ready"))
        vh_ready, v_ready = sem("vh_ready"), sem("v_ready")
        tk_done, tk_evac, ta_done, ta_evac, tb_done, tb_evac = (
            sem(k) for k in ("tk_done", "tk_evac", "ta_done", "ta_evac", "tb_done", "tb_evac"))
        s1_done, maxed, m_ready = sem("s1_done"), sem("maxed"), sem("m_ready")
        st_done, exp_done, sel_done, ph_ready, pl_ready = (
            sem(k) for k in ("st_done", "exp_done", "sel_done", "ph_ready", "pl_ready"))
        pv_done, rsum_ready, normed = sem("pv_done"), sem("rsum_ready"), sem("normed")
        ot_done, ot_evac, op_done, op_added = (sem(k) for k in ("ot_done", "ot_evac", "op_done", "op_added"))
        acc_zero = sem("acc_zero")
        dve_passed, pool_passed = sem("dve_passed"), sem("pool_passed")
        r_mul, r_add = sem("r_mul"), sem("r_add")
        fs = {k: sem("f_" + k) for k in (
            "h2", "gate_mm", "lg", "v1", "eq", "rv", "fi", "oh1", "mk2", "v2", "eq2", "rv2", "fi2", "oh2",
            "dv", "ex", "den", "w1", "w2", "wide", "dwide", "mT_mm", "mT", "t_mm", "tm", "tmd",
            "h_mm", "silu", "p", "a", "g", "d_mm", "z_mm", "zm", "u", "o_mm", "og", "o")}
        stored = sem("stored")

        block = ctx.enter_context(nc.Block())

        fsm = sb("fsm", [P, 8, T, E])
        fs1 = sb("fs1", [P, 12, T])
        rev = sb("rev", [P, E])
        wide = over(src, [P, 5, T, P])
        maskT = over(wq_sb, [P, 5, S])
        wq_flat = over(wq_sb, [P, KVH * DK * QKV])

        def wq_part(at, shape):
            n = int(np.prod(shape[1:]))
            v = wq_flat[:, at:at + n]
            if len(shape) == 3:
                v = v.rearrange("p (a b) -> p a b", a=shape[1])
            return v
        tmask = over(prob, [P, 4, S])
        gsum = wq_part(5 * S, [P, FT, S])
        assert 5 * S + FT * S <= KVH * DK * QKV
        sil = over(ra, [P, 2, S])
        pr = over(rb, [P, 2, S])
        av = over(rot, [P, 2, S])
        uT = over(on, [P, 2, S])
        y1 = over(ph, [P, 2, D])
        y2 = over(pl, [P, 2, D])

        def form(par, item, t, ab):
            return src[:, par, item, t, ab, :]

        @block.sync
        def _(sp):
            xv = x.rearrange("b (t p) d -> p (b t) d", p=P)
            sp.dma_start(xs[:, 0:T, :], xv[:, 0:T, :]).then_inc(ld_x, 16)
            sp.dma_start(wmod_sb, wmod[:, :, 0:1024]).then_inc(ld_mod, 16)
            sp.dma_start(wmod_gb, wmod[:, :, 1024:1536]).then_inc(ld_mod, 16)
            for g in range(1, KVH):
                sp.dma_start(wq_sb[:, g, :, :], wqkv[g]).then_inc(ld_w, 16)
            sp.dma_start(w1_sb[:, :, :], w1T).then_inc(ld_ffn, 16)
            sp.dma_start(w3_sb[:, :, :], w3T).then_inc(ld_ffn, 16)
            full = F // P
            sp.dma_start(w2_sb[:, 0:full, :], w2T[0:full * P, :].rearrange("(f p) d -> p f d", p=P)).then_inc(ld_ffn, 16)
            sp.dma_start(w2_sb[0:F - full * P, full, :], w2T[full * P:F, :]).then_inc(ld_ffn, 16)
            sp.dma_start(a2_sb[:, 0:full, :], a2T[0:full * P, :].rearrange("(f p) d -> p f d", p=P)).then_inc(ld_ffn, 16)
            sp.dma_start(a2_sb[0:F - full * P, full, :], a2T[full * P:F, :]).then_inc(ld_ffn, 16)
            for dst, s in ((gate_sb, gateT), (a1_sb, a1T), (a3_sb, a3T)):
                sp.dma_start(dst[:, :, :], s).then_inc(ld_ffn, 16)
            for dst, s in ((b1_sb, b1T), (b3_sb, b3T), (b2_sb, b2T)):
                sp.dma_start(dst[:, :], s).then_inc(ld_ffn, 16)
            ov = out.rearrange("b (t p) d -> p (b t) d", p=P)
            for i in range(B * T // 2):
                sp.wait_ge(fs["o"], i + 1)
                sp.dma_start(ov[:, 2 * i:2 * i + 2, :], xs[:, 2 * i:2 * i + 2, :]).then_inc(stored, 16)
            sp.wait_ge(stored, 16 * (B * T // 2))

        @block.tensor
        def _(pe):
            pe.wait_ge(c_silu, 1)
            pe.wait_ge(ld_mod, 32)
            for ch in range(12):
                for k in range(DK):
                    w = wmod_sb[:, k, ch * P:(ch + 1) * P] if ch < 8 else wmod_gb[:, k, (ch - 8) * P:(ch - 7) * P]
                    mm = pe.matmul(ps[:, PV_BANK, 2 * ch:2 * ch + 2], w, c_s[:, k, :], start=(k == 0), stop=(k == DK - 1))
            mm.then_inc(mod_mm, 1)
            pe.wait_ge(s_const, 1)

            def transpose_rows(b, bank0, buf, done, count):
                for k in range(DK):
                    for t in range(T):
                        if k == 0:
                            pe.wait_ge(xn_ready, count + t + 1)
                        mm = pe.transpose(ps[:, bank0 + k, t * P:(t + 1) * P], buf[:, t, k * P:(k + 1) * P], ident[:, :])
                    mm.then_inc(done, 1)

            transpose_rows(0, 0, xn, xnT_mm, 0)
            transpose_rows(1, 2, xn2, xnT_mm, T)

            def project(g, w, b, t, bank):
                for k in range(DK):
                    mm = pe.matmul(ps[:, bank, 0:QKV], hT[:, b, k, t * P:(t + 1) * P], wq_sb[:, w, k, :],
                                   start=(k == 0), stop=(k == DK - 1))
                mm.then_inc(proj_done, 1)

            def tk(g, par):
                pe.wait_ge(kh_ready, g + 1)
                pe.wait_ge(kl_ready, g + 1)
                for ab in range(2):
                    for t in range(T):
                        mm = pe.transpose(ps[:, T_BANK, ab * 256 + t * 64:ab * 256 + (t + 1) * 64].bitcast(F16),
                                          form(par, G, t, ab), ident16[:, :])
                mm.then_inc(tk_done, 1)

            def tq(par, item, ab, done):
                for t in range(T):
                    mm = pe.transpose(ps[:, T_BANK, t * 64:(t + 1) * 64].bitcast(F16), form(par, item, t, ab), ident16[:, :])
                mm.then_inc(done, 1)

            def ta(m, par, item):
                pe.wait_ge(qh_ready, m + 1)
                tq(par, item, 0, ta_done)

            def tb(m, par, item):
                pe.wait_ge(ql_ready, m + 1)
                pe.wait_ge(m_ready, m + 1)
                tq(par, item, 1, tb_done)

            def s1(m, mpar, kpar, f):
                bank = S1_BANK + (mpar + f) % 2
                wait(pe, maxed, 3 * m + f - 1)
                off = 0
                for qt in ([3], [2], [0, 1])[f]:
                    n = (qt + 1) * P
                    mm = pe.matmul(ps[:, bank, off:off + n], qT[:, mpar, 0, qt * P:(qt + 1) * P], kT[:, kpar, 0, 0:n],
                                   start=True, stop=True)
                    off += n
                mm.then_inc(s1_done, 1)

            def st(n, npar, kpar, f):
                bank = ST_BANK + (npar + f) % 2
                wait(pe, exp_done, 3 * n + f - 1)
                off = 0
                for kt in ([0], [1], [2, 3])[f]:
                    w = S - kt * P
                    for ab in range(2):
                        mm = pe.matmul(ps[:, bank, off:off + w], kT[:, kpar, ab, kt * P:(kt + 1) * P],
                                       qT[:, npar, ab, kt * P:S], start=(ab == 0), stop=(ab == 1))
                    off += w
                mm.then_inc(st_done, 1)

            def pv(n, npar, g, vpar):
                pe.wait_ge(ph_ready, n + 1)
                pe.wait_ge(pl_ready, n + 1)
                pe.wait_ge(v_ready, g + 1)
                wait(pe, normed, n)
                for qt in range(T):
                    at = qt * (HD + 1)
                    for kt in range(qt + 1):
                        c = KEY_OFF[kt] + (qt - kt) * P
                        first, last = kt == 0, kt == qt
                        pe.matmul(ps[:, PV_BANK, at:at + HD + 1], ph[:, npar, c:c + P], vh[:, vpar, kt, :],
                                  start=first, stop=False)
                        pe.matmul(ps[:, PV_BANK, at:at + HD], ph[:, npar, c:c + P], vl[:, vpar, kt, :],
                                  start=False, stop=False)
                        mm = pe.matmul(ps[:, PV_BANK, at:at + HD + 1], pl[:, npar, c:c + P], vh[:, vpar, kt, :],
                                       start=False, stop=last)
                mm.then_inc(pv_done, 1)

            def ot(pair, p, bank):
                pe.wait_ge(normed, 2 * pair + 2)
                for t in range(T):
                    mm = pe.transpose(ps[:, bank, t * P:(t + 1) * P], on[:, p, t, :], ident[:, :])
                mm.then_inc(ot_done, 1)

            def op(g, w, half, bank):
                pe.wait_ge(ot_evac, 2 * g + 2)
                for t in range(2 * half, 2 * half + 2):
                    for p in range(2):
                        mm = pe.matmul(ps[:, bank, (t % 2) * D:(t % 2) * D + D], oT[:, p, t * P:(t + 1) * P],
                                       wo_sb[:, w + p, :], start=(p == 0), stop=(p == 1))
                mm.then_inc(op_done, 1)

            pe.wait_ge(ld_w, 16)
            pe.wait_ge(hT_ready, 2)
            M0, M1 = MISC_BANK, MISC_BANK + 1
            for t in range(T):
                if t >= 2:
                    pe.wait_ge(rope_done, t - 1)
                project(0, 0, 0, t, MISC_BANK + t % 2)
            pe.wait_ge(hT_ready, 2 * B)
            pe.wait_ge(g_wide, 2)
            for i in range(4 * B):
                kind, b, k = i // 4, (i // 2) % 2, i % 2
                wd = (gwide if kind == 0 else gwide2)[:, 2 * b + k, :]
                mm = pe.transpose(ps[:, 2 * (i // 4) % 4, (i % 4) * P:(i % 4 + 1) * P], wd, ident[:, :])
            mm.then_inc(g_mm, 1)
            tk(0, 0)
            pe.wait_ge(tk_evac, 1)
            ta(0, 0, 0)
            pe.wait_ge(ta_evac, 1)
            ta(1, 0, 1)
            pe.wait_ge(ta_evac, 2)
            pe.wait_ge(g_ready, 2)
            for f in range(3):
                s1(0, 0, 0, f)
            tb(0, 0, 0)
            pe.wait_ge(ld_w, 16 * KVH)
            pe.wait_ge(ld_wo, 16)

            def group(g, par, w_next, b_next, w_prev, first=False, last=False):
                for j in range(G):
                    n = 4 * g + j
                    jp = j % 2
                    more1, more2 = not (last and j == 3), not (last and j >= 2)
                    par1, item1 = (par, j + 1) if j < 3 else (1 - par, 0)
                    par2, item2 = (par, j + 2) if j < 2 else (1 - par, j - 2)
                    wait(pe, tb_evac, n + 1)
                    if j < 3:
                        if more1:
                            pe.wait_ge(ta_evac, n + 2)
                        for f in range(3):
                            if more1:
                                s1(n + 1, 1 - jp, par1, f)
                            st(n, jp, par, f)
                    else:
                        for f in range(3):
                            st(n, jp, par, f)
                    if j < 2 and more2:
                        wait(pe, tb_evac, n + 1)
                        ta(n + 2, par2, item2)
                    if j == 0 and not last:
                        wait(pe, op_added, 2 * g - 2)
                        project(g + 1, w_next, b_next, 0, M0)
                        wait(pe, ot_evac, 2 * g - 1)
                        project(g + 1, w_next, b_next, 1, M1)
                    if j == 1 and not last:
                        pe.wait_ge(rope_done, 4 * g + 5)
                        project(g + 1, w_next, b_next, 2, M0)
                        pe.wait_ge(rope_done, 4 * g + 6)
                        project(g + 1, w_next, b_next, 3, M1)
                    if j == 1 and not first:
                        if last:
                            pe.wait_ge(op_added, 2 * g - 2)
                        else:
                            pe.wait_ge(rope_done, 4 * g + 7)
                        ot(2 * g - 1, 1, M0)
                    if j == 2 and not first:
                        if last:
                            pe.wait_ge(ot_evac, 2 * g - 1)
                        else:
                            pe.wait_ge(rope_done, 4 * g + 8)
                        op(g - 1, w_prev, 0, M1)
                    if j == 3:
                        if not first:
                            op(g - 1, w_prev, 1, M0)
                        if more1:
                            pe.wait_ge(ta_evac, n + 2)
                            pe.wait_ge(tk_evac, g + 2)
                            for f in range(3):
                                s1(n + 1, 1 - jp, par1, f)
                        if first:
                            pe.wait_ge(rope_done, 8)
                        else:
                            pe.wait_ge(op_added, 2 * g - 1)
                        ot(2 * g, 0, M1)
                        if more2:
                            pe.wait_ge(ta_evac, n + 2)
                            ta(n + 2, par2, item2)
                    if more1:
                        if j == 2:
                            wait(pe, tb_evac, n + 1)
                        else:
                            pe.wait_ge(ta_evac, n + 3 if more2 else n + 2)
                        tb(n + 1, par1, item1)
                    if not (first and j == 0):
                        if j == 0:
                            pv(n - 1, 1 - jp, g - 1, 1 - par)
                        else:
                            pv(n - 1, 1 - jp, g, par)
                    if j == 2 and not last:
                        pe.wait_ge(tb_evac, n + 2)
                        tk(g + 1, 1 - par)
                        pe.wait_ge(tk_evac, g + 2)
                        ta(n + 2, par2, item2)

            group(0, 0, 1, 0, 0, first=True)
            with pe.Fori(1, KVH - 2, 2) as g:
                group(g, 1, g + 1, 0, 2 * g - 2)
                group(g + 1, 0, g + 2, 0, 2 * g)
            group(KVH - 1, 1, 0, 1, 2 * KVH - 4)
            group(KVH, 0, 1, 1, 2 * KVH - 2)
            with pe.Fori(KVH + 1, GROUPS - 2, 2) as g:
                group(g, 1, g + 1 - KVH, 1, 2 * g - 2 - 2 * KVH)
                group(g + 1, 0, g + 2 - KVH, 1, 2 * g - 2 * KVH)
            group(GROUPS - 1, 1, 0, 1, 2 * KVH - 4, last=True)
            L = GROUPS - 1
            pv(HEADS - 1, 1, L, 1)
            pe.wait_ge(op_added, 2 * L)
            ot(2 * L + 1, 1, M0)
            op(L, 2 * KVH - 2, 0, M1)
            pe.wait_ge(ot_evac, 2 * L + 2)
            op(L, 2 * KVH - 2, 1, M0)

            pe.wait_ge(maxed, 3 * HEADS)
            pe.wait_ge(exp_done, 3 * HEADS)
            for b in range(B):
                transpose_rows(b, 2 * b, (xn, xn2)[b], xnT_mm, (B + b) * T)
            pe.wait_ge(ld_ffn, 16 * 12)
            for b in range(B):
                pe.wait_ge(fs["h2"], 2 * (b + 1))
                if b == 0:
                    pe.wait_ge(tb_evac, HEADS)
                else:
                    pe.wait_ge(fs["zm"], 2)
                for t in range(T):
                    for k in range(DK):
                        mm = pe.matmul(ps[:, 4, t * E:(t + 1) * E], hT[:, b, k, t * P:(t + 1) * P], gate_sb[:, k, :],
                                       start=(k == 0), stop=(k == DK - 1))
                mm.then_inc(fs["gate_mm"], 1)
                if b == 0:
                    pe.wait_ge(op_added, 2 * GROUPS)
                else:
                    pe.wait_ge(fs["o"], 2)
                for i, a in enumerate((a1_sb, a3_sb)):
                    for k in range(DK):
                        mm = pe.matmul(ps[:, 6 + i, :], a[:, k, :], hT[:, b, k, :], start=(k == 0), stop=(k == DK - 1))
                mm.then_inc(fs["t_mm"], 1)
                for i in range(5):
                    if i < 3:
                        pe.wait_ge(fs["wide"] if i < 2 else fs["dwide"], (2 * b + i + 1) if i < 2 else b + 1)
                    else:
                        pe.wait_ge(fs["wide"], 2 * b + 2)
                    if i == 0:
                        pe.wait_ge(fs["lg"], b + 1)
                    if i == 1:
                        if b == 0:
                            pe.wait_ge(normed, HEADS)
                        else:
                            pe.wait_ge(fs["zm"], 2)
                    if i >= 2:
                        pe.wait_ge(fs["mT"], 5 * b + i - 1)
                    if i == 3:
                        pe.wait_ge(fs["w1"], b + 1)
                    if i == 4:
                        pe.wait_ge(fs["w2"], b + 1)
                    for t in range(T):
                        mm = pe.transpose(ps[:, 4 + i % 2, t * P:(t + 1) * P], wide[:, i, t, :], ident[:, :])
                    mm.then_inc(fs["mT_mm"], 1)
                def z_product(f, s):
                    m = min(P, F - f * P)
                    pe.wait_ge(fs["a"], 2 * (b * FT + f) + s + 1)
                    if f == 0 and s == 0:
                        pe.wait_ge(fs["mT"], 5 * b + 5)
                    mm = pe.matmul(ps[:, 4 + s, :], a2_sb[0:m, f, :], av[0:m, s, :], start=(f == 0), stop=(f == FT - 1))
                    mm.then_inc(fs["z_mm"], 1)

                for f in range(FT):
                    m = min(P, F - f * P)
                    i = b * FT + f
                    bank = 2 * (i % 2)
                    if b == 0 and f < 2:
                        pe.wait_ge(fs["h2"], 2 * B)
                    else:
                        pe.wait_ge(fs["p"], 2 * (i - 2) + 2)
                    fc = slice(f * P, f * P + m)
                    if f == 0:
                        pe.wait_ge(fs["tm"], 2 * b + 2)
                    for c, (w, bb) in enumerate(((w1_sb, b1_sb), (w3_sb, b3_sb))):
                        for k in range(DK):
                            pe.matmul(ps[0:m, bank + c, :], w[:, k, fc], hT[:, b, k, :], start=(k == 0), stop=False)
                        mm = pe.matmul(ps[0:m, bank + c, :], bb[:, fc], tmask[:, c, :], start=False, stop=True)
                        mm.then_inc(fs["h_mm"], 1)
                    if f > 0:
                        z_product(f - 1, 1)
                    pe.wait_ge(fs["p"], 2 * i + 1)
                    if f == 0:
                        pe.wait_ge(fs["tmd"], 2 * b + 2)
                    for c, bb in enumerate((b1_sb, b3_sb)):
                        mm = pe.matmul(ps[0:m, bank + c, :], bb[:, fc], tmask[:, 2 + c, :], start=False, stop=True,
                                       skip_group_check=True)
                        mm.then_inc(fs["d_mm"], 1)
                    z_product(f, 0)
                z_product(FT - 1, 1)
                pe.wait_ge(fs["g"], FT * (b + 1))
                pe.wait_ge(fs["u"], b + 1)
                for i in range(2):
                    for t in range(2 * i, 2 * i + 2):
                        at = (t % 2) * D
                        for f in range(FT):
                            m = min(P, F - f * P)
                            pe.matmul(ps[:, 6 + i, at:at + D], gsum[0:m, f, t * P:(t + 1) * P], w2_sb[0:m, f, :],
                                      start=(f == 0), stop=False)
                        mm = pe.matmul(ps[:, 6 + i, at:at + D], uT[:, 1, t * P:(t + 1) * P], b2_sb[:, :],
                                       start=False, stop=True)
                    mm.then_inc(fs["o_mm"], 1)

        @block.scalar
        def _(act):
            act.dma_start(c_sb[:, :, :], cT).then_inc(ld_c, 16)
            act.dma_start(wq_sb[:, 0, :, :], wqkv[0]).then_inc(ld_w, 16)
            act.dma_start(cos_sb[:, :, :], cos).then_inc(ld_rope, 16)
            act.dma_start(sin_sb[:, :, :], sin).then_inc(ld_rope, 16)
            xv = x.rearrange("b (t p) d -> p (b t) d", p=P)
            act.dma_start(xs[:, T:2 * T, :], xv[:, T:2 * T, :]).then_inc(ld_x, 16)
            act.dma_start(wo_sb[:, :, :], wo).then_inc(ld_wo, 16)
            act.wait_ge(ld_c, 16)
            act.activation(c_e[:, :, :], c_sb[:, :, :], ACT.Exp, scale=-1.0).then_inc(c_exp, 1)
            for b in range(B):
                act.wait_ge(ln_eps, b + 1)
                act.activation(sd[:, b * T:(b + 1) * T], ve[:, b * T:(b + 1) * T], ACT.Sqrt).then_inc(ln_sqrt, 1)

            def modulate(b, bank0, add, done, base):
                for k in range(DK):
                    act.wait_ge(xnT_mm, base + 2 * b + k + 1)
                    act.activation(hT[:, b, k, :], ps[:, bank0 + k, :], ACT.Identity, bias=modT[:, add + k, b:b + 1],
                                   scale=modT[:, add + 2 + k, b:b + 1]).then_inc(done, 1)

            act.wait_ge(mod_add, 2)
            for b in range(B):
                modulate(b, 2 * b, 0, hT_ready, 0)

            def k_high(g, par):
                act.wait_ge(rot_ready, g + 1)
                act.activation(src[:, par, G, :, :, 0:HD],
                               rot[:, :, G, :].unsqueeze(2).broadcast_to([P, T, 2, HD]), ACT.Copy).then_inc(kh_ready, 1)

            def q_high(m, par, item, g):
                act.wait_ge(rot_ready, g + 1)
                act.activation(src[:, par, item, :, 0, :].rearrange("p t (c d) -> p t c d", c=2),
                               rot[:, :, item, :].unsqueeze(2).broadcast_to([P, T, 2, HD]), ACT.Copy).then_inc(qh_ready, 1)

            def ta_out(m, mpar):
                act.wait_ge(ta_done, m + 1)
                act.activation(qT[:, mpar, 0, :], ps[:, T_BANK, 0:256].bitcast(F16), ACT.Copy).then_inc(ta_evac, 1)

            def tk_out(g, par):
                act.wait_ge(tk_done, g + 1)
                act.activation(kT[:, par, :, :].rearrange("p a s -> p (a s)"), ps[:, T_BANK, :].bitcast(F16),
                               ACT.Copy).then_inc(tk_evac, 1)

            def exps(n, npar):
                wait(act, pl_ready, n - 1)
                for f in range(3):
                    act.wait_ge(st_done, 3 * n + f + 1)
                    w, off = (512, 384, 384)[f], (0, 512, 896)[f]
                    act.activation(prob[:, npar, off:off + w], ps[:, ST_BANK + (npar + f) % 2, 0:w], ACT.Exp,
                                   scale=HD ** -0.5).then_inc(exp_done, 1)

            def p_high(n, npar):
                act.wait_ge(sel_done, n + 1)
                wait(act, pv_done, n - 1)
                act.activation(ph[:, npar, :], prob[:, npar, :], ACT.Copy).then_inc(ph_ready, 1)

            def ot_out(pair, p, bank):
                act.wait_ge(ot_done, pair + 1)
                act.activation(oT[:, p, :], ps[:, bank, :], ACT.Copy).then_inc(ot_evac, 1)

            act.wait_ge(s_const, 1)
            k_high(0, 0)
            q_high(0, 0, 0, 0)
            act.wait_ge(g_mm, 1)
            for i in range(2):
                act.activation(gates[:, 2 * i:2 * i + 2, :].rearrange("p a d -> p (a d)"), ps[:, 2 * i, :],
                               ACT.Copy).then_inc(g_ready, 1)
            tk_out(0, 0)
            ta_out(0, 0)
            q_high(1, 0, 1, 0)
            ta_out(1, 1)
            q_high(2, 0, 2, 0)
            q_high(3, 0, 3, 0)

            def group(g, par, first=False, last=False):
                for j in range(G):
                    n = 4 * g + j
                    jp = j % 2
                    exps(n, jp)
                    if j < 2:
                        ta_out(n + 2, jp)
                    p_high(n, jp)
                    if j == 1 and not first:
                        ot_out(2 * g - 1, 1, MISC_BANK)
                    if j == 2 and not last:
                        k_high(g + 1, 1 - par)
                        q_high(n + 2, 1 - par, 0, g + 1)
                        tk_out(g + 1, 1 - par)
                        ta_out(n + 2, jp)
                        q_high(n + 3, 1 - par, 1, g + 1)
                    if j == 3:
                        ot_out(2 * g, 0, MISC_BANK + 1)
                        if not last:
                            ta_out(n + 2, jp)
                            q_high(n + 3, 1 - par, 2, g + 1)
                            q_high(n + 4, 1 - par, 3, g + 1)

            group(0, 0, first=True)
            with act.Fori(1, KVH - 2, 2) as g:
                group(g, 1)
                group(g + 1, 0)
            group(KVH - 1, 1)
            group(KVH, 0)
            with act.Fori(KVH + 1, GROUPS - 2, 2) as g:
                group(g, 1)
                group(g + 1, 0)
            group(GROUPS - 1, 1, last=True)
            ot_out(2 * GROUPS - 1, 1, MISC_BANK)

            for b in range(B):
                act.wait_ge(ln_eps, B + b + 1)
                act.activation(sd[:, b * T:(b + 1) * T], ve[:, b * T:(b + 1) * T], ACT.Sqrt).then_inc(ln_sqrt, 1)
            for b in range(B):
                modulate(b, 2 * b, 6, fs["h2"], 2 * B)
            for b in range(B):
                act.wait_ge(fs["dv"], b + 1)
                act.activation(fs1[:, 4, :], fs1[:, 3, :], ACT.Exp).then_inc(fs["ex"], 1)
                for f in range(FT):
                    m = min(P, F - f * P)
                    i = b * FT + f
                    bank = 2 * (i % 2)
                    for s in range(2):
                        act.wait_ge(fs["h_mm"] if s == 0 else fs["d_mm"], 2 * i + 1)
                        wait(act, fs["p"], 2 * i + s - 1)
                        act.activation(sil[0:m, s, :], ps[0:m, bank, :], ACT.Silu).then_inc(fs["silu"], 1)

        @block.vector
        def _(dve):
            dve.wait_ge(c_exp, 1)
            dve.tensor_scalar(c_e[:, :, :], c_e[:, :, :], 1.0, None, ALU.add).then_inc(c_one, 1)
            dve.wait_ge(c_one, 1)
            dve.reciprocal(c_e[:, :, :], c_e[:, :, :]).then_inc(c_rec, 1)
            dve.wait_ge(c_rec, 1)
            dve.tensor_tensor(c_s[:, :, :], c_sb[:, :, :], c_e[:, :, :], ALU.mult).then_inc(c_silu, 1)

            def row_stats(b, base):
                for t in range(T):
                    i = b * T + t
                    dve.bn_stats(stats[:, i, :], xs[:, i, :]).then_inc(ln_stat, 1)
                for t in range(T):
                    i = b * T + t
                    dve.wait_ge(ln_stat, base * T + i + 1)
                    dve.bn_aggr(mv[:, i, :], stats[:, i, :]).then_inc(ln_aggr, 1)
                dve.wait_ge(ln_aggr, (base + b + 1) * T if base == 0 else (B + b + 1) * T)
                dve.tensor_scalar(ve[:, b * T:(b + 1) * T], mv[:, b * T:(b + 1) * T, 1], EPS, None, ALU.add)\
                   .then_inc(ln_eps, 1)

            def normalise(b, rnd, buf):
                c = slice(b * T, (b + 1) * T)
                k = rnd * B + b + 1
                dve.wait_ge(ln_sqrt, k)
                dve.reciprocal(rstd[:, c], sd[:, c]).then_inc(ln_rec, 1)
                dve.wait_ge(ln_rec, k)
                dve.tensor_tensor(nrt[:, c], rstd[:, c], rstd[:, c], ALU.mult).then_inc(ln_n1, 1)
                dve.wait_ge(ln_n1, 3 * k - 2)
                dve.tensor_tensor(nrt[:, c], nrt[:, c], ve[:, c], ALU.mult).then_inc(ln_n1, 1)
                dve.wait_ge(ln_n1, 3 * k - 1)
                dve.tensor_scalar(nrt[:, c], nrt[:, c], -0.5, 1.5, ALU.mult, ALU.add).then_inc(ln_n1, 1)
                dve.wait_ge(ln_n1, 3 * k)
                dve.tensor_tensor(rstd[:, c], rstd[:, c], nrt[:, c], ALU.mult).then_inc(ln_rstd, 1)
                dve.wait_ge(ln_rstd, k)
                for t in range(T):
                    i = b * T + t
                    dve.tensor_scalar(buf[:, t, :], xs[:, i, :], mv[:, i, 0:1], rstd[:, i:i + 1],
                                      ALU.subtract, ALU.mult).then_inc(xn_ready, 1)

            dve.wait_ge(ld_x, 32)
            row_stats(0, 0)
            row_stats(1, 0)
            normalise(0, 0, xn)
            normalise(1, 0, xn2)
            dve.wait_ge(mod_mm, 1)
            dve.tensor_copy(modT[:, :, :].rearrange("p c b -> p (c b)"), ps[:, PV_BANK, 0:24]).then_inc(mod_sb, 1)
            dve.wait_ge(mod_sb, 1)
            for c in (2, 8):
                dve.tensor_scalar(modT[:, c:c + 2, :], modT[:, c:c + 2, :], 1.0, None, ALU.add).then_inc(mod_add, 1)
            for i, c in enumerate((4, 10)):
                gsrc = modT[:, c:c + 2, :]
                gs, gab = g_sign[:, 2 * i:2 * i + 2, :], g_abs[:, 2 * i:2 * i + 2, :]
                dve.tensor_scalar(gs, gsrc, 0.0, 2.0, ALU.is_ge, ALU.mult).then_inc(g_s, 1)
                dve.wait_ge(g_s, 2 * i + 1)
                dve.tensor_scalar(gs, gs, -1.0, None, ALU.add).then_inc(g_s, 1)
                dve.wait_ge(g_s, 2 * i + 2)
                dve.tensor_tensor(gab, gs, gsrc, ALU.mult).then_inc(g_a, 1)
                dve.wait_ge(g_a, 2 * i + 1)
                dve.tensor_scalar(gab, gab, 0.25, None, ALU.max).then_inc(g_a, 1)
                dve.wait_ge(g_a, 2 * i + 2)
                dve.tensor_tensor(gab, gab, gs, ALU.mult).then_inc(g_m, 1)
                dve.wait_ge(g_m, i + 1)
                dst = (gwide, gwide2)[i].rearrange("p (b k) d -> p b k d", b=B)
                dve.tensor_copy(dst, gab.rearrange("p k b -> p b k").unsqueeze(3).broadcast_to([P, B, 2, P]))\
                   .then_inc(g_wide, 1)

            def rope(g, t, bank):
                wait(dve, v_ready, g)
                dve.wait_ge(proj_done, 4 * g + t + 1)
                dve.tensor_tensor(ra[:, t, :], ps[:, bank, 0:QKV], cos_sb[:, t, :], ALU.mult)
                dve.tensor_tensor(rb[:, t, :], ps[:, bank, 0:ROT], sin_sb[:, t, :], ALU.mult).then_inc(rope_done, 1)

            def rotate(g):
                wait(dve, kh_ready, g)
                wait(dve, qh_ready, 4 * g)
                dve.wait_ge(rope_done, 4 * g + 4)
                hw = HD // 2
                for half in range(2):
                    a = ra[:, :, 0:ROT].rearrange("p t (h c) -> p t h c", c=HD)
                    s = rb[:, :, :].rearrange("p t (h c) -> p t h c", c=HD)
                    lo, hi = half * hw, (1 - half) * hw
                    dve.tensor_tensor(rot[:, :, :, lo:lo + hw], a[:, :, :, lo:lo + hw], s[:, :, :, hi:hi + hw], ALU.add)\
                       .then_inc(rot_half if half == 0 else rot_ready, 1)

            def k_low(g, par):
                dve.wait_ge(kh_ready, g + 1)
                dve.tensor_tensor(src[:, par, G, :, 0, HD:P], rot[:, :, G, :], src[:, par, G, :, 0, 0:HD],
                                  ALU.subtract).then_inc(kl_ready, 1)

            def q_low(m, par, item):
                dve.wait_ge(qh_ready, m + 1)
                dve.tensor_tensor(src[:, par, item, :, 1, 0:HD], rot[:, :, item, :], src[:, par, item, :, 0, 0:HD],
                                  ALU.subtract).then_inc(ql_ready, 1)

            def row_max(m, mpar, par, item):
                for f in range(3):
                    wait_apart(dve, s1_done, 3 * m + f + 1, dve_passed)
                    bank = S1_BANK + (mpar + f) % 2
                    off, at = 0, (0, 512, 896)[f]
                    for qt in ([3], [2], [0, 1])[f]:
                        w = (qt + 1) * P
                        ins = dve.tensor_tensor_reduce(junk[:, at + off:at + off + w], ps[:, bank, off:off + w], causal[:, S - w:S], 1.0,
                                                       -3.0e38, ALU.add, ALU.max, mx[:, mpar, qt:qt + 1])
                        off += w
                    ins.then_inc(maxed, 1)
                dve.wait_ge(maxed, 3 * m + 3)
                dve.tensor_scalar(src[:, par, item, :, 1, HD:HD + 1], mx[:, mpar, :].unsqueeze(2), -1.0 / SHIFT_UNIT,
                                  SHIFT_BIAS, ALU.mult, ALU.add).then_inc(m_ready, 1)

            def tb_out(m, mpar):
                dve.wait_ge(tb_done, m + 1)
                dve.tensor_copy(qT[:, mpar, 1, :], ps[:, T_BANK, 0:256].bitcast(F16)).then_inc(tb_evac, 1)

            def norm(n, pair, p, half):
                dve.wait_ge(pv_done, n + 1)
                o = ps[:, PV_BANK, 0:T * (HD + 1)].rearrange("p (t c) -> p t c", c=HD + 1)
                dve.reciprocal(rsum[:, :].unsqueeze(2), o[:, :, HD:HD + 1]).then_inc(rsum_ready, 1)
                dve.wait_ge(rsum_ready, n + 1)
                wait(dve, ot_done, pair - 1)
                dve.tensor_tensor(on[:, p, :, half * HD:(half + 1) * HD], o[:, :, 0:HD],
                                  rsum[:, :].unsqueeze(2).broadcast_to([P, T, HD]), ALU.mult).then_inc(normed, 1)

            def op_add(g, b, half, bank):
                at = b * T + 2 * half
                dve.wait_ge(op_done, 2 * g + half + 1)
                a = acc[:, at:at + 2, :].rearrange("p t d -> p (t d)")
                dve.tensor_tensor(a, ps[:, bank, :], a, ALU.add).then_inc(op_added, 1)

            dve.wait_ge(ld_rope, 32)
            dve.wait_ge(s_const, 1)
            dve.wait_ge(xnT_mm, 2 * B)
            for t in range(T):
                rope(0, t, MISC_BANK + t % 2)
            rotate(0)
            k_low(0, 0)
            q_low(0, 0, 0)
            q_low(1, 0, 1)
            row_max(0, 0, 0, 0)
            tb_out(0, 0)
            q_low(2, 0, 2)
            q_low(3, 0, 3)
            M0, M1 = MISC_BANK, MISC_BANK + 1

            def group(g, par, b_prev, first=False, last=False):
                for j in range(G):
                    n = 4 * g + j
                    jp = j % 2
                    more1 = not (last and j == 3)
                    par1, item1 = (par, j + 1) if j < 3 else (1 - par, 0)
                    if j == 3 and not first:
                        op_add(g - 1, b_prev, 1, M0)
                    if more1:
                        row_max(n + 1, 1 - jp, par1, item1)
                    if not (first and j < 2):
                        norm(n - 2, 2 * g - 1 + j // 2, 1 - j // 2, jp)
                    if j < 2 and not last:
                        rope(g + 1, 2 * j, M0)
                    if j == 2 and not last:
                        k_low(g + 1, 1 - par)
                        q_low(n + 2, 1 - par, 0)
                    if j == 2 and not first:
                        op_add(g - 1, b_prev, 0, M1)
                    if more1:
                        tb_out(n + 1, 1 - jp)
                    if j < 2 and not last:
                        rope(g + 1, 2 * j + 1, M1)
                    if j == 1 and not last:
                        rotate(g + 1)
                    if j == 2 and not last:
                        q_low(n + 3, 1 - par, 1)
                    if j == 3 and not last:
                        q_low(n + 3, 1 - par, 2)
                        q_low(n + 4, 1 - par, 3)

            group(0, 0, 0, first=True)
            with dve.Fori(1, KVH - 2, 2) as g:
                group(g, 1, 0)
                group(g + 1, 0, 0)
            group(KVH - 1, 1, 0)
            group(KVH, 0, 0)
            with dve.Fori(KVH + 1, GROUPS - 2, 2) as g:
                group(g, 1, 1)
                group(g + 1, 0, 1)
            group(GROUPS - 1, 1, 1, last=True)
            L = GROUPS - 1
            norm(HEADS - 2, 2 * L + 1, 1, 0)
            norm(HEADS - 1, 2 * L + 1, 1, 1)

            def residual(b):
                a, xb = acc[:, b * T:(b + 1) * T, :], xs[:, b * T:(b + 1) * T, :]
                dve.tensor_tensor(a, a, gates[:, b, :].unsqueeze(1).broadcast_to([P, T, D]), ALU.mult).then_inc(r_mul, 1)
                dve.wait_ge(r_mul, b + 1)
                dve.tensor_tensor(xb, xb, a, ALU.add).then_inc(r_add, 1)
                dve.wait_ge(r_add, b + 1)
            residual(0)
            row_stats(0, B)
            normalise(0, 1, xn)
            for half in range(2):
                op_add(L, 1, half, (M1, M0)[half])
            dve.wait_ge(op_added, 2 * GROUPS)
            residual(1)
            row_stats(1, B)
            normalise(1, 1, xn2)

            for b in range(B):
                def one(i):
                    return fsm[:, i, :, :]

                def col(i):
                    return fs1[:, i, :].unsqueeze(2).broadcast_to([P, T, E])
                revb = rev[:, :].unsqueeze(1).broadcast_to([P, T, E])
                k = b + 1
                dve.wait_ge(fs["gate_mm"], k)
                dve.tensor_copy(one(0).rearrange("p t e -> p (t e)"), ps[:, 4, 0:T * E]).then_inc(fs["lg"], 1)
                dve.wait_ge(fs["lg"], k)

                def first_max(logits, oh, vmax, s_v, s_eq, s_rv, s_fi, s_oh, scratch):
                    dve.tensor_reduce(fs1[:, vmax, :], one(logits), AX.X, ALU.max).then_inc(fs[s_v], 1)
                    dve.wait_ge(fs[s_v], k)
                    dve.tensor_tensor(one(scratch), one(logits), col(vmax), ALU.is_equal).then_inc(fs[s_eq], 1)
                    dve.wait_ge(fs[s_eq], k)
                    dve.tensor_tensor(one(scratch + 1), one(scratch), revb, ALU.mult).then_inc(fs[s_rv], 1)
                    dve.wait_ge(fs[s_rv], k)
                    dve.tensor_reduce(fs1[:, vmax + 8, :], one(scratch + 1), AX.X, ALU.max).then_inc(fs[s_fi], 1)
                    dve.wait_ge(fs[s_fi], k)
                    dve.tensor_tensor(one(oh), one(scratch + 1), col(vmax + 8), ALU.is_equal).then_inc(fs[s_oh], 1)
                    dve.wait_ge(fs[s_oh], k)

                first_max(0, 1, 0, "v1", "eq", "rv", "fi", "oh1", 4)
                dve.scalar_tensor_tensor(out=one(2), in0=one(1), scalar=-3.0e38, in1=one(0), op0=ALU.mult, op1=ALU.add)\
                   .then_inc(fs["mk2"], 1)
                dve.wait_ge(fs["mk2"], k)
                first_max(2, 3, 1, "v2", "eq2", "rv2", "fi2", "oh2", 6)
                for i, oh in enumerate((1, 3)):
                    o = wide[:, i, :, :].rearrange("p t (e r) -> p t e r", r=R)
                    dve.tensor_scalar(o, one(oh).unsqueeze(3).broadcast_to([P, T, E, R]), LORA_SCALE, None, ALU.mult)\
                       .then_inc(fs["wide"], 1)
                dve.tensor_tensor(fs1[:, 3, :], fs1[:, 1, :], fs1[:, 0, :], ALU.subtract).then_inc(fs["dv"], 1)
                dve.wait_ge(fs["wide"], 2 * b + 2)
                dve.tensor_tensor(wide[:, 2, :, :], wide[:, 1, :, :], wide[:, 0, :, :], ALU.subtract).then_inc(fs["dwide"], 1)
                dve.wait_ge(fs["ex"], k)
                dve.tensor_scalar(fs1[:, 5, :], fs1[:, 4, :], 1.0, None, ALU.add).then_inc(fs["den"], 1)
                dve.wait_ge(fs["den"], 3 * b + 1)
                dve.reciprocal(fs1[:, 6, :], fs1[:, 5, :]).then_inc(fs["den"], 1)
                dve.wait_ge(fs["den"], 3 * b + 2)
                dve.tensor_tensor(fs1[:, 7, :], fs1[:, 4, :], fs1[:, 6, :], ALU.mult).then_inc(fs["den"], 1)
                dve.tensor_copy(wide[:, 3, :, :], fs1[:, 6, :].unsqueeze(2).broadcast_to([P, T, P])).then_inc(fs["w1"], 1)
                dve.wait_ge(fs["den"], 3 * b + 3)
                dve.tensor_copy(wide[:, 4, :, :], fs1[:, 7, :].unsqueeze(2).broadcast_to([P, T, P])).then_inc(fs["w2"], 1)
                for i in range(5):
                    dve.wait_ge(fs["mT_mm"], 5 * b + i + 1)
                    dve.tensor_copy(maskT[:, i, :], ps[:, 4 + i % 2, :]).then_inc(fs["mT"], 1)
                    if i == 0:
                        dve.wait_ge(fs["mT"], 5 * b + 1)
                        dve.wait_ge(fs["t_mm"], k)
                        for c in range(2):
                            dve.tensor_tensor(tmask[:, c, :], ps[:, 6 + c, :], maskT[:, 0, :], ALU.mult).then_inc(fs["tm"], 1)
                    if i == 2:
                        dve.wait_ge(fs["mT"], 5 * b + 3)
                        for c in range(2):
                            dve.tensor_tensor(tmask[:, 2 + c, :], ps[:, 6 + c, :], maskT[:, 2, :], ALU.mult)\
                               .then_inc(fs["tmd"], 1)
                dve.wait_ge(fs["mT"], 5 * b + 5)
                for f in range(FT):
                    m = min(P, F - f * P)
                    i = b * FT + f
                    bank = 2 * (i % 2)
                    for s in range(2):
                        q = 2 * i + s
                        dve.wait_ge(fs["silu"], q + 1)
                        dve.wait_ge(fs["h_mm"] if s == 0 else fs["d_mm"], 2 * i + 2)
                        dve.tensor_tensor(pr[0:m, s, :], ps[0:m, bank + 1, :], sil[0:m, s, :], ALU.mult).then_inc(fs["p"], 1)
                        dve.wait_ge(fs["p"], q + 1)
                        wait(dve, fs["z_mm"], q - 1)
                        if i > 0:
                            dve.wait_ge(fs["g"], i)
                        dve.tensor_tensor(av[0:m, s, :], pr[0:m, s, :], maskT[0:m, 3 + s, :], ALU.mult).then_inc(fs["a"], 1)
                dve.wait_ge(fs["z_mm"], 2 * FT * (b + 1))
                for s in range(2):
                    dve.tensor_tensor(uT[:, s, :], ps[:, 4 + s, :], maskT[:, s, :], ALU.mult).then_inc(fs["zm"], 1)
                dve.wait_ge(fs["zm"], 2 * b + 2)
                dve.tensor_tensor(uT[:, 1, :], uT[:, 1, :], uT[:, 0, :], ALU.add).then_inc(fs["u"], 1)
                gb = gates[:, B + b, :].unsqueeze(1).broadcast_to([P, 2, D])
                for i in range(2):
                    q = 2 * b + i
                    dve.wait_ge(fs["o_mm"], q + 1)
                    y = (y1, y2)[i]
                    dve.tensor_tensor(y, ps[:, 6 + i, :].rearrange("p (t d) -> p t d", t=2), gb, ALU.mult).then_inc(fs["og"], 1)
                    dve.wait_ge(fs["og"], q + 1)
                    xb = xs[:, 2 * q:2 * q + 2, :]
                    dve.tensor_tensor(xb, xb, y, ALU.add).then_inc(fs["o"], 1)

        @block.gpsimd
        def _(pool):
            k_ones = sem("k_ones")
            pool.memset(ident[:, :], 0.0).then_inc(k_ones, 1)
            pool.memset(ident16[:, :], 0.0).then_inc(k_ones, 1)
            pool.memset(causal[:, :], 0.0).then_inc(k_ones, 1)
            pool.memset(src[:, :, :, :, :, :].rearrange("p a b c d e -> p (a b c d e)").bitcast(F32), 0.0).then_inc(k_ones, 1)
            pool.memset(vh[:, :, :, HD:HD + 1], 1.0).then_inc(k_ones, 1)
            pool.memset(acc[:, :, :], 0.0).then_inc(acc_zero, 1)
            for e in range(E):
                pool.memset(rev[:, e:e + 1], float(E - e)).then_inc(k_ones, 1)
            n_ones = 5 + E
            pool.wait_ge(k_ones, n_ones)
            for m in (ident, ident16):
                pool.affine_select(out=m[:, :], in_=m[:, :], compare_op=ALU.not_equal, fill=1.0, base=0,
                                   pattern=[[-1, P]], channel_multiplier=1).then_inc(k_ones, 1)
            diag = causal[:, S - P:S]
            pool.affine_select(out=diag, in_=diag, compare_op=ALU.is_ge, fill=MASKED, base=0,
                               pattern=[[-1, P]], channel_multiplier=1).then_inc(k_ones, 1)
            pool.memset(src[:, :, G, :, 1, HD:HD + 1], SHIFT_UNIT).then_inc(k_ones, 1)
            pool.wait_ge(k_ones, n_ones + 4)
            pool.wait_ge(acc_zero, 1)
            pool.memset(rsum[:, :], 0.0).then_inc(s_const, 1)

            def values(g, par):
                pool.wait_ge(rope_done, 4 * g + 4)
                wait_apart(pool, pv_done, 4 * g - 4, pool_passed)
                v = ra[:, :, ROT:QKV]
                pool.tensor_scalar(vh[:, par, :, 0:HD], v, 1.0, None, ALU.mult).then_inc(vh_ready, 1)
                pool.wait_ge(vh_ready, g + 1)
                pool.tensor_tensor(vl[:, par, :, :], v, vh[:, par, :, 0:HD], ALU.subtract).then_inc(v_ready, 1)

            def split(n, npar):
                for i, (off, step, need) in enumerate(((0, 512, 2), (896, 256, 3))):
                    wait_apart(pool, exp_done, 3 * n + need, pool_passed)
                    if step == 512:
                        v = prob[:, npar, 0:1024].rearrange("p (a c) -> p a c", a=2)[:, :, 0:P]
                    else:
                        v = prob[:, npar, 896:1280].rearrange("p (a c) -> p a c", a=3)[:, 0:3:2, :]
                    ins = pool.affine_select(out=v, in_=v, compare_op=ALU.is_ge, fill=0.0, base=0,
                                             pattern=[[0, 2], [1, P]], channel_multiplier=-1)
                ins.then_inc(sel_done, 1)
                pool.wait_ge(ph_ready, n + 1)
                wait(pool, pv_done, n - 1)
                pool.tensor_tensor(pl[:, npar, :], prob[:, npar, :], ph[:, npar, :], ALU.subtract).then_inc(pl_ready, 1)

            values(0, 0)

            def group(g, par, last=False):
                for j in range(G):
                    split(4 * g + j, j % 2)
                    if j == 2 and not last:
                        values(g + 1, 1 - par)

            group(0, 0)
            with pool.Fori(1, KVH - 2, 2) as g:
                group(g, 1)
                group(g + 1, 0)
            group(KVH - 1, 1)
            group(KVH, 0)
            with pool.Fori(KVH + 1, GROUPS - 2, 2) as g:
                group(g, 1)
                group(g + 1, 0)
            group(GROUPS - 1, 1, last=True)
            for i in range(B * FT):
                f = i % FT
                m = min(P, F - f * P)
                pool.wait_ge(fs["a"], 2 * i + 2)
                if f == 0 and i > 0:
                    pool.wait_ge(fs["o_mm"], 2)
                pool.tensor_tensor(gsum[0:m, f, :], av[0:m, 0, :], av[0:m, 1, :], ALU.add).then_inc(fs["g"], 1)


def kernel(L0_attn_hidden_states, L0_attn_Wq, L0_attn_Wk, L0_attn_Wv, L0_attn_Wo, L0_ffn_gate_w, L0_ffn_w1,
           L0_ffn_w3, L0_ffn_w2, L0_ffn_a1, L0_ffn_b1, L0_ffn_a3, L0_ffn_b3, L0_ffn_a2, L0_ffn_b2, L0_c, L0_wmod):
    import concourse.bacc as bacc
    from concourse.bass_utils import run_bass_kernel_spmd

    def con(a):
        return np.ascontiguousarray(a)

    def by_width(a):
        a = np.asarray(a)
        return con(a.T.reshape(-1, P, a.shape[0]).transpose(1, 0, 2))

    wq = np.asarray(L0_attn_Wq).reshape(KVH, G * HD, D)
    wk = np.asarray(L0_attn_Wk).reshape(KVH, HD, D)
    wv = np.asarray(L0_attn_Wv).reshape(KVH, HD, D)
    wqkv = np.concatenate([wq, wk, wv], axis=1)
    wqkv = con(wqkv.transpose(0, 2, 1).reshape(KVH, DK, P, QKV).transpose(0, 2, 1, 3))
    wo = con(np.asarray(L0_attn_Wo).T.reshape(H // 2, P, D).transpose(1, 0, 2))
    inv = (np.float32(1.0) / np.float32(10000.0) ** (np.arange(0, HD, 2, dtype=np.float32) / np.float32(HD)))
    ang = np.arange(S, dtype=np.float32)[:, None] * inv.astype(np.float32)[None, :]
    c1, s1 = np.cos(ang).astype(np.float32), np.sin(ang).astype(np.float32)
    cos = np.concatenate([np.tile(np.concatenate([c1, c1], 1), (1, G + 1)), np.ones((S, HD), np.float32)], 1)
    sin = np.tile(np.concatenate([s1, -s1], 1), (1, G + 1))
    by_token = lambda a: con(a.reshape(T, P, -1).transpose(1, 0, 2))
    a1, a3, a2 = (np.asarray(v) for v in (L0_ffn_a1, L0_ffn_a3, L0_ffn_a2))
    b1, b3, b2 = (con(np.asarray(v).transpose(0, 2, 1).reshape(E * R, -1)) for v in (L0_ffn_b1, L0_ffn_b3, L0_ffn_b2))
    arrays = {
        "x": con(L0_attn_hidden_states), "wqkv": wqkv, "wo": wo, "cos": by_token(cos), "sin": by_token(sin),
        "cT": by_width(L0_c), "wmod": con(np.asarray(L0_wmod).reshape(DK, P, 6 * D).transpose(1, 0, 2)),
        "w1T": by_width(L0_ffn_w1), "w3T": by_width(L0_ffn_w3), "w2T": con(np.asarray(L0_ffn_w2).T),
        "gateT": by_width(L0_ffn_gate_w), "a1T": by_width(a1.reshape(E * R, D)), "a3T": by_width(a3.reshape(E * R, D)),
        "b1T": b1, "b3T": b3, "a2T": con(a2.reshape(E * R, F).T), "b2T": b2,
    }
    nc = bacc.Bacc("TRN2", target_bir_lowering=False, num_devices=1)
    args = [nc.dram_tensor(k, a.shape, mybir.dt.from_np(a.dtype), kind="ExternalInput").ap() for k, a in arrays.items()]
    args.append(nc.dram_tensor("out", (B, S, D), F32, kind="ExternalOutput").ap())
    block_kernel(nc, *args)
    r = run_bass_kernel_spmd(nc, [arrays], core_ids=[0])
    return r.results[0]["out"]
```

```python
from contextlib import ExitStack

import numpy as np

import concourse.bass as bass
from concourse import mybir

F32 = mybir.dt.float32
F16 = mybir.dt.float16
ALU = mybir.AluOpType
ACT = mybir.ActivationFunctionType
AX = mybir.AxisListType

P = 128
B, S, D = 2, 512, 256
H, KVH, HD = 32, 8, 64
F, E, R = 704, 8, 16
T = S // P
DK = D // P
G = H // KVH
GROUPS = B * KVH
HEADS = B * H
QKV = (G + 2) * HD
ROT = (G + 1) * HD
FT = -(-F // P)
EPS = 1e-5
SHIFT_UNIT = 64.0
SHIFT_BIAS = 4.0 * HD ** 0.5 / SHIFT_UNIT
MASKED = -1.0e30
KEY_OFF = [0, 512, 896, 1152]
PROBS = 1280
LORA_SCALE = 2.0


def wait(eng, sem, value):
    if isinstance(value, int) and value < 1:
        return
    eng.wait_ge(sem, value)


def wait_apart(eng, sem, value, passed):
    wait(eng, sem, value)
    eng.sem_inc(passed, 1)


def block_kernel(nc, x, wqkv, wo, cos, sin, cT, wmod, w1T, w3T, w2T, gateT, a1T, a3T, b1T, b3T, a2T, b2T, out):
    ctx = ExitStack()
    with ctx:
        def sb(name, shape, dt=F32):
            return ctx.enter_context(nc.sbuf_tensor(name, shape, dt))

        def sem(name):
            return ctx.enter_context(nc.semaphore(name))

        ps = ctx.enter_context(nc.psum_tensor("ps", [P, 8, 512], F32))
        S1_BANK, ST_BANK, T_BANK, PV_BANK, MISC_BANK = 0, 2, 4, 5, 6

        xs = sb("xs", [P, B * T, D])
        wq_sb = sb("wq_sb", [P, KVH, DK, QKV])
        wo_sb = sb("wo_sb", [P, H // 2, D])
        cos_sb = sb("cos_sb", [P, T, QKV])
        sin_sb = sb("sin_sb", [P, T, ROT])
        hT = sb("hT", [P, B, DK, S])
        acc = sb("acc", [P, B * T, D])
        w1_sb = sb("w1_sb", [P, DK, F])
        w3_sb = sb("w3_sb", [P, DK, F])
        w2_sb = sb("w2_sb", [P, FT, D])
        gate_sb = sb("gate_sb", [P, DK, E])
        a1_sb = sb("a1_sb", [P, DK, P])
        a3_sb = sb("a3_sb", [P, DK, P])
        b1_sb = sb("b1_sb", [P, F])
        b3_sb = sb("b3_sb", [P, F])
        a2_sb = sb("a2_sb", [P, FT, P])
        b2_sb = sb("b2_sb", [P, D])
        ident = sb("ident", [P, P])
        ident16 = sb("ident16", [P, P], F16)
        causal = sb("causal", [P, S])
        gates = sb("gates", [P, 2 * B, D])
        modT = sb("modT", [P, 12, B])
        c_sb = sb("c_sb", [P, DK, B])
        c_e = sb("c_e", [P, DK, B])
        c_s = sb("c_s", [P, DK, B])
        stats = sb("stats", [P, B * T, 6])
        mv = sb("mv", [P, B * T, 2])
        ve = sb("ve", [P, B * T])
        sd = sb("sd", [P, B * T])
        rstd = sb("rstd", [P, B * T])
        nrt = sb("nrt", [P, B * T])
        g_sign = sb("g_sign", [P, 4, B])
        g_abs = sb("g_abs", [P, 4, B])

        ra = sb("ra", [P, 2, T, QKV])
        rb = sb("rb", [P, T, ROT])
        rot = sb("rot", [P, T, G + 1, HD])
        src = sb("src", [P, 2, G + 1, T, 2, P], F16)
        qT = sb("qT", [P, 2, 2, S], F16)
        kT = sb("kT", [P, 2, 2, S], F16)
        vh = sb("vh", [P, 2, T, HD + 1], F16)
        vl = sb("vl", [P, 2, T, HD], F16)
        prob = sb("prob", [P, 2, PROBS])
        ph = sb("ph", [P, 2, PROBS], F16)
        pl = sb("pl", [P, 2, PROBS], F16)
        mx = sb("mx", [P, 2, T])
        rsum = sb("rsum", [P, T])
        on = sb("on", [P, 2, T, 2 * HD])
        oT = sb("oT", [P, 2, 2, S])
        junk = sb("junk", [P, PROBS], F16)

        def over(t, shape):
            flat = t[tuple([slice(None)] * len(t.shape))]
            names = " ".join("abcdefg"[:len(t.shape) - 1])
            flat = flat.rearrange(f"p {names} -> p ({names})") if len(t.shape) > 2 else flat
            if t.dtype != F32:
                flat = flat.bitcast(F32)
            n = int(np.prod(shape[1:]))
            flat = flat[:, 0:n]
            if len(shape) == 3:
                flat = flat.rearrange("p (a b) -> p a b", a=shape[1])
            if len(shape) == 4:
                flat = flat.rearrange("p (a b c) -> p a b c", a=shape[1], b=shape[2])
            return flat

        wmod_sb = over(prob, [P, DK, 1024])
        wmod_gb = over(ph, [P, DK, 512])
        xn = over(ra, [P, T, D])
        xn2 = over(rb, [P, T, D])
        gwide = over(pl, [P, 4, P])
        gwide2 = over(oT, [P, 4, P])

        ld_x, ld_c, ld_mod, ld_rope, ld_wo, ld_ffn = (sem(f"ld_{k}") for k in ("x", "c", "mod", "rope", "wo", "ffn"))
        ld_w = sem("ld_w")
        s_const = sem("s_const")
        c_exp, c_one, c_rec, c_silu = (sem(f"c_{k}") for k in ("exp", "one", "rec", "silu"))
        mod_mm, mod_sb = sem("mod_mm"), sem("mod_sb")
        mod_add = sem("mod_add")
        ln_stat, ln_aggr, ln_eps, ln_sqrt, ln_rec = (sem(f"ln_{k}") for k in ("stat", "aggr", "eps", "sqrt", "rec"))
        ln_n1, ln_n2, ln_rstd, xn_ready, xnT_mm, hT_ready = (
            sem(k) for k in ("ln_n1", "ln_n2", "ln_rstd", "xn_ready", "xnT_mm", "hT_ready"))
        g_s, g_a, g_m, g_wide, g_mm, g_ready = (sem(f"g_{k}") for k in ("s", "a", "m", "wide", "mm", "ready"))
        proj_done, rope_done, rotk_ready, rotq_ready = (
            sem(k) for k in ("proj_done", "rope_done", "rotk_ready", "rotq_ready"))
        kh_ready, kl_ready, qh_ready, ql_ready = (sem(k) for k in ("kh_ready", "kl_ready", "qh_ready", "ql_ready"))
        vh_ready, v_ready = sem("vh_ready"), sem("v_ready")
        tk_done, tk_evac, ta_done, ta_evac, tb_done, tb_evac = (
            sem(k) for k in ("tk_done", "tk_evac", "ta_done", "ta_evac", "tb_done", "tb_evac"))
        s1_done, maxed, m_ready = sem("s1_done"), sem("maxed"), sem("m_ready")
        st_done, exp_done, sel_done, ph_ready, pl_ready = (
            sem(k) for k in ("st_done", "exp_done", "sel_done", "ph_ready", "pl_ready"))
        pv_done, rsum_ready, normed = sem("pv_done"), sem("rsum_ready"), sem("normed")
        ot_done, ot_evac, op_done, op_added = (sem(k) for k in ("ot_done", "ot_evac", "op_done", "op_added"))
        acc_zero = sem("acc_zero")
        dve_passed, pool_passed = sem("dve_passed"), sem("pool_passed")
        r_mul, r_add = sem("r_mul"), sem("r_add")
        fs = {k: sem("f_" + k) for k in (
            "h2", "gate_mm", "lg", "v1", "eq", "rv", "fi", "oh1", "mk2", "v2", "eq2", "rv2", "fi2", "oh2",
            "dv", "ex", "den", "w1", "w2", "wide", "dwide", "mT_mm", "mT", "t_mm", "tm", "tmd",
            "h_mm", "silu", "p", "a", "g", "d_mm", "z_mm", "zm", "u", "o_mm", "og", "o")}
        stored = sem("stored")

        block = ctx.enter_context(nc.Block())

        fsm = sb("fsm", [P, 8, T, E])
        fs1 = sb("fs1", [P, 12, T])
        rev = sb("rev", [P, E])
        wide = over(src, [P, 5, T, P])
        maskT = over(wq_sb, [P, 5, S])
        wq_flat = over(wq_sb, [P, KVH * DK * QKV])

        def wq_part(at, shape):
            n = int(np.prod(shape[1:]))
            v = wq_flat[:, at:at + n]
            if len(shape) == 3:
                v = v.rearrange("p (a b) -> p a b", a=shape[1])
            return v
        tmask = over(prob, [P, 4, S])
        gsum = wq_part(5 * S, [P, FT, S])
        assert 5 * S + FT * S <= KVH * DK * QKV
        sil = over(ra, [P, 2, S])
        pr = over(rb, [P, 2, S])
        av = over(rot, [P, 2, S])
        uT = over(on, [P, 2, S])
        y1 = over(ph, [P, 2, D])
        y2 = over(pl, [P, 2, D])

        def form(par, item, t, ab):
            return src[:, par, item, t, ab, :]

        @block.sync
        def _(sp):
            xv = x.rearrange("b (t p) d -> p (b t) d", p=P)
            sp.dma_start(xs[:, 0:T, :], xv[:, 0:T, :]).then_inc(ld_x, 16)
            sp.dma_start(wmod_sb, wmod[:, :, 0:1024]).then_inc(ld_mod, 16)
            sp.dma_start(wmod_gb, wmod[:, :, 1024:1536]).then_inc(ld_mod, 16)
            for g in range(1, KVH):
                sp.dma_start(wq_sb[:, g, :, :], wqkv[g]).then_inc(ld_w, 16)
            sp.dma_start(w1_sb[:, :, :], w1T).then_inc(ld_ffn, 16)
            sp.dma_start(w3_sb[:, :, :], w3T).then_inc(ld_ffn, 16)
            full = F // P
            sp.dma_start(w2_sb[:, 0:full, :], w2T[0:full * P, :].rearrange("(f p) d -> p f d", p=P)).then_inc(ld_ffn, 16)
            sp.dma_start(w2_sb[0:F - full * P, full, :], w2T[full * P:F, :]).then_inc(ld_ffn, 16)
            sp.dma_start(a2_sb[:, 0:full, :], a2T[0:full * P, :].rearrange("(f p) d -> p f d", p=P)).then_inc(ld_ffn, 16)
            sp.dma_start(a2_sb[0:F - full * P, full, :], a2T[full * P:F, :]).then_inc(ld_ffn, 16)
            for dst, s in ((gate_sb, gateT), (a1_sb, a1T), (a3_sb, a3T)):
                sp.dma_start(dst[:, :, :], s).then_inc(ld_ffn, 16)
            for dst, s in ((b1_sb, b1T), (b3_sb, b3T), (b2_sb, b2T)):
                sp.dma_start(dst[:, :], s).then_inc(ld_ffn, 16)
            ov = out.rearrange("b (t p) d -> p (b t) d", p=P)
            for i in range(B * T // 2):
                sp.wait_ge(fs["o"], i + 1)
                sp.dma_start(ov[:, 2 * i:2 * i + 2, :], xs[:, 2 * i:2 * i + 2, :]).then_inc(stored, 16)
            sp.wait_ge(stored, 16 * (B * T // 2))

        @block.tensor
        def _(pe):
            pe.wait_ge(c_silu, 1)
            pe.wait_ge(ld_mod, 32)
            for ch in range(12):
                for k in range(DK):
                    w = wmod_sb[:, k, ch * P:(ch + 1) * P] if ch < 8 else wmod_gb[:, k, (ch - 8) * P:(ch - 7) * P]
                    mm = pe.matmul(ps[:, PV_BANK, 2 * ch:2 * ch + 2], w, c_s[:, k, :], start=(k == 0), stop=(k == DK - 1))
            mm.then_inc(mod_mm, 1)
            pe.wait_ge(s_const, 1)

            def transpose_rows(b, bank0, buf, done, count):
                for k in range(DK):
                    for t in range(T):
                        if k == 0:
                            pe.wait_ge(xn_ready, count + t + 1)
                        mm = pe.transpose(ps[:, bank0 + k, t * P:(t + 1) * P], buf[:, t, k * P:(k + 1) * P], ident[:, :])
                    mm.then_inc(done, 1)

            transpose_rows(0, 0, xn, xnT_mm, 0)
            transpose_rows(1, 2, xn2, xnT_mm, T)

            def project(g, w, b, t, bank):
                for k in range(DK):
                    mm = pe.matmul(ps[:, bank, 0:QKV], hT[:, b, k, t * P:(t + 1) * P], wq_sb[:, w, k, :],
                                   start=(k == 0), stop=(k == DK - 1))
                mm.then_inc(proj_done, 1)

            def tk(g, par):
                pe.wait_ge(kh_ready, g + 1)
                pe.wait_ge(kl_ready, g + 1)
                for ab in range(2):
                    for t in range(T):
                        mm = pe.transpose(ps[:, T_BANK, ab * 256 + t * 64:ab * 256 + (t + 1) * 64].bitcast(F16),
                                          form(par, G, t, ab), ident16[:, :])
                mm.then_inc(tk_done, 1)

            def tq(par, item, ab, done):
                for t in range(T):
                    mm = pe.transpose(ps[:, T_BANK, t * 64:(t + 1) * 64].bitcast(F16), form(par, item, t, ab), ident16[:, :])
                mm.then_inc(done, 1)

            def ta(m, par, item):
                pe.wait_ge(qh_ready, m + 1)
                tq(par, item, 0, ta_done)

            def tb(m, par, item):
                pe.wait_ge(ql_ready, m + 1)
                pe.wait_ge(m_ready, m + 1)
                tq(par, item, 1, tb_done)

            def s1(m, mpar, kpar, f):
                bank = S1_BANK + (mpar + f) % 2
                wait(pe, maxed, 3 * m + f - 1)
                off = 0
                for qt in ([3], [2], [0, 1])[f]:
                    n = (qt + 1) * P
                    mm = pe.matmul(ps[:, bank, off:off + n], qT[:, mpar, 0, qt * P:(qt + 1) * P], kT[:, kpar, 0, 0:n],
                                   start=True, stop=True)
                    off += n
                mm.then_inc(s1_done, 1)

            def st(n, npar, kpar, f):
                bank = ST_BANK + (npar + f) % 2
                wait(pe, exp_done, 3 * n + f - 1)
                off = 0
                for kt in ([0], [1], [2, 3])[f]:
                    w = S - kt * P
                    for ab in range(2):
                        mm = pe.matmul(ps[:, bank, off:off + w], kT[:, kpar, ab, kt * P:(kt + 1) * P],
                                       qT[:, npar, ab, kt * P:S], start=(ab == 0), stop=(ab == 1))
                    off += w
                mm.then_inc(st_done, 1)

            def pv(n, npar, g, vpar):
                pe.wait_ge(ph_ready, n + 1)
                pe.wait_ge(pl_ready, n + 1)
                pe.wait_ge(v_ready, g + 1)
                wait(pe, normed, n)
                for qt in range(T):
                    at = qt * (HD + 1)
                    for kt in range(qt + 1):
                        c = KEY_OFF[kt] + (qt - kt) * P
                        first, last = kt == 0, kt == qt
                        pe.matmul(ps[:, PV_BANK, at:at + HD + 1], ph[:, npar, c:c + P], vh[:, vpar, kt, :],
                                  start=first, stop=False)
                        pe.matmul(ps[:, PV_BANK, at:at + HD], ph[:, npar, c:c + P], vl[:, vpar, kt, :],
                                  start=False, stop=False)
                        mm = pe.matmul(ps[:, PV_BANK, at:at + HD + 1], pl[:, npar, c:c + P], vh[:, vpar, kt, :],
                                       start=False, stop=last)
                mm.then_inc(pv_done, 1)

            def ot(pair, p, bank):
                pe.wait_ge(normed, 2 * pair + 2)
                for t in range(T):
                    mm = pe.transpose(ps[:, bank, t * P:(t + 1) * P], on[:, p, t, :], ident[:, :])
                mm.then_inc(ot_done, 1)

            def op(gg, g, par, t, bank):
                pe.wait_ge(ot_evac, 2 * gg + 2)
                for p in range(2):
                    mm = pe.matmul(ps[:, bank, 0:D], oT[:, par, p, t * P:(t + 1) * P],
                                   wo_sb[:, 2 * g + p, :], start=(p == 0), stop=(p == 1))
                mm.then_inc(op_done, 1)

            M0, M1 = MISC_BANK, MISC_BANK + 1
            pe.wait_ge(ld_w, 16)
            for t in range(T):
                if t == 0:
                    pe.wait_ge(hT_ready, 2)
                if t >= 2:
                    pe.wait_ge(rope_done, t - 1)
                project(0, 0, 0, t, MISC_BANK + t % 2)
            pe.wait_ge(hT_ready, 2 * B)
            pe.wait_ge(g_wide, 2)
            for i in range(4 * B):
                kind, b, k = i // 4, (i // 2) % 2, i % 2
                wd = (gwide if kind == 0 else gwide2)[:, 2 * b + k, :]
                mm = pe.transpose(ps[:, 2 * (i // 4) % 4, (i % 4) * P:(i % 4 + 1) * P], wd, ident[:, :])
            mm.then_inc(g_mm, 1)
            for t in range(T - 1):
                pe.wait_ge(rope_done, t + 3)
                project(1, 0, 1, t, MISC_BANK + t % 2)
            tk(0, 0)
            pe.wait_ge(tk_evac, 1)
            ta(0, 0, 0)
            pe.wait_ge(ta_evac, 1)
            ta(1, 0, 1)
            pe.wait_ge(ta_evac, 2)
            pe.wait_ge(g_ready, 2)
            for f in range(3):
                s1(0, 0, 0, f)
            tb(0, 0, 0)
            pe.wait_ge(ld_w, 16 * KVH)
            pe.wait_ge(ld_wo, 16)

            def group(g, b, known=None):
                gg, par = 2 * g + b, b
                before = known if known is not None else 2
                after = GROUPS - 1 - known if known is not None else 2
                for j in range(G):
                    n, jp = 4 * gg + j, j % 2
                    more1, more2 = after > 0 or j < 3, after > 0 or j < 2
                    par1, item1 = (par, j + 1) if j < 3 else (1 - par, 0)
                    par2, item2 = (par, j + 2) if j < 2 else (1 - par, j - 2)
                    pe.wait_ge(tb_evac, n + 1)
                    if more1:
                        pe.wait_ge(ta_evac, n + 2)
                        if j == 3:
                            pe.wait_ge(tk_evac, gg + 2)
                    for f in range(3):
                        if more1:
                            s1(n + 1, 1 - jp, par1, f)
                        st(n, jp, par, f)
                    if j == 2 and after:
                        tk(gg + 1, 1 - par)
                    elif more2:
                        ta(n + 2, par2, item2)
                    if j == 0 and after > 0:
                        if before < 2:
                            pe.wait_ge(rope_done, 4 * gg + 7)
                        wait(pe, op_added, 4 * gg - 6)
                        project(gg + 1, g + b, 1 - b, 3, M0)
                    if j > 0 and after > 1:
                        if j == 1:
                            pe.wait_ge(rope_done, 4 * gg + 8)
                        elif j == 2:
                            wait(pe, ot_evac, 2 * gg - 1)
                            wait(pe, op_added, 4 * gg - 4)
                        else:
                            pe.wait_ge(rope_done, 4 * gg + 10)
                        project(gg + 2, g + 1, b, j - 1, M0 if j == 1 else M1)
                    if j == 2 and after:
                        pe.wait_ge(tk_evac, gg + 2)
                        ta(n + 2, par2, item2)
                    if j == 0 and before > 1:
                        pe.wait_ge(ot_evac, 2 * gg - 1)
                        op(gg - 2, g - 1, par, 2, M1)
                    if j == 1 and before > 1:
                        pe.wait_ge(op_added, 4 * gg - 5)
                        op(gg - 2, g - 1, par, 3, M1)
                    if j == 2 and before > 0:
                        op(gg - 1, g + b - 1, 1 - par, 0, M0)
                    if j == 3 and before > 0:
                        pe.wait_ge(op_added, 4 * gg - 3)
                        op(gg - 1, g + b - 1, 1 - par, 1, M0)
                    if j == 1 and before > 0:
                        if after > 1:
                            pe.wait_ge(rope_done, 4 * gg + 9)
                        else:
                            pe.wait_ge(rope_done, 4 * GROUPS)
                            pe.wait_ge(op_added, 4 * gg - 6)
                        ot(2 * gg - 1, 1, M0)
                    if j == 3:
                        if after > 1:
                            pe.wait_ge(rope_done, 4 * gg + 11)
                        else:
                            pe.wait_ge(op_added, 4 * gg - 4)
                        ot(2 * gg, 0, M1)
                    if more1:
                        if more2:
                            pe.wait_ge(ta_evac, n + 3)
                        tb(n + 1, par1, item1)
                    if before > 0 or j > 0:
                        gp, vpar = (gg, par) if j > 0 else (gg - 1, 1 - par)
                        pv(n - 1, 1 - jp, gp, vpar)

            group(0, 0, 0)
            group(0, 1, 1)
            with pe.Fori(1, KVH - 1) as g:
                group(g, 0)
                group(g, 1)
            group(KVH - 1, 0, GROUPS - 2)
            group(KVH - 1, 1, GROUPS - 1)
            L = GROUPS - 1
            pv(HEADS - 1, 1, L, 1)
            for t in (2, 3):
                pe.wait_ge(ot_evac, 2 * L + 1)
                pe.wait_ge(op_added, 4 * L - 4 + t)
                op(L - 1, KVH - 1, 0, t, M1)
            ot(2 * L + 1, 1, M0)
            for t in range(T):
                pe.wait_ge(op_added, 4 * L - 1 + t)
                op(L, KVH - 1, 1, t, MISC_BANK + t % 2)

            pe.wait_ge(maxed, 3 * HEADS)
            pe.wait_ge(exp_done, 3 * HEADS)
            for b in range(B):
                transpose_rows(b, 2 * b, (xn, xn2)[b], xnT_mm, (B + b) * T)
            pe.wait_ge(ld_ffn, 16 * 12)
            for b in range(B):
                pe.wait_ge(fs["h2"], 2 * (b + 1))
                if b == 0:
                    pe.wait_ge(tb_evac, HEADS)
                else:
                    pe.wait_ge(fs["zm"], 2)
                for t in range(T):
                    for k in range(DK):
                        mm = pe.matmul(ps[:, 4, t * E:(t + 1) * E], hT[:, b, k, t * P:(t + 1) * P], gate_sb[:, k, :],
                                       start=(k == 0), stop=(k == DK - 1))
                mm.then_inc(fs["gate_mm"], 1)
                if b == 0:
                    pe.wait_ge(op_added, 4 * GROUPS)
                else:
                    pe.wait_ge(fs["o"], 2)
                for i, a in enumerate((a1_sb, a3_sb)):
                    for k in range(DK):
                        mm = pe.matmul(ps[:, 6 + i, :], a[:, k, :], hT[:, b, k, :], start=(k == 0), stop=(k == DK - 1))
                mm.then_inc(fs["t_mm"], 1)
                for i in range(5):
                    if i < 3:
                        pe.wait_ge(fs["wide"] if i < 2 else fs["dwide"], (2 * b + i + 1) if i < 2 else b + 1)
                    else:
                        pe.wait_ge(fs["wide"], 2 * b + 2)
                    if i == 0:
                        pe.wait_ge(fs["lg"], b + 1)
                    if i == 1:
                        if b == 0:
                            pe.wait_ge(normed, HEADS)
                        else:
                            pe.wait_ge(fs["zm"], 2)
                    if i >= 2:
                        pe.wait_ge(fs["mT"], 5 * b + i - 1)
                    if i == 3:
                        pe.wait_ge(fs["w1"], b + 1)
                    if i == 4:
                        pe.wait_ge(fs["w2"], b + 1)
                    for t in range(T):
                        mm = pe.transpose(ps[:, 4 + i % 2, t * P:(t + 1) * P], wide[:, i, t, :], ident[:, :])
                    mm.then_inc(fs["mT_mm"], 1)
                def z_product(f, s):
                    m = min(P, F - f * P)
                    pe.wait_ge(fs["a"], 2 * (b * FT + f) + s + 1)
                    if f == 0 and s == 0:
                        pe.wait_ge(fs["mT"], 5 * b + 5)
                    mm = pe.matmul(ps[:, 4 + s, :], a2_sb[0:m, f, :], av[0:m, s, :], start=(f == 0), stop=(f == FT - 1))
                    mm.then_inc(fs["z_mm"], 1)

                for f in range(FT):
                    m = min(P, F - f * P)
                    i = b * FT + f
                    bank = 2 * (i % 2)
                    if b == 0 and f < 2:
                        pe.wait_ge(fs["h2"], 2 * B)
                    else:
                        pe.wait_ge(fs["p"], 2 * (i - 2) + 2)
                    fc = slice(f * P, f * P + m)
                    if f == 0:
                        pe.wait_ge(fs["tm"], 2 * b + 2)
                    for c, (w, bb) in enumerate(((w1_sb, b1_sb), (w3_sb, b3_sb))):
                        for k in range(DK):
                            pe.matmul(ps[0:m, bank + c, :], w[:, k, fc], hT[:, b, k, :], start=(k == 0), stop=False)
                        mm = pe.matmul(ps[0:m, bank + c, :], bb[:, fc], tmask[:, c, :], start=False, stop=True)
                        mm.then_inc(fs["h_mm"], 1)
                    if f > 0:
                        z_product(f - 1, 1)
                    pe.wait_ge(fs["p"], 2 * i + 1)
                    if f == 0:
                        pe.wait_ge(fs["tmd"], 2 * b + 2)
                    for c, bb in enumerate((b1_sb, b3_sb)):
                        mm = pe.matmul(ps[0:m, bank + c, :], bb[:, fc], tmask[:, 2 + c, :], start=False, stop=True,
                                       skip_group_check=True)
                        mm.then_inc(fs["d_mm"], 1)
                    z_product(f, 0)
                z_product(FT - 1, 1)
                pe.wait_ge(fs["g"], FT * (b + 1))
                pe.wait_ge(fs["u"], b + 1)
                for i in range(2):
                    for t in range(2 * i, 2 * i + 2):
                        at = (t % 2) * D
                        for f in range(FT):
                            m = min(P, F - f * P)
                            pe.matmul(ps[:, 6 + i, at:at + D], gsum[0:m, f, t * P:(t + 1) * P], w2_sb[0:m, f, :],
                                      start=(f == 0), stop=False)
                        mm = pe.matmul(ps[:, 6 + i, at:at + D], uT[:, 1, t * P:(t + 1) * P], b2_sb[:, :],
                                       start=False, stop=True)
                    mm.then_inc(fs["o_mm"], 1)

        @block.scalar
        def _(act):
            act.dma_start(c_sb[:, :, :], cT).then_inc(ld_c, 16)
            act.dma_start(wq_sb[:, 0, :, :], wqkv[0]).then_inc(ld_w, 16)
            act.dma_start(cos_sb[:, :, :], cos).then_inc(ld_rope, 16)
            act.dma_start(sin_sb[:, :, :], sin).then_inc(ld_rope, 16)
            xv = x.rearrange("b (t p) d -> p (b t) d", p=P)
            act.dma_start(xs[:, T:2 * T, :], xv[:, T:2 * T, :]).then_inc(ld_x, 16)
            act.dma_start(wo_sb[:, :, :], wo).then_inc(ld_wo, 16)
            act.wait_ge(ld_c, 16)
            act.activation(c_e[:, :, :], c_sb[:, :, :], ACT.Exp, scale=-1.0).then_inc(c_exp, 1)
            for b in range(B):
                act.wait_ge(ln_eps, b + 1)
                act.activation(sd[:, b * T:(b + 1) * T], ve[:, b * T:(b + 1) * T], ACT.Sqrt).then_inc(ln_sqrt, 1)

            def modulate(b, bank0, add, done, base):
                for k in range(DK):
                    act.wait_ge(xnT_mm, base + 2 * b + k + 1)
                    act.activation(hT[:, b, k, :], ps[:, bank0 + k, :], ACT.Identity, bias=modT[:, add + k, b:b + 1],
                                   scale=modT[:, add + 2 + k, b:b + 1]).then_inc(done, 1)

            act.wait_ge(mod_add, 2)
            for b in range(B):
                modulate(b, 2 * b, 0, hT_ready, 0)

            def k_high(g, par):
                act.wait_ge(rotk_ready, g + 1)
                act.activation(src[:, par, G, :, :, 0:HD],
                               rot[:, :, G, :].unsqueeze(2).broadcast_to([P, T, 2, HD]), ACT.Copy).then_inc(kh_ready, 1)

            def q_high(m, par, item, g):
                act.wait_ge(rotq_ready, g + 1)
                act.activation(src[:, par, item, :, 0, :].rearrange("p t (c d) -> p t c d", c=2),
                               rot[:, :, item, :].unsqueeze(2).broadcast_to([P, T, 2, HD]), ACT.Copy).then_inc(qh_ready, 1)

            def ta_out(m, mpar):
                act.wait_ge(ta_done, m + 1)
                act.activation(qT[:, mpar, 0, :], ps[:, T_BANK, 0:256].bitcast(F16), ACT.Copy).then_inc(ta_evac, 1)

            def exps(n, npar):
                wait(act, pl_ready, n - 1)
                for f in range(3):
                    act.wait_ge(st_done, 3 * n + f + 1)
                    w, off = (512, 384, 384)[f], (0, 512, 896)[f]
                    act.activation(prob[:, npar, off:off + w], ps[:, ST_BANK + (npar + f) % 2, 0:w], ACT.Exp,
                                   scale=HD ** -0.5).then_inc(exp_done, 1)

            def p_high(n, npar):
                act.wait_ge(sel_done, n + 1)
                wait(act, pv_done, n - 1)
                act.activation(ph[:, npar, :], prob[:, npar, :], ACT.Copy).then_inc(ph_ready, 1)

            def ot_out(pair, par, p, bank):
                act.wait_ge(ot_done, pair + 1)
                act.activation(oT[:, par, p, :], ps[:, bank, :], ACT.Copy).then_inc(ot_evac, 1)

            act.wait_ge(s_const, 1)
            k_high(0, 0)
            q_high(0, 0, 0, 0)
            act.wait_ge(g_mm, 1)
            for i in range(2):
                act.activation(gates[:, 2 * i:2 * i + 2, :].rearrange("p a d -> p (a d)"), ps[:, 2 * i, :],
                               ACT.Copy).then_inc(g_ready, 1)
            ta_out(0, 0)
            q_high(1, 0, 1, 0)
            ta_out(1, 1)
            q_high(2, 0, 2, 0)

            def group(g, b, known=None):
                gg, par = 2 * g + b, b
                before = known if known is not None else 2
                after = GROUPS - 1 - known if known is not None else 2
                for j in range(G):
                    n, jp = 4 * gg + j, j % 2
                    exps(n, jp)
                    if j != 2 and (after > 0 or j < 2):
                        ta_out(n + 2, jp)
                    if j == 1 and after > 0:
                        k_high(gg + 1, 1 - par)
                    p_high(n, jp)
                    if j == 2 and after > 0:
                        ta_out(n + 2, jp)
                    if j == 1 and before > 0:
                        ot_out(2 * gg - 1, 1 - par, 1, MISC_BANK)
                    if j == 0:
                        q_high(n + 3, par, 3, gg)
                    elif after > 0:
                        q_high(n + 3, 1 - par, j - 1, gg + 1)
                    if j == 3:
                        ot_out(2 * gg, par, 0, MISC_BANK + 1)

            group(0, 0, 0)
            group(0, 1, 1)
            with act.Fori(1, KVH - 1) as g:
                group(g, 0)
                group(g, 1)
            group(KVH - 1, 0, GROUPS - 2)
            group(KVH - 1, 1, GROUPS - 1)
            ot_out(2 * GROUPS - 1, 1, 1, MISC_BANK)

            for b in range(B):
                act.wait_ge(ln_eps, B + b + 1)
                act.activation(sd[:, b * T:(b + 1) * T], ve[:, b * T:(b + 1) * T], ACT.Sqrt).then_inc(ln_sqrt, 1)
            for b in range(B):
                modulate(b, 2 * b, 6, fs["h2"], 2 * B)
            for b in range(B):
                act.wait_ge(fs["dv"], b + 1)
                act.activation(fs1[:, 4, :], fs1[:, 3, :], ACT.Exp).then_inc(fs["ex"], 1)
                for f in range(FT):
                    m = min(P, F - f * P)
                    i = b * FT + f
                    bank = 2 * (i % 2)
                    for s in range(2):
                        act.wait_ge(fs["h_mm"] if s == 0 else fs["d_mm"], 2 * i + 1)
                        wait(act, fs["p"], 2 * i + s - 1)
                        act.activation(sil[0:m, s, :], ps[0:m, bank, :], ACT.Silu).then_inc(fs["silu"], 1)

        @block.vector
        def _(dve):
            dve.wait_ge(c_exp, 1)
            dve.tensor_scalar(c_e[:, :, :], c_e[:, :, :], 1.0, None, ALU.add).then_inc(c_one, 1)
            dve.wait_ge(c_one, 1)
            dve.reciprocal(c_e[:, :, :], c_e[:, :, :]).then_inc(c_rec, 1)
            dve.wait_ge(c_rec, 1)
            dve.tensor_tensor(c_s[:, :, :], c_sb[:, :, :], c_e[:, :, :], ALU.mult).then_inc(c_silu, 1)

            def row_stats(b, base):
                for t in range(T):
                    i = b * T + t
                    dve.bn_stats(stats[:, i, :], xs[:, i, :]).then_inc(ln_stat, 1)
                for t in range(T):
                    i = b * T + t
                    dve.wait_ge(ln_stat, base * T + i + 1)
                    dve.bn_aggr(mv[:, i, :], stats[:, i, :]).then_inc(ln_aggr, 1)
                dve.wait_ge(ln_aggr, (base + b + 1) * T if base == 0 else (B + b + 1) * T)
                dve.tensor_scalar(ve[:, b * T:(b + 1) * T], mv[:, b * T:(b + 1) * T, 1], EPS, None, ALU.add)\
                   .then_inc(ln_eps, 1)

            def normalise(b, rnd, buf):
                c = slice(b * T, (b + 1) * T)
                k = rnd * B + b + 1
                dve.wait_ge(ln_sqrt, k)
                dve.reciprocal(rstd[:, c], sd[:, c]).then_inc(ln_rec, 1)
                dve.wait_ge(ln_rec, k)
                dve.tensor_tensor(nrt[:, c], rstd[:, c], rstd[:, c], ALU.mult).then_inc(ln_n1, 1)
                dve.wait_ge(ln_n1, 3 * k - 2)
                dve.tensor_tensor(nrt[:, c], nrt[:, c], ve[:, c], ALU.mult).then_inc(ln_n1, 1)
                dve.wait_ge(ln_n1, 3 * k - 1)
                dve.tensor_scalar(nrt[:, c], nrt[:, c], -0.5, 1.5, ALU.mult, ALU.add).then_inc(ln_n1, 1)
                dve.wait_ge(ln_n1, 3 * k)
                dve.tensor_tensor(rstd[:, c], rstd[:, c], nrt[:, c], ALU.mult).then_inc(ln_rstd, 1)
                dve.wait_ge(ln_rstd, k)
                for t in range(T):
                    i = b * T + t
                    dve.tensor_scalar(buf[:, t, :], xs[:, i, :], mv[:, i, 0:1], rstd[:, i:i + 1],
                                      ALU.subtract, ALU.mult).then_inc(xn_ready, 1)

            dve.wait_ge(ld_x, 32)
            row_stats(0, 0)
            row_stats(1, 0)
            normalise(0, 0, xn)
            normalise(1, 0, xn2)
            dve.wait_ge(mod_mm, 1)
            dve.tensor_copy(modT[:, :, :].rearrange("p c b -> p (c b)"), ps[:, PV_BANK, 0:24]).then_inc(mod_sb, 1)
            dve.wait_ge(mod_sb, 1)
            for c in (2, 8):
                dve.tensor_scalar(modT[:, c:c + 2, :], modT[:, c:c + 2, :], 1.0, None, ALU.add).then_inc(mod_add, 1)
            for i, c in enumerate((4, 10)):
                gsrc = modT[:, c:c + 2, :]
                gs, gab = g_sign[:, 2 * i:2 * i + 2, :], g_abs[:, 2 * i:2 * i + 2, :]
                dve.tensor_scalar(gs, gsrc, 0.0, 2.0, ALU.is_ge, ALU.mult).then_inc(g_s, 1)
                dve.wait_ge(g_s, 2 * i + 1)
                dve.tensor_scalar(gs, gs, -1.0, None, ALU.add).then_inc(g_s, 1)
                dve.wait_ge(g_s, 2 * i + 2)
                dve.tensor_tensor(gab, gs, gsrc, ALU.mult).then_inc(g_a, 1)
                dve.wait_ge(g_a, 2 * i + 1)
                dve.tensor_scalar(gab, gab, 0.25, None, ALU.max).then_inc(g_a, 1)
                dve.wait_ge(g_a, 2 * i + 2)
                dve.tensor_tensor(gab, gab, gs, ALU.mult).then_inc(g_m, 1)
                dve.wait_ge(g_m, i + 1)
                dst = (gwide, gwide2)[i].rearrange("p (b k) d -> p b k d", b=B)
                dve.tensor_copy(dst, gab.rearrange("p k b -> p b k").unsqueeze(3).broadcast_to([P, B, 2, P]))\
                   .then_inc(g_wide, 1)

            def rope(g, par, t, bank):
                wait(dve, v_ready, g - 1)
                wait(dve, rotk_ready, g)
                wait(dve, rotq_ready, g)
                dve.wait_ge(proj_done, 4 * g + t + 1)
                dve.tensor_tensor(ra[:, par, t, :], ps[:, bank, 0:QKV], cos_sb[:, t, :], ALU.mult)
                dve.tensor_tensor(rb[:, t, :], ps[:, bank, 0:ROT], sin_sb[:, t, :], ALU.mult).then_inc(rope_done, 1)

            def rotate(par, items, done):
                hw = HD // 2
                for half in range(2):
                    a = ra[:, par, :, 0:ROT].rearrange("p t (h c) -> p t h c", c=HD)[:, :, items, :]
                    s = rb[:, :, :].rearrange("p t (h c) -> p t h c", c=HD)[:, :, items, :]
                    lo, hi = half * hw, (1 - half) * hw
                    ins = dve.tensor_tensor(rot[:, :, items, lo:lo + hw], a[:, :, :, lo:lo + hw], s[:, :, :, hi:hi + hw],
                                            ALU.add)
                ins.then_inc(done, 1)

            def rotate_key(g, par):
                wait(dve, kh_ready, g)
                wait(dve, kl_ready, g)
                dve.wait_ge(rope_done, 4 * g + 4)
                rotate(par, slice(G, G + 1), rotk_ready)

            def rotate_queries(g, par):
                wait(dve, qh_ready, 4 * g)
                wait(dve, ql_ready, 4 * g)
                dve.wait_ge(rope_done, 4 * g + 4)
                rotate(par, slice(0, G), rotq_ready)

            def k_low(g, par):
                dve.wait_ge(kh_ready, g + 1)
                dve.wait_ge(rotk_ready, g + 1)
                dve.tensor_tensor(src[:, par, G, :, 0, HD:P], rot[:, :, G, :], src[:, par, G, :, 0, 0:HD],
                                  ALU.subtract).then_inc(kl_ready, 1)

            def q_low(m, par, item):
                dve.wait_ge(qh_ready, m + 1)
                dve.tensor_tensor(src[:, par, item, :, 1, 0:HD], rot[:, :, item, :], src[:, par, item, :, 0, 0:HD],
                                  ALU.subtract).then_inc(ql_ready, 1)

            def row_max(m, mpar, par, item):
                for f in range(3):
                    wait_apart(dve, s1_done, 3 * m + f + 1, dve_passed)
                    bank = S1_BANK + (mpar + f) % 2
                    off, at = 0, (0, 512, 896)[f]
                    for qt in ([3], [2], [0, 1])[f]:
                        w = (qt + 1) * P
                        ins = dve.tensor_tensor_reduce(junk[:, at + off:at + off + w], ps[:, bank, off:off + w], causal[:, S - w:S], 1.0,
                                                       -3.0e38, ALU.add, ALU.max, mx[:, mpar, qt:qt + 1])
                        off += w
                    ins.then_inc(maxed, 1)
                dve.wait_ge(maxed, 3 * m + 3)
                dve.tensor_scalar(src[:, par, item, :, 1, HD:HD + 1], mx[:, mpar, :].unsqueeze(2), -1.0 / SHIFT_UNIT,
                                  SHIFT_BIAS, ALU.mult, ALU.add).then_inc(m_ready, 1)

            def tb_out(m, mpar):
                dve.wait_ge(tb_done, m + 1)
                dve.tensor_copy(qT[:, mpar, 1, :], ps[:, T_BANK, 0:256].bitcast(F16)).then_inc(tb_evac, 1)

            def tk_out(g, par):
                dve.wait_ge(tk_done, g + 1)
                dve.tensor_copy(kT[:, par, :, :].rearrange("p a s -> p (a s)"), ps[:, T_BANK, :].bitcast(F16))\
                   .then_inc(tk_evac, 1)

            def norm(n, pair, p, half):
                dve.wait_ge(pv_done, n + 1)
                o = ps[:, PV_BANK, 0:T * (HD + 1)].rearrange("p (t c) -> p t c", c=HD + 1)
                dve.reciprocal(rsum[:, :].unsqueeze(2), o[:, :, HD:HD + 1]).then_inc(rsum_ready, 1)
                dve.wait_ge(rsum_ready, n + 1)
                wait(dve, ot_done, pair - 1)
                dve.tensor_tensor(on[:, p, :, half * HD:(half + 1) * HD], o[:, :, 0:HD],
                                  rsum[:, :].unsqueeze(2).broadcast_to([P, T, HD]), ALU.mult).then_inc(normed, 1)

            def op_add(g, b, t, bank):
                a = acc[:, b * T + t, :]
                dve.wait_ge(op_done, 4 * g + t + 1)
                dve.tensor_tensor(a, ps[:, bank, 0:D], a, ALU.add).then_inc(op_added, 1)

            dve.wait_ge(ld_rope, 32)
            dve.wait_ge(s_const, 1)
            dve.wait_ge(xnT_mm, 2 * B)
            for t in range(T):
                rope(0, 0, t, MISC_BANK + t % 2)
            rotate_key(0, 0)
            rotate_queries(0, 0)
            k_low(0, 0)
            for t in range(T - 1):
                rope(1, 1, t, MISC_BANK + t % 2)
            tk_out(0, 0)
            q_low(0, 0, 0)
            row_max(0, 0, 0, 0)
            tb_out(0, 0)
            q_low(1, 0, 1)
            M0, M1 = MISC_BANK, MISC_BANK + 1

            def group(g, b, known=None):
                gg, par = 2 * g + b, b
                before = known if known is not None else 2
                after = GROUPS - 1 - known if known is not None else 2
                for j in range(G):
                    n, jp = 4 * gg + j, j % 2
                    more1, more2 = after > 0 or j < 3, after > 0 or j < 2
                    par1, item1 = (par, j + 1) if j < 3 else (1 - par, 0)
                    par2, item2 = (par, j + 2) if j < 2 else (1 - par, j - 2)
                    if more1:
                        row_max(n + 1, 1 - jp, par1, item1)
                    if j == 2 and after > 0:
                        tk_out(gg + 1, 1 - par)
                    if before > 0 or j > 1:
                        norm(n - 2, 2 * gg - 1 + j // 2, 1 - j // 2, jp)
                    if more2:
                        q_low(n + 2, par2, item2)
                    if j == 1 and after > 0:
                        k_low(gg + 1, 1 - par)
                        rotate_queries(gg + 1, 1 - par)
                    if j == 0 and after > 0:
                        rope(gg + 1, 1 - par, 3, M0)
                    if j > 0 and after > 1:
                        rope(gg + 2, par, j - 1, M0 if j == 1 else M1)
                    if more1:
                        tb_out(n + 1, 1 - jp)
                    if j < 2 and before > 1:
                        op_add(gg - 2, b, j + 2, M1)
                    if j > 1 and before > 0:
                        op_add(gg - 1, 1 - b, j - 2, M0)
                    if j == 0 and after > 0:
                        rotate_key(gg + 1, 1 - par)

            group(0, 0, 0)
            group(0, 1, 1)
            with dve.Fori(1, KVH - 1) as g:
                group(g, 0)
                group(g, 1)
            group(KVH - 1, 0, GROUPS - 2)
            group(KVH - 1, 1, GROUPS - 1)
            L = GROUPS - 1
            norm(HEADS - 2, 2 * L + 1, 1, 0)
            for t in (2, 3):
                op_add(L - 1, 0, t, M1)
            norm(HEADS - 1, 2 * L + 1, 1, 1)

            def residual(b):
                a, xb = acc[:, b * T:(b + 1) * T, :], xs[:, b * T:(b + 1) * T, :]
                dve.tensor_tensor(a, a, gates[:, b, :].unsqueeze(1).broadcast_to([P, T, D]), ALU.mult).then_inc(r_mul, 1)
                dve.wait_ge(r_mul, b + 1)
                dve.tensor_tensor(xb, xb, a, ALU.add).then_inc(r_add, 1)
                dve.wait_ge(r_add, b + 1)
            dve.wait_ge(op_added, 4 * L)
            residual(0)
            row_stats(0, B)
            normalise(0, 1, xn)
            for t in range(T):
                op_add(L, 1, t, MISC_BANK + t % 2)
            dve.wait_ge(op_added, 4 * GROUPS)
            residual(1)
            row_stats(1, B)
            normalise(1, 1, xn2)

            for b in range(B):
                def one(i):
                    return fsm[:, i, :, :]

                def col(i):
                    return fs1[:, i, :].unsqueeze(2).broadcast_to([P, T, E])
                revb = rev[:, :].unsqueeze(1).broadcast_to([P, T, E])
                k = b + 1
                dve.wait_ge(fs["gate_mm"], k)
                dve.tensor_copy(one(0).rearrange("p t e -> p (t e)"), ps[:, 4, 0:T * E]).then_inc(fs["lg"], 1)
                dve.wait_ge(fs["lg"], k)

                def first_max(logits, oh, vmax, s_v, s_eq, s_rv, s_fi, s_oh, scratch):
                    dve.tensor_reduce(fs1[:, vmax, :], one(logits), AX.X, ALU.max).then_inc(fs[s_v], 1)
                    dve.wait_ge(fs[s_v], k)
                    dve.tensor_tensor(one(scratch), one(logits), col(vmax), ALU.is_equal).then_inc(fs[s_eq], 1)
                    dve.wait_ge(fs[s_eq], k)
                    dve.tensor_tensor(one(scratch + 1), one(scratch), revb, ALU.mult).then_inc(fs[s_rv], 1)
                    dve.wait_ge(fs[s_rv], k)
                    dve.tensor_reduce(fs1[:, vmax + 8, :], one(scratch + 1), AX.X, ALU.max).then_inc(fs[s_fi], 1)
                    dve.wait_ge(fs[s_fi], k)
                    dve.tensor_tensor(one(oh), one(scratch + 1), col(vmax + 8), ALU.is_equal).then_inc(fs[s_oh], 1)
                    dve.wait_ge(fs[s_oh], k)

                first_max(0, 1, 0, "v1", "eq", "rv", "fi", "oh1", 4)
                dve.scalar_tensor_tensor(out=one(2), in0=one(1), scalar=-3.0e38, in1=one(0), op0=ALU.mult, op1=ALU.add)\
                   .then_inc(fs["mk2"], 1)
                dve.wait_ge(fs["mk2"], k)
                first_max(2, 3, 1, "v2", "eq2", "rv2", "fi2", "oh2", 6)
                for i, oh in enumerate((1, 3)):
                    o = wide[:, i, :, :].rearrange("p t (e r) -> p t e r", r=R)
                    dve.tensor_scalar(o, one(oh).unsqueeze(3).broadcast_to([P, T, E, R]), LORA_SCALE, None, ALU.mult)\
                       .then_inc(fs["wide"], 1)
                dve.tensor_tensor(fs1[:, 3, :], fs1[:, 1, :], fs1[:, 0, :], ALU.subtract).then_inc(fs["dv"], 1)
                dve.wait_ge(fs["wide"], 2 * b + 2)
                dve.tensor_tensor(wide[:, 2, :, :], wide[:, 1, :, :], wide[:, 0, :, :], ALU.subtract).then_inc(fs["dwide"], 1)
                dve.wait_ge(fs["ex"], k)
                dve.tensor_scalar(fs1[:, 5, :], fs1[:, 4, :], 1.0, None, ALU.add).then_inc(fs["den"], 1)
                dve.wait_ge(fs["den"], 3 * b + 1)
                dve.reciprocal(fs1[:, 6, :], fs1[:, 5, :]).then_inc(fs["den"], 1)
                dve.wait_ge(fs["den"], 3 * b + 2)
                dve.tensor_tensor(fs1[:, 7, :], fs1[:, 4, :], fs1[:, 6, :], ALU.mult).then_inc(fs["den"], 1)
                dve.tensor_copy(wide[:, 3, :, :], fs1[:, 6, :].unsqueeze(2).broadcast_to([P, T, P])).then_inc(fs["w1"], 1)
                dve.wait_ge(fs["den"], 3 * b + 3)
                dve.tensor_copy(wide[:, 4, :, :], fs1[:, 7, :].unsqueeze(2).broadcast_to([P, T, P])).then_inc(fs["w2"], 1)
                for i in range(5):
                    dve.wait_ge(fs["mT_mm"], 5 * b + i + 1)
                    dve.tensor_copy(maskT[:, i, :], ps[:, 4 + i % 2, :]).then_inc(fs["mT"], 1)
                    if i == 0:
                        dve.wait_ge(fs["mT"], 5 * b + 1)
                        dve.wait_ge(fs["t_mm"], k)
                        for c in range(2):
                            dve.tensor_tensor(tmask[:, c, :], ps[:, 6 + c, :], maskT[:, 0, :], ALU.mult).then_inc(fs["tm"], 1)
                    if i == 2:
                        dve.wait_ge(fs["mT"], 5 * b + 3)
                        for c in range(2):
                            dve.tensor_tensor(tmask[:, 2 + c, :], ps[:, 6 + c, :], maskT[:, 2, :], ALU.mult)\
                               .then_inc(fs["tmd"], 1)
                dve.wait_ge(fs["mT"], 5 * b + 5)
                for f in range(FT):
                    m = min(P, F - f * P)
                    i = b * FT + f
                    bank = 2 * (i % 2)
                    for s in range(2):
                        q = 2 * i + s
                        dve.wait_ge(fs["silu"], q + 1)
                        dve.wait_ge(fs["h_mm"] if s == 0 else fs["d_mm"], 2 * i + 2)
                        dve.tensor_tensor(pr[0:m, s, :], ps[0:m, bank + 1, :], sil[0:m, s, :], ALU.mult).then_inc(fs["p"], 1)
                        dve.wait_ge(fs["p"], q + 1)
                        wait(dve, fs["z_mm"], q - 1)
                        if i > 0:
                            dve.wait_ge(fs["g"], i)
                        dve.tensor_tensor(av[0:m, s, :], pr[0:m, s, :], maskT[0:m, 3 + s, :], ALU.mult).then_inc(fs["a"], 1)
                dve.wait_ge(fs["z_mm"], 2 * FT * (b + 1))
                for s in range(2):
                    dve.tensor_tensor(uT[:, s, :], ps[:, 4 + s, :], maskT[:, s, :], ALU.mult).then_inc(fs["zm"], 1)
                dve.wait_ge(fs["zm"], 2 * b + 2)
                dve.tensor_tensor(uT[:, 1, :], uT[:, 1, :], uT[:, 0, :], ALU.add).then_inc(fs["u"], 1)
                gb = gates[:, B + b, :].unsqueeze(1).broadcast_to([P, 2, D])
                for i in range(2):
                    q = 2 * b + i
                    dve.wait_ge(fs["o_mm"], q + 1)
                    y = (y1, y2)[i]
                    dve.tensor_tensor(y, ps[:, 6 + i, :].rearrange("p (t d) -> p t d", t=2), gb, ALU.mult).then_inc(fs["og"], 1)
                    dve.wait_ge(fs["og"], q + 1)
                    xb = xs[:, 2 * q:2 * q + 2, :]
                    dve.tensor_tensor(xb, xb, y, ALU.add).then_inc(fs["o"], 1)

        @block.gpsimd
        def _(pool):
            k_ones = sem("k_ones")
            pool.memset(ident[:, :], 0.0).then_inc(k_ones, 1)
            pool.memset(ident16[:, :], 0.0).then_inc(k_ones, 1)
            pool.memset(causal[:, :], 0.0).then_inc(k_ones, 1)
            pool.memset(src[:, :, :, :, :, :].rearrange("p a b c d e -> p (a b c d e)").bitcast(F32), 0.0).then_inc(k_ones, 1)
            pool.memset(vh[:, :, :, HD:HD + 1], 1.0).then_inc(k_ones, 1)
            pool.memset(acc[:, :, :], 0.0).then_inc(acc_zero, 1)
            for e in range(E):
                pool.memset(rev[:, e:e + 1], float(E - e)).then_inc(k_ones, 1)
            n_ones = 5 + E
            pool.wait_ge(k_ones, n_ones)
            for m in (ident, ident16):
                pool.affine_select(out=m[:, :], in_=m[:, :], compare_op=ALU.not_equal, fill=1.0, base=0,
                                   pattern=[[-1, P]], channel_multiplier=1).then_inc(k_ones, 1)
            diag = causal[:, S - P:S]
            pool.affine_select(out=diag, in_=diag, compare_op=ALU.is_ge, fill=MASKED, base=0,
                               pattern=[[-1, P]], channel_multiplier=1).then_inc(k_ones, 1)
            pool.memset(src[:, :, G, :, 1, HD:HD + 1], SHIFT_UNIT).then_inc(k_ones, 1)
            pool.wait_ge(k_ones, n_ones + 4)
            pool.wait_ge(acc_zero, 1)
            pool.memset(rsum[:, :], 0.0).then_inc(s_const, 1)

            def values(g, par):
                pool.wait_ge(rope_done, 4 * g + 4)
                wait_apart(pool, pv_done, 4 * g - 4, pool_passed)
                v = ra[:, par, :, ROT:QKV]
                pool.tensor_scalar(vh[:, par, :, 0:HD], v, 1.0, None, ALU.mult).then_inc(vh_ready, 1)
                pool.wait_ge(vh_ready, g + 1)
                pool.tensor_tensor(vl[:, par, :, :], v, vh[:, par, :, 0:HD], ALU.subtract).then_inc(v_ready, 1)

            def causal_zero(n, npar):
                for off, step, need in ((0, 512, 2), (896, 256, 3)):
                    wait_apart(pool, exp_done, 3 * n + need, pool_passed)
                    if step == 512:
                        v = prob[:, npar, 0:1024].rearrange("p (a c) -> p a c", a=2)[:, :, 0:P]
                    else:
                        v = prob[:, npar, 896:1280].rearrange("p (a c) -> p a c", a=3)[:, 0:3:2, :]
                    ins = pool.affine_select(out=v, in_=v, compare_op=ALU.is_ge, fill=0.0, base=0,
                                             pattern=[[0, 2], [1, P]], channel_multiplier=-1)
                ins.then_inc(sel_done, 1)

            def p_low(n, npar):
                pool.wait_ge(ph_ready, n + 1)
                wait(pool, pv_done, n - 1)
                pool.tensor_tensor(pl[:, npar, :], prob[:, npar, :], ph[:, npar, :], ALU.subtract).then_inc(pl_ready, 1)

            values(0, 0)

            def group(g, b, known=None):
                gg = 2 * g + b
                for j in range(G):
                    n, jp = 4 * gg + j, j % 2
                    causal_zero(n, jp)
                    if j == 1 and known != GROUPS - 1:
                        values(gg + 1, 1 - b)
                    p_low(n, jp)

            group(0, 0, 0)
            group(0, 1, 1)
            with pool.Fori(1, KVH - 1) as g:
                group(g, 0)
                group(g, 1)
            group(KVH - 1, 0, GROUPS - 2)
            group(KVH - 1, 1, GROUPS - 1)
            for i in range(B * FT):
                f = i % FT
                m = min(P, F - f * P)
                pool.wait_ge(fs["a"], 2 * i + 2)
                if f == 0 and i > 0:
                    pool.wait_ge(fs["o_mm"], 2)
                pool.tensor_tensor(gsum[0:m, f, :], av[0:m, 0, :], av[0:m, 1, :], ALU.add).then_inc(fs["g"], 1)


def kernel(L0_attn_hidden_states, L0_attn_Wq, L0_attn_Wk, L0_attn_Wv, L0_attn_Wo, L0_ffn_gate_w, L0_ffn_w1,
           L0_ffn_w3, L0_ffn_w2, L0_ffn_a1, L0_ffn_b1, L0_ffn_a3, L0_ffn_b3, L0_ffn_a2, L0_ffn_b2, L0_c, L0_wmod):
    import concourse.bacc as bacc
    from concourse.bass_utils import run_bass_kernel_spmd

    def con(a):
        return np.ascontiguousarray(a)

    def by_width(a):
        a = np.asarray(a)
        return con(a.T.reshape(-1, P, a.shape[0]).transpose(1, 0, 2))

    wq = np.asarray(L0_attn_Wq).reshape(KVH, G * HD, D)
    wk = np.asarray(L0_attn_Wk).reshape(KVH, HD, D)
    wv = np.asarray(L0_attn_Wv).reshape(KVH, HD, D)
    wqkv = np.concatenate([wq, wk, wv], axis=1)
    wqkv = con(wqkv.transpose(0, 2, 1).reshape(KVH, DK, P, QKV).transpose(0, 2, 1, 3))
    wo = con(np.asarray(L0_attn_Wo).T.reshape(H // 2, P, D).transpose(1, 0, 2))
    inv = (np.float32(1.0) / np.float32(10000.0) ** (np.arange(0, HD, 2, dtype=np.float32) / np.float32(HD)))
    ang = np.arange(S, dtype=np.float32)[:, None] * inv.astype(np.float32)[None, :]
    c1, s1 = np.cos(ang).astype(np.float32), np.sin(ang).astype(np.float32)
    cos = np.concatenate([np.tile(np.concatenate([c1, c1], 1), (1, G + 1)), np.ones((S, HD), np.float32)], 1)
    sin = np.tile(np.concatenate([s1, -s1], 1), (1, G + 1))
    by_token = lambda a: con(a.reshape(T, P, -1).transpose(1, 0, 2))
    a1, a3, a2 = (np.asarray(v) for v in (L0_ffn_a1, L0_ffn_a3, L0_ffn_a2))
    b1, b3, b2 = (con(np.asarray(v).transpose(0, 2, 1).reshape(E * R, -1)) for v in (L0_ffn_b1, L0_ffn_b3, L0_ffn_b2))
    arrays = {
        "x": con(L0_attn_hidden_states), "wqkv": wqkv, "wo": wo, "cos": by_token(cos), "sin": by_token(sin),
        "cT": by_width(L0_c), "wmod": con(np.asarray(L0_wmod).reshape(DK, P, 6 * D).transpose(1, 0, 2)),
        "w1T": by_width(L0_ffn_w1), "w3T": by_width(L0_ffn_w3), "w2T": con(np.asarray(L0_ffn_w2).T),
        "gateT": by_width(L0_ffn_gate_w), "a1T": by_width(a1.reshape(E * R, D)), "a3T": by_width(a3.reshape(E * R, D)),
        "b1T": b1, "b3T": b3, "a2T": con(a2.reshape(E * R, F).T), "b2T": b2,
    }
    nc = bacc.Bacc("TRN2", target_bir_lowering=False, num_devices=1)
    args = [nc.dram_tensor(k, a.shape, mybir.dt.from_np(a.dtype), kind="ExternalInput").ap() for k, a in arrays.items()]
    args.append(nc.dram_tensor("out", (B, S, D), F32, kind="ExternalOutput").ap())
    block_kernel(nc, *args)
    r = run_bass_kernel_spmd(nc, [arrays], core_ids=[0])
    return r.results[0]["out"]
```

```python
from contextlib import ExitStack

import numpy as np

import concourse.bass as bass
from concourse import mybir

F32 = mybir.dt.float32
F16 = mybir.dt.float16
F32R = mybir.dt.float32r
ALU = mybir.AluOpType
ACT = mybir.ActivationFunctionType
AX = mybir.AxisListType

P = 128
B, S, D = 2, 512, 256
H, KVH, HD = 32, 8, 64
F, E, R = 704, 8, 16
T = S // P
DK = D // P
G = H // KVH
GROUPS = B * KVH
HEADS = B * H
QKV = (G + 2) * HD
ROT = (G + 1) * HD
FT = -(-F // P)
EPS = 1e-5
SHIFT_UNIT = 64.0
SHIFT_BIAS = 4.0 * HD ** 0.5 / SHIFT_UNIT
MASKED = -1.0e30
KEY_OFF = [0, 512, 896, 1152]
PROBS = 1280
LORA_SCALE = 2.0


def wait(eng, sem, value):
    if isinstance(value, int) and value < 1:
        return
    eng.wait_ge(sem, value)


def wait_apart(eng, sem, value, passed):
    wait(eng, sem, value)
    eng.sem_inc(passed, 1)


def block_kernel(nc, x, wqkv, wo, cos, sin, cT, wmod, w1T, w3T, w2T, gateT, a1T, a3T, b1T, b3T, a2T, b2T, out):
    ctx = ExitStack()
    with ctx:
        def sb(name, shape, dt=F32):
            return ctx.enter_context(nc.sbuf_tensor(name, shape, dt))

        def sem(name):
            return ctx.enter_context(nc.semaphore(name))

        ps = ctx.enter_context(nc.psum_tensor("ps", [P, 8, 512], F32))
        S1_BANK, ST_BANK, T_BANK, PV_BANK, MISC_BANK = 0, 2, 4, 5, 6

        xs = sb("xs", [P, B * T, D])
        hT = sb("hT", [P, B, DK, S])
        hT_h, hT_l = (sb(f"hT_{k}", [P, B, DK, S], F32R) for k in "hl")
        acc = sb("acc", [P, B * T, D])
        w13_sb = sb("w13_sb", [P, 2, DK, F])
        b13_sb = sb("b13_sb", [P, 2, F])
        a13_sb = sb("a13_sb", [P, 2, DK, P])
        gate_sb = sb("gate_sb", [P, DK, E])
        a2_sb = sb("a2_sb", [P, FT, P])
        b2_sb = sb("b2_sb", [P, D])
        ident = sb("ident", [P, P])
        gates = sb("gates", [P, 2 * B, D])
        modT = sb("modT", [P, 12, B])
        c_sb = sb("c_sb", [P, DK, B])
        c_e = sb("c_e", [P, DK, B])
        c_s = sb("c_s", [P, DK, B])
        stats = sb("stats", [P, B * T, 6])
        mv = sb("mv", [P, B * T, 2])
        ve = sb("ve", [P, B * T])
        sd = sb("sd", [P, B * T])
        rstd = sb("rstd", [P, B * T])
        nrt = sb("nrt", [P, B * T])
        g_sign = sb("g_sign", [P, 4, B])
        g_abs = sb("g_abs", [P, 4, B])
        fsm = sb("fsm", [P, 8, T, E])
        fs1 = sb("fs1", [P, 12, T])
        rev = sb("rev", [P, E])

        attention_buffers = ExitStack()

        def at_sb(name, shape, dt=F32):
            return attention_buffers.enter_context(nc.sbuf_tensor(name, shape, dt))

        wq_sb = at_sb("wq_sb", [P, DK, QKV])
        wq_h, wq_l = (at_sb(f"wq_{k}", [P, 2, DK, QKV], F32R) for k in "hl")
        cos_sb = at_sb("cos_sb", [P, T, HD])
        sin_sb = at_sb("sin_sb", [P, T, HD])
        ra = at_sb("ra", [P, 2, T, QKV])
        rb = at_sb("rb", [P, 2, T, ROT])
        rot = at_sb("rot", [P, T, G + 1, HD])
        src = at_sb("src", [P, 2, G + 1, T, 2, P], F16)
        wo_sb = at_sb("wo_sb", [P, 2, D])
        wo_h, wo_l = (at_sb(f"wo_{k}", [P, 2, 2, D], F32R) for k in "hl")
        qT = at_sb("qT", [P, 2, 2, S], F16)
        kT = at_sb("kT", [P, 2, 2, S], F16)
        vh = at_sb("vh", [P, 2, T, HD + 1], F16)
        vl = at_sb("vl", [P, 2, T, HD], F16)
        prob = at_sb("prob", [P, 2, PROBS])
        ph = at_sb("ph", [P, 2, PROBS], F16)
        pl = at_sb("pl", [P, 2, PROBS], F16)
        mx = at_sb("mx", [P, 2, T])
        rsum = at_sb("rsum", [P, T])
        on = at_sb("on", [P, 2, T, 2 * HD])
        oT_h, oT_l = (at_sb(f"oT_{k}", [P, 2, 2, S], F32R) for k in "hl")
        junk = at_sb("junk", [P, PROBS], F16)
        ident16 = at_sb("ident16", [P, P], F16)
        causal = at_sb("causal", [P, S])
        attention_buffers.close()

        w13_h, w13_l = (sb(f"w13_{k}", [P, 2, DK, F], F32R) for k in "hl")
        b13_h, b13_l = (sb(f"b13_{k}", [P, 2, F], F32R) for k in "hl")
        a13_h, a13_l = (sb(f"a13_{k}", [P, 2, DK, P], F32R) for k in "hl")
        w2_sb = sb("w2_sb", [P, FT, D])
        xn_f = sb("xn_f", [P, B, T, D])
        wide = sb("wide", [P, 5, T, P])
        sil = sb("sil", [P, 2, S])
        tm_h, tm_l = (sb(f"tm_{k}", [P, B, 4, S], F32R) for k in "hl")
        gsum = sb("gsum", [P, FT, S])
        av = sb("av", [P, 2, S])
        uT = sb("uT", [P, 2, S])
        maskT1 = sb("maskT1", [P, 5, S])

        def over(t, shape):
            flat = t[tuple([slice(None)] * len(t.shape))]
            names = " ".join("abcdefg"[:len(t.shape) - 1])
            flat = flat.rearrange(f"p {names} -> p ({names})") if len(t.shape) > 2 else flat
            if t.dtype != F32:
                flat = flat.bitcast(F32)
            n = int(np.prod(shape[1:]))
            flat = flat[:, 0:n]
            if len(shape) == 3:
                flat = flat.rearrange("p (a b) -> p a b", a=shape[1])
            if len(shape) == 4:
                flat = flat.rearrange("p (a b c) -> p a b c", a=shape[1], b=shape[2])
            return flat

        wmod_1 = over(prob, [P, 2, DK, 512])[:, 0]
        wmod_2 = (over(prob, [P, 2, DK, 512])[:, 1], over(ph, [P, DK, 512]))
        xn = over(ra, [P, T, D])
        xn2 = over(on, [P, T, D])
        gwide, gwide2 = (over(w13_sb, [P, 2, 4, P])[:, i] for i in range(2))

        ld_x, ld_x1, ld_c, ld_mod, ld_rope, ld_wo, ld_ffn = (sem(f"ld_{k}") for k in ("x", "x1", "c", "mod", "rope", "wo", "ffn"))
        ld_w0, ld_w, ld_mod2 = sem("ld_w0"), sem("ld_w"), sem("ld_mod2")
        s_const = sem("s_const")
        c_exp, c_one, c_rec, c_silu = (sem(f"c_{k}") for k in ("exp", "one", "rec", "silu"))
        mod_mm, mod_sb = sem("mod_mm"), sem("mod_sb")
        mod_add = sem("mod_add")
        ln_stat, ln_aggr, ln_eps, ln_sqrt, ln_rec = (sem(f"ln_{k}") for k in ("stat", "aggr", "eps", "sqrt", "rec"))
        ln_n1, ln_n2, ln_rstd, xn_ready, xnT_mm, hT_ready = (
            sem(k) for k in ("ln_n1", "ln_n2", "ln_rstd", "xn_ready", "xnT_mm", "hT_ready"))
        g_s, g_a, g_m, g_wide, g_mm, g_ready = (sem(f"g_{k}") for k in ("s", "a", "m", "wide", "mm", "ready"))
        proj_done, rope_done, rotk_ready, rotq_ready = (
            sem(k) for k in ("proj_done", "rope_done", "rotk_ready", "rotq_ready"))
        kh_ready, kl_ready, qh_ready, ql_ready = (sem(k) for k in ("kh_ready", "kl_ready", "qh_ready", "ql_ready"))
        vh_ready, v_ready = sem("vh_ready"), sem("v_ready")
        tk_done, tk_evac, ta_done, ta_evac, tb_done, tb_evac = (
            sem(k) for k in ("tk_done", "tk_evac", "ta_done", "ta_evac", "tb_done", "tb_evac"))
        s1_done, maxed, m_ready = sem("s1_done"), sem("maxed"), sem("m_ready")
        st_done, exp_done, sel_done, ph_ready, pl_ready = (
            sem(k) for k in ("st_done", "exp_done", "sel_done", "ph_ready", "pl_ready"))
        pv_done, rsum_ready, normed = sem("pv_done"), sem("rsum_ready"), sem("normed")
        ot_done, ot_evac, ot_low_done, op_done, op_added = (
            sem(k) for k in ("ot_done", "ot_evac", "ot_low_done", "op_done", "op_added"))
        wqh_ready, wql_ready, woh_ready, wol_ready = (
            sem(k) for k in ("wqh_ready", "wql_ready", "woh_ready", "wol_ready"))
        hh_ready, hl_ready, ld_w2 = sem("hh_ready"), sem("hl_ready"), sem("ld_w2")
        acc_zero = sem("acc_zero")
        dve_passed, pool_passed = sem("dve_passed"), sem("pool_passed")
        r_mul, r_add = sem("r_mul"), sem("r_add")
        fs = {k: sem("f_" + k) for k in (
            "h2", "gate_mm", "lg", "v1", "eq", "rv", "fi", "oh1", "mk2", "v2", "eq2", "rv2", "fi2", "oh2",
            "dv", "ex", "den", "w1", "w2", "wide", "dwide", "mT_mm", "mT", "t_mm", "tm", "tmh", "tml", "tmd_l",
            "wh", "wl_v", "wl_p", "h2h", "h2l",
            "h_mm", "silu", "p", "a", "g", "d_mm", "z_mm", "zm", "u", "o_mm", "og", "o")}
        stored = sem("stored")

        block = ctx.enter_context(nc.Block())

        maskT = (over(w13_sb, [P, 5, S]), maskT1)
        pr = over(b13_sb, [P, 2, S])
        tm = (over(gsum, [P, 4, S]), over(acc, [P, 4, S]))
        y1, y2 = (tm[1][:, i, :].rearrange("p (a d) -> p a d", a=2) for i in range(2))

        def form(par, item, t, ab):
            return src[:, par, item, t, ab, :]

        @block.sync
        def _(sp):
            xv = x.rearrange("b (t p) d -> p (b t) d", p=P)
            sp.dma_start(xs[:, 0:T, :], xv[:, 0:T, :]).then_inc(ld_x, 16)
            sp.dma_start(wmod_1, wmod[:, :, 0:512]).then_inc(ld_mod, 16)
            for i in range(2):
                sp.dma_start(wmod_2[i], wmod[:, :, 512 * (i + 1):512 * (i + 2)]).then_inc(ld_mod2, 16)
            sp.dma_start(sin_sb[:, :, :], sin).then_inc(ld_rope, 16)
            sp.dma_start(cos_sb[:, :, :], cos).then_inc(ld_rope, 16)
            sp.dma_start(wo_sb[:, :, :], wo[:, 0:2, :]).then_inc(ld_wo, 16)
            sp.wait_ge(proj_done, 7)
            for g in range(1, KVH):
                sp.wait_ge(wqh_ready, g)
                sp.wait_ge(wql_ready, g)
                sp.dma_start(wq_sb[:, :, :], wqkv[g]).then_inc(ld_w, 16)
                if g == 2:
                    sp.wait_ge(g_mm, 2)
                    sp.dma_start(w13_sb[:, 0, :, :], w1T).then_inc(ld_ffn, 16)
                    sp.dma_start(w13_sb[:, 1, :, :], w3T).then_inc(ld_ffn, 16)
                    full = F // P
                    sp.dma_start(a2_sb[:, 0:full, :], a2T[0:full * P, :].rearrange("(f p) d -> p f d", p=P))\
                        .then_inc(ld_ffn, 16)
                    sp.dma_start(a2_sb[0:F - full * P, full, :], a2T[full * P:F, :]).then_inc(ld_ffn, 16)
                    for dst, s in ((gate_sb[:, :, :], gateT), (a13_sb[:, 0, :, :], a1T), (a13_sb[:, 1, :, :], a3T),
                                   (b13_sb[:, 0, :], b1T), (b13_sb[:, 1, :], b3T), (b2_sb[:, :], b2T)):
                        sp.dma_start(dst, s).then_inc(ld_ffn, 16)
                sp.wait_ge(woh_ready, g)
                sp.wait_ge(wol_ready, g)
                sp.dma_start(wo_sb[:, :, :], wo[:, 2 * g:2 * g + 2, :]).then_inc(ld_wo, 16)
            sp.wait_ge(fs["wh"], 1)
            sp.dma_start(w2_sb[:, 0:full, :], w2T[0:full * P, :].rearrange("(f p) d -> p f d", p=P)).then_inc(ld_w2, 16)
            sp.dma_start(w2_sb[0:F - full * P, full, :], w2T[full * P:F, :]).then_inc(ld_w2, 16)
            ov = out.rearrange("b (t p) d -> p (b t) d", p=P)
            for i in range(B * T // 2):
                sp.wait_ge(fs["o"], i + 1)
                sp.dma_start(ov[:, 2 * i:2 * i + 2, :], xs[:, 2 * i:2 * i + 2, :]).then_inc(stored, 16)
            sp.wait_ge(stored, 16 * (B * T // 2))

        @block.tensor
        def _(pe):
            pe.wait_ge(c_silu, 1)
            pe.wait_ge(ld_mod, 16)

            def modulation(chunks):
                for ch in chunks:
                    for k in range(DK):
                        w = wmod_1 if ch < 4 else wmod_2[ch // 4 - 1]
                        mm = pe.matmul(ps[:, PV_BANK, 2 * ch:2 * ch + 2], w[:, k, ch % 4 * P:(ch % 4 + 1) * P], c_s[:, k, :],
                                       start=(k == 0), stop=(k == DK - 1))
                mm.then_inc(mod_mm, 1)

            modulation(range(4))
            pe.wait_ge(s_const, 1)

            def transpose_rows(b, bank0, buf, done, count):
                for k in range(DK):
                    for t in range(T):
                        if k == 0:
                            pe.wait_ge(xn_ready, count + t + 1)
                        mm = pe.transpose(ps[:, bank0 + k, t * P:(t + 1) * P], buf[:, t, k * P:(k + 1) * P], ident[:, :])
                    mm.then_inc(done, 1)

            transpose_rows(0, 0, xn, xnT_mm, 0)

            def project_first(b, t, bank):
                for k in range(DK):
                    mm = pe.matmul(ps[:, bank, 0:QKV], hT[:, b, k, t * P:(t + 1) * P], wq_sb[:, k, :],
                                   start=(k == 0), stop=(k == DK - 1))
                mm.then_inc(proj_done, 1)

            def mm3(o, lh, ll, rh, rl, first, last):
                pe.matmul(o, lh, rh, start=first, stop=False)
                pe.matmul(o, lh, rl, start=False, stop=False)
                return pe.matmul(o, ll, rh, start=False, stop=last)

            def project(g, w, b, t, bank, halves=(0, 1)):
                for k in halves:
                    mm = mm3(ps[:, bank, 0:QKV], hT_h[:, b, k, t * P:(t + 1) * P], hT_l[:, b, k, t * P:(t + 1) * P],
                             wq_h[:, w, k, :], wq_l[:, w, k, :], k == 0, k == DK - 1)
                    if k == DK - 1:
                        mm.then_inc(proj_done, 1)

            def tk(g, par):
                pe.wait_ge(kh_ready, g + 1)
                pe.wait_ge(kl_ready, g + 1)
                for ab in range(2):
                    for t in range(T):
                        mm = pe.transpose(ps[:, T_BANK, ab * 256 + t * 64:ab * 256 + (t + 1) * 64].bitcast(F16),
                                          form(par, G, t, ab), ident16[:, :])
                mm.then_inc(tk_done, 1)

            def tq(par, item, ab, done):
                for t in range(T):
                    mm = pe.transpose(ps[:, T_BANK, t * 64:(t + 1) * 64].bitcast(F16), form(par, item, t, ab), ident16[:, :])
                mm.then_inc(done, 1)

            def ta(m, par, item):
                pe.wait_ge(qh_ready, m + 1)
                tq(par, item, 0, ta_done)

            def tb(m, par, item):
                pe.wait_ge(ql_ready, m + 1)
                pe.wait_ge(m_ready, m + 1)
                tq(par, item, 1, tb_done)

            def s1(m, mpar, kpar, f):
                bank = S1_BANK + (mpar + f) % 2
                wait(pe, maxed, 3 * m + f - 1)
                off = 0
                for qt in ([3], [2], [0, 1])[f]:
                    n = (qt + 1) * P
                    mm = pe.matmul(ps[:, bank, off:off + n], qT[:, mpar, 0, qt * P:(qt + 1) * P], kT[:, kpar, 0, 0:n],
                                   start=True, stop=True)
                    off += n
                mm.then_inc(s1_done, 1)

            def st(n, npar, kpar, f):
                bank = ST_BANK + (npar + f) % 2
                wait(pe, exp_done, 3 * n + f - 1)
                off = 0
                for kt in ([0], [1], [2, 3])[f]:
                    w = S - kt * P
                    for ab in range(2):
                        mm = pe.matmul(ps[:, bank, off:off + w], kT[:, kpar, ab, kt * P:(kt + 1) * P],
                                       qT[:, npar, ab, kt * P:S], start=(ab == 0), stop=(ab == 1))
                    off += w
                mm.then_inc(st_done, 1)

            def pv(n, npar, g, vpar):
                pe.wait_ge(ph_ready, n + 1)
                pe.wait_ge(pl_ready, n + 1)
                pe.wait_ge(v_ready, g + 1)
                wait(pe, normed, n)
                for qt in range(T):
                    at = qt * (HD + 1)
                    for kt in range(qt + 1):
                        c = KEY_OFF[kt] + (qt - kt) * P
                        first, last = kt == 0, kt == qt
                        pe.matmul(ps[:, PV_BANK, at:at + HD + 1], ph[:, npar, c:c + P], vh[:, vpar, kt, :],
                                  start=first, stop=False)
                        pe.matmul(ps[:, PV_BANK, at:at + HD], ph[:, npar, c:c + P], vl[:, vpar, kt, :],
                                  start=False, stop=False)
                        mm = pe.matmul(ps[:, PV_BANK, at:at + HD + 1], pl[:, npar, c:c + P], vh[:, vpar, kt, :],
                                       start=False, stop=last)
                mm.then_inc(pv_done, 1)

            def ot(pair, p, bank):
                pe.wait_ge(normed, 2 * pair + 2)
                for t in range(T):
                    mm = pe.transpose(ps[:, bank, t * P:(t + 1) * P], on[:, p, t, :], ident[:, :])
                mm.then_inc(ot_done, 1)

            def op(gg, g, w, par, t, bank):
                pe.wait_ge(ot_low_done, 2 * gg + 2)
                pe.wait_ge(wol_ready, g + 1)
                for p in range(2):
                    c = slice(t * P, (t + 1) * P)
                    mm = mm3(ps[:, bank, 0:D], oT_h[:, par, p, c], oT_l[:, par, p, c], wo_h[:, w, p, :], wo_l[:, w, p, :],
                             p == 0, p == 1)
                mm.then_inc(op_done, 1)

            M0, M1 = MISC_BANK, MISC_BANK + 1
            pe.wait_ge(ld_w0, 16)
            for t in range(T):
                if t == 0:
                    pe.wait_ge(hT_ready, 2)
                if t >= 2:
                    pe.wait_ge(rope_done, t - 1)
                project_first(0, t, MISC_BANK + t % 2)
                if t == 1:
                    transpose_rows(1, 2, xn2, xnT_mm, T)
            pe.wait_ge(hT_ready, 2 * B)
            for t in range(2):
                pe.wait_ge(rope_done, t + 3)
                project_first(1, t, MISC_BANK + t % 2)
            tk(0, 0)
            pe.wait_ge(ld_mod2, 32)
            pe.wait_ge(mod_sb, 1)
            modulation(range(4, 8))
            pe.wait_ge(tk_evac, 1)
            ta(0, 0, 0)
            pe.wait_ge(rope_done, 5)
            project_first(1, 2, M0)
            pe.wait_ge(ta_evac, 1)
            for f in range(3):
                s1(0, 0, 0, f)
            ta(1, 0, 1)
            pe.wait_ge(ta_evac, 2)
            tb(0, 0, 0)

            def gates_transposed(i, bank):
                pe.wait_ge(g_wide, i + 1)
                for c in range(2 * B):
                    mm = pe.transpose(ps[:, bank, c * P:(c + 1) * P], (gwide, gwide2)[i][:, c, :], ident[:, :])
                mm.then_inc(g_mm, 1)

            def group(g, b, odd, known=None):
                before_w, w_now, w_next = 1 - odd, odd, 1 - odd
                gg, par = 2 * g + b, b
                before = known if known is not None else 2
                after = GROUPS - 1 - known if known is not None else 3
                for j in range(G):
                    n, jp = 4 * gg + j, j % 2
                    more1, more2 = after > 0 or j < 3, after > 0 or j < 2
                    par1, item1 = (par, j + 1) if j < 3 else (1 - par, 0)
                    par2, item2 = (par, j + 2) if j < 2 else (1 - par, j - 2)
                    pe.wait_ge(tb_evac, n + 1)
                    if more1:
                        pe.wait_ge(ta_evac, n + 2)
                        if j == 3:
                            pe.wait_ge(tk_evac, gg + 2)
                    for f in range(3):
                        if f == 2 and j == 2 and after:
                            tk(gg + 1, 1 - par)
                        if more1:
                            s1(n + 1, 1 - jp, par1, f)
                        st(n, jp, par, f)
                    if j != 2 and more2:
                        ta(n + 2, par2, item2)
                    if known == 0 and j == 0:
                        modulation(range(8, 12))
                    if known == 0 and j == 1:
                        pe.wait_ge(mod_sb, 2)
                    if known == 0 and j == 3:
                        pe.wait_ge(rope_done, 4 * gg + 9)
                        gates_transposed(0, M0)
                    if known == 1 and j == 1:
                        pe.wait_ge(rope_done, 4 * gg + 7)
                        gates_transposed(1, M1)
                    if j == 0 and before > 1:
                        if after > 0:
                            pe.wait_ge(rope_done, 4 * gg + 7)
                        op(gg - 2, g - 1, before_w, par, 1, M1)
                    if j == 1 and before > 1:
                        pe.wait_ge(op_added, 4 * gg - 6)
                        op(gg - 2, g - 1, before_w, par, 2, M1)
                    if j == 2 and before > 1:
                        if after > 0:
                            pe.wait_ge(rope_done, 4 * gg + (9 if after > 1 else 8))
                        else:
                            pe.wait_ge(ot_low_done, 2 * gg - 1)
                        op(gg - 2, g - 1, before_w, par, 3, M0)
                    g1, w1 = (g, w_now) if b == 1 else (g - 1, before_w)
                    if j == 3 and before > 0:
                        if before > 1:
                            pe.wait_ge(op_added, 4 * gg - 4)
                        else:
                            pe.wait_ge(rope_done, 4 * gg + 9)
                        op(gg - 1, g1, w1, 1 - par, 0 if after else 1, M0)
                    if j > 1 and after == 0:
                        if j == 3:
                            pe.wait_ge(op_added, 4 * gg - 3)
                        op(gg - 1, g1, w1, 1 - par, 2 * j - 4, M1)
                    if j == 2 and after:
                        pe.wait_ge(tk_evac, gg + 2)
                        ta(n + 2, par2, item2)

                    def projection(halves):
                        if j == 0 and after > 0:
                            if 0 in halves:
                                if before > 0:
                                    pe.wait_ge(ot_low_done, 2 * gg - 1)
                                else:
                                    pe.wait_ge(rope_done, 4 * gg + 7)
                                    pe.wait_ge(hl_ready, B)
                                    pe.wait_ge(wql_ready, 1)
                            project(gg + 1, w_next if b == 1 else w_now, 1 - b, 3, M0, halves)
                        if j > 0 and after > 1:
                            if 0 in halves:
                                if j == 1:
                                    pe.wait_ge(rope_done, 4 * gg + 8)
                                    pe.wait_ge(wql_ready, g + 2)
                                elif j == 2:
                                    if before > 0:
                                        pe.wait_ge(ot_low_done, 2 * gg)
                                else:
                                    pe.wait_ge(rope_done, 4 * gg + 10)
                            project(gg + 2, w_next, b, j - 1, M0 if j == 1 else M1, halves)

                    first_half = (0,) if j != 2 else (0, 1)
                    projection(first_half)
                    if more1:
                        if more2:
                            pe.wait_ge(ta_evac, n + 3)
                        tb(n + 1, par1, item1)
                    if j != 2:
                        projection((1,))
                    if j == 1 and before > 0:
                        if before > 1:
                            pe.wait_ge(op_added, 4 * gg - 5)
                        else:
                            pe.wait_ge(g_ready, 2)
                        ot(2 * gg - 1, 1, M1)
                    if j == 3:
                        if before > 0:
                            pe.wait_ge(op_added, 4 * gg - 3 if after else 4 * gg - 2)
                        else:
                            pe.wait_ge(g_ready, 1)
                        ot(2 * gg, 0, M0)
                    if before > 0 or j > 0:
                        gp, vpar = (gg, par) if j > 0 else (gg - 1, 1 - par)
                        pv(n - 1, 1 - jp, gp, vpar)

            group(0, 0, 0, 0)
            group(0, 1, 0, 1)
            with pe.Fori(1, KVH - 1, 2) as g:
                for odd in (1, 0):
                    group(g + (1 - odd), 0, odd)
                    group(g + (1 - odd), 1, odd)
            group(KVH - 1, 0, 1, GROUPS - 2)
            group(KVH - 1, 1, 1, GROUPS - 1)
            L = GROUPS - 1
            pe.wait_ge(op_added, 4 * L - 1)
            op(L - 1, KVH - 1, 1, 0, 3, M1)
            pv(HEADS - 1, 1, L, 1)
            pe.wait_ge(ot_low_done, 2 * L + 1)
            ot(2 * L + 1, 1, M0)
            pe.wait_ge(maxed, 3 * HEADS)
            transpose_rows(0, 0, xn_f[:, 0], xnT_mm, B * T)

            def last_op(t):
                pe.wait_ge(op_added, 4 * L + max(t - 1, 0))
                op(L, KVH - 1, 1, 1, t, MISC_BANK + (t + 1) % 2)

            last_op(0)
            last_op(1)

            def gate_logits(b):
                pe.wait_ge(fs["h2"], 2 * (b + 1))
                if b == 0:
                    pe.wait_ge(tb_evac, HEADS)
                else:
                    pe.wait_ge(fs["h2h"], 2 * B)
                for t in range(T):
                    for k in range(DK):
                        mm = pe.matmul(ps[:, 4 + 2 * b, t * E:(t + 1) * E], hT[:, b, k, t * P:(t + 1) * P], gate_sb[:, k, :],
                                       start=(k == 0), stop=(k == DK - 1))
                mm.then_inc(fs["gate_mm"], 1)

            def mask_transposes(b, which):
                for i in which:
                    if i < 2:
                        pe.wait_ge(fs["wide"], 2 * b + i + 1)
                    else:
                        pe.wait_ge(fs[("dwide", "w1", "w2")[i - 2]], b + 1)
                    if i == 0 and b == 0:
                        pe.wait_ge(normed, HEADS)
                    elif i == 1:
                        pe.wait_ge(fs["lg"], b + 1)
                    elif i == 2:
                        pe.wait_ge(fs["mT"], 5 * b + 1)
                    elif i > 2:
                        pe.wait_ge(fs["tm"], 4 * b + i)
                    bank = 4 + 2 * b + ((i + 1) % 2 if i < 3 else i - 3)
                    for t in range(T):
                        mm = pe.transpose(ps[:, bank, t * P:(t + 1) * P], wide[:, i, t, :], ident[:, :])
                    mm.then_inc(fs["mT_mm"], 1)

            def lora_inputs(b):
                pe.wait_ge(fs["h2l"], 2 * (b + 1))
                pe.wait_ge(fs["wl_p"], 3)
                for c in range(2):
                    pe.wait_ge(fs["mT"], 5 * b + 2 + c)
                    for k in range(DK):
                        mm = mm3(ps[:, 4 + 2 * b + c, :], a13_h[:, c, k, :], a13_l[:, c, k, :], hT_h[:, b, k, :], hT_l[:, b, k, :],
                                 k == 0, k == DK - 1)
                    mm.then_inc(fs["t_mm"], 1)

            def h_base(b, f):
                m, i = min(P, F - f * P), b * FT + f
                bank = 2 * (i % 2)
                if i == 0:
                    pe.wait_ge(fs["wl_v"], 1)
                    pe.wait_ge(fs["wl_p"], 1)
                    pe.wait_ge(fs["h2h"], 2)
                elif i == 1:
                    pe.wait_ge(exp_done, 3 * HEADS)
                else:
                    pe.wait_ge(fs["p"], 2 * i - 2)
                if f < 2:
                    pe.wait_ge(fs["h2l"], 2 * (b + 1))
                fc = slice(f * P, f * P + m)
                for c in range(2):
                    for k in range(DK):
                        mm3(ps[0:m, bank + c, :], w13_h[:, c, k, fc], w13_l[:, c, k, fc], hT_h[:, b, k, :], hT_l[:, b, k, :],
                            k == 0, False)

            def h_lora(b, f):
                m, i = min(P, F - f * P), b * FT + f
                bank = 2 * (i % 2)
                if f == 0:
                    pe.wait_ge(fs["tmh"], 4 * b + 2)
                    pe.wait_ge(fs["tml"], 2 * b + 2)
                fc = slice(f * P, f * P + m)
                for c in range(2):
                    mm = mm3(ps[0:m, bank + c, :], b13_h[:, c, fc], b13_l[:, c, fc], tm_h[:, b, c, :], tm_l[:, b, c, :],
                             False, True)
                    mm.then_inc(fs["h_mm"], 1)

            def h_second(b, f):
                m, i = min(P, F - f * P), b * FT + f
                bank = 2 * (i % 2)
                pe.wait_ge(fs["p"], 2 * i + 1)
                if f == 0:
                    pe.wait_ge(fs["tmh"], 4 * b + 4)
                    pe.wait_ge(fs["tmd_l"], 2 * b + 2)
                fc = slice(f * P, f * P + m)
                for c in range(2):
                    o = ps[0:m, bank + c, :]
                    for l, r in ((b13_h, tm_h), (b13_h, tm_l), (b13_l, tm_h)):
                        mm = pe.matmul(o, l[:, c, fc], r[:, b, 2 + c, :], start=False, stop=(l is b13_l),
                                       skip_group_check=True)
                    mm.then_inc(fs["d_mm"], 1)

            def z_product(b, f, s):
                m = min(P, F - f * P)
                pe.wait_ge(fs["a"], 2 * (b * FT + f) + s + 1)
                if f == 0 and s == 0:
                    pe.wait_ge(fs["mT"] if b == 0 else fs["zm"], 5 if b == 0 else 2)
                mm = pe.matmul(ps[:, 4 + s, :], a2_sb[0:m, f, :], av[0:m, s, :], start=(f == 0), stop=(f == FT - 1))
                mm.then_inc(fs["z_mm"], 1)

            gate_logits(0)
            h_base(0, 0)
            h_base(0, 1)
            mask_transposes(0, (0, 1, 2))
            last_op(2)
            last_op(3)
            lora_inputs(0)
            mask_transposes(0, (3, 4))
            h_lora(0, 0)
            for b in range(B):
                for f in range(FT):
                    if f < FT - 1:
                        if b > 0 or f > 0:
                            h_base(b, f + 1)
                        h_lora(b, f + 1)
                        if b == 0 and f == 1:
                            pe.wait_ge(op_added, 4 * GROUPS)
                            transpose_rows(1, 6, xn_f[:, 1], xnT_mm, (B + 1) * T)
                    elif b == 0:
                        h_base(1, 0)
                        h_lora(1, 0)
                    h_second(b, f)
                    if f > 0:
                        z_product(b, f - 1, 1)
                    z_product(b, f, 0)
                    if b == 0:
                        if f == 1:
                            gate_logits(1)
                        if f == 2:
                            mask_transposes(1, (0, 1, 2))
                        if f == 3:
                            lora_inputs(1)
                        if f == 4:
                            mask_transposes(1, (3, 4))
                z_product(b, FT - 1, 1)
                pe.wait_ge(ld_w2, 32)
                pe.wait_ge(fs["g"], FT * (b + 1))
                if b == 0:
                    pe.wait_ge(fs["mT"], 5 * B)
                else:
                    pe.wait_ge(fs["og"], 2)
                for i in range(2):
                    for t in range(2 * i, 2 * i + 2):
                        at = (t % 2) * D
                        for f in range(FT):
                            m = min(P, F - f * P)
                            pe.matmul(ps[:, 6 + i, at:at + D], gsum[0:m, f, t * P:(t + 1) * P], w2_sb[0:m, f, :],
                                      start=(f == 0), stop=False)
                        if t == 0:
                            pe.wait_ge(fs["u"], b + 1)
                        mm = pe.matmul(ps[:, 6 + i, at:at + D], uT[:, 1, t * P:(t + 1) * P], b2_sb[:, :],
                                       start=False, stop=True)
                    mm.then_inc(fs["o_mm"], 1)

        @block.scalar
        def _(act):
            act.dma_start(c_sb[:, :, :], cT).then_inc(ld_c, 16)
            xv = x.rearrange("b (t p) d -> p (b t) d", p=P)
            act.dma_start(xs[:, T:2 * T, :], xv[:, T:2 * T, :]).then_inc(ld_x1, 16)
            act.dma_start(wq_sb[:, :, :], wqkv[0]).then_inc(ld_w0, 16)
            act.wait_ge(ld_c, 16)
            act.activation(c_e[:, :, :], c_sb[:, :, :], ACT.Exp, scale=-1.0).then_inc(c_exp, 1)

            def root(b, k):
                act.wait_ge(ln_eps, k)
                act.activation(sd[:, b * T:(b + 1) * T], ve[:, b * T:(b + 1) * T], ACT.Sqrt).then_inc(ln_sqrt, 1)

            def modulate(b, bank0):
                for k in range(DK):
                    act.wait_ge(xnT_mm, 2 * b + k + 1)
                    act.activation(hT[:, b, k, :], ps[:, bank0 + k, :], ACT.Identity, bias=modT[:, k, b:b + 1],
                                   scale=modT[:, 2 + k, b:b + 1]).then_inc(hT_ready, 1)

            for b in range(B):
                root(b, b + 1)
                act.wait_ge(mod_add, 1)
                modulate(b, 2 * b)
            for b in range(B):
                act.wait_ge(hT_ready, 2 * b + 2)
                act.activation(hT_h[:, b, :, :], hT[:, b, :, :], ACT.Copy).then_inc(hh_ready, 1)

            def wq_high(g, w):
                if isinstance(g, int) and g == 0:
                    act.wait_ge(ld_w0, 16)
                else:
                    act.wait_ge(ld_w, 16 * g)
                    wait(act, proj_done, 8 * g - 8)
                act.activation(wq_h[:, w, :, :], wq_sb[:, :, :], ACT.Copy).then_inc(wqh_ready, 1)

            def wo_high(g, w):
                act.wait_ge(ld_wo, 16 * g + 16)
                wait(act, op_done, 8 * g - 7)
                act.activation(wo_h[:, w, :, :], wo_sb[:, :, :], ACT.Copy).then_inc(woh_ready, 1)

            wq_high(0, 0)
            act.wait_ge(c_silu, 1)
            act.activation(c_e[:, :, :], c_sb[:, :, :], ACT.Exp).then_inc(c_exp, 1)

            def k_high(g, par):
                act.wait_ge(rotk_ready, g + 1)
                act.activation(src[:, par, G, :, :, 0:HD],
                               rot[:, :, G, :].unsqueeze(2).broadcast_to([P, T, 2, HD]), ACT.Copy).then_inc(kh_ready, 1)

            def q_high(m, par, item, g):
                act.wait_ge(rotq_ready, 2 * g + 1 + item // 2)
                act.activation(src[:, par, item, :, 0, :].rearrange("p t (c d) -> p t c d", c=2),
                               rot[:, :, item, :].unsqueeze(2).broadcast_to([P, T, 2, HD]), ACT.Copy).then_inc(qh_ready, 1)

            def v_high(g, par):
                act.wait_ge(rope_done, 4 * g + 4)
                wait(act, pv_done, 4 * g - 4)
                act.activation(vh[:, par, :, 0:HD], ra[:, par, :, ROT:QKV], ACT.Copy).then_inc(vh_ready, 1)

            def tk_out(g, par):
                act.wait_ge(tk_done, g + 1)
                act.activation(kT[:, par, :, :].rearrange("p a s -> p (a s)"), ps[:, T_BANK, :].bitcast(F16), ACT.Copy)\
                   .then_inc(tk_evac, 1)

            def ta_out(m, mpar):
                act.wait_ge(ta_done, m + 1)
                act.activation(qT[:, mpar, 0, :], ps[:, T_BANK, 0:256].bitcast(F16), ACT.Copy).then_inc(ta_evac, 1)

            def exps(n, npar, fills):
                if 0 in fills:
                    wait(act, pl_ready, n - 1)
                for f in fills:
                    act.wait_ge(st_done, 3 * n + f + 1)
                    w, off = (512, 384, 384)[f], (0, 512, 896)[f]
                    act.activation(prob[:, npar, off:off + w], ps[:, ST_BANK + (npar + f) % 2, 0:w], ACT.Exp,
                                   scale=HD ** -0.5).then_inc(exp_done, 1)

            def p_high(n, npar):
                act.wait_ge(sel_done, n + 1)
                wait(act, pv_done, n - 1)
                act.activation(ph[:, npar, :], prob[:, npar, :], ACT.Copy).then_inc(ph_ready, 1)

            def w13_high(c, k):
                if c == 0 and k == 0:
                    act.wait_ge(ld_ffn, 16 * 10)
                    act.wait_ge(proj_done, 4 * GROUPS)
                    act.wait_ge(rotk_ready, GROUPS)
                    act.wait_ge(rotq_ready, 2 * GROUPS)
                    act.wait_ge(v_ready, GROUPS)
                    act.wait_ge(kl_ready, GROUPS)
                    act.wait_ge(ql_ready, HEADS)
                    act.wait_ge(qh_ready, HEADS)
                    act.wait_ge(vh_ready, GROUPS)
                act.activation(w13_h[:, c, k, :], w13_sb[:, c, k, :], ACT.Copy).then_inc(fs["wh"], 1)

            def ot_out(pair, par, p, bank):
                act.wait_ge(ot_done, pair + 1)
                act.activation(oT_h[:, par, p, :], ps[:, bank, :], ACT.Copy).then_inc(ot_evac, 1)

            act.wait_ge(s_const, 1)
            k_high(0, 0)
            q_high(0, 0, 0, 0)
            tk_out(0, 0)
            q_high(1, 0, 1, 0)
            ta_out(0, 0)
            ta_out(1, 1)
            q_high(2, 0, 2, 0)

            def gates_wide(i):
                act.wait_ge(g_m, i + 1)
                act.activation((gwide, gwide2)[i].rearrange("p (b k) d -> p b k d", b=B),
                               g_abs[:, 2 * i:2 * i + 2, :].rearrange("p k b -> p b k").unsqueeze(3).broadcast_to([P, B, 2, P]),
                               ACT.Copy).then_inc(g_wide, 1)

            def gates_out(i, bank):
                act.wait_ge(g_mm, i + 1)
                act.activation(gates[:, 2 * i:2 * i + 2, :].rearrange("p a d -> p (a d)"), ps[:, bank, :],
                               ACT.Copy).then_inc(g_ready, 1)

            def group(g, b, odd, known=None):
                gg, par = 2 * g + b, b
                before = known if known is not None else 2
                after = GROUPS - 1 - known if known is not None else 3
                for j in range(G):
                    n, jp = 4 * gg + j, j % 2
                    exps(n, jp, (0, 1))
                    if j == 2 and after > 0:
                        tk_out(gg + 1, 1 - par)
                    exps(n, jp, (2,))
                    if j > 1 and after == 0:
                        w13_high(0, j - 2)
                    if after > 0 or j < 2:
                        ta_out(n + 2, jp)
                    if j == 1 and after > 0:
                        k_high(gg + 1, 1 - par)
                    if j == 0:
                        v_high(gg, par)
                    if j == 0 and b == 0 and after > 1:
                        wq_high(g + 1, 1 - odd)
                    if known == 0 and j == 0:
                        act.wait_ge(mod_mm, 3)
                    if known == 0 and j == 3:
                        gates_out(0, MISC_BANK)
                    if known == 1 and j == 1:
                        gates_out(1, MISC_BANK + 1)
                    p_high(n, jp)
                    if j == 1 and before > 0:
                        ot_out(2 * gg - 1, 1 - par, 1, MISC_BANK + 1)
                    if j == 0:
                        q_high(n + 3, par, 3, gg)
                    elif after > 0:
                        q_high(n + 3, 1 - par, j - 1, gg + 1)
                    if j == 3:
                        ot_out(2 * gg, par, 0, MISC_BANK)
                    if j == 2 and b == 0:
                        wo_high(g, odd)
                    if known == 0 and j == 2:
                        gates_wide(0)
                    if known == 1 and j == 0:
                        gates_wide(1)

            group(0, 0, 0, 0)
            group(0, 1, 0, 1)
            with act.Fori(1, KVH - 1, 2) as g:
                for odd in (1, 0):
                    group(g + (1 - odd), 0, odd)
                    group(g + (1 - odd), 1, odd)
            group(KVH - 1, 0, 1, GROUPS - 2)
            group(KVH - 1, 1, 1, GROUPS - 1)
            for k in range(DK):
                w13_high(1, k)
            act.activation(b13_h[:, :, :], b13_sb[:, :, :], ACT.Copy).then_inc(fs["wh"], 1)
            act.activation(a13_h[:, :, :, :], a13_sb[:, :, :, :], ACT.Copy).then_inc(fs["wh"], 1)

            def modulate_ffn(b, bank0):
                for k in range(DK):
                    act.wait_ge(xnT_mm, 2 * B + 2 * b + k + 1)
                    act.activation(hT[:, b, k, :], ps[:, bank0 + k, :], ACT.Identity, bias=modT[:, 6 + k, b:b + 1],
                                   scale=modT[:, 8 + k, b:b + 1]).then_inc(fs["h2"], 1)
                    act.activation(hT_h[:, b, k, :], ps[:, bank0 + k, :], ACT.Identity, bias=modT[:, 6 + k, b:b + 1],
                                   scale=modT[:, 8 + k, b:b + 1]).then_inc(fs["h2h"], 1)

            def tm_high(b):
                for i in range(4):
                    act.wait_ge(fs["tm"], 4 * b + i + 1)
                    act.activation(tm_h[:, b, i, :], tm[b][:, i, :], ACT.Copy).then_inc(fs["tmh"], 1)

            def masks_out(b, which):
                for i in which:
                    act.wait_ge(fs["mT_mm"], 5 * b + i + 1)
                    bank = 4 + 2 * b + ((i + 1) % 2 if i < 3 else i - 3)
                    act.activation(maskT[b][:, i, :], ps[:, bank, :], ACT.Copy).then_inc(fs["mT"], 1)

            def weights_wide(b):
                act.wait_ge(fs["dv"], b + 1)
                act.activation(fs1[:, 4, :], fs1[:, 3, :], ACT.Exp).then_inc(fs["ex"], 1)
                if b > 0:
                    act.wait_ge(fs["mT_mm"], 5)
                for i, name in enumerate(("w1", "w2")):
                    act.wait_ge(fs["den"], 3 * b + 2 + i)
                    act.activation(wide[:, 3 + i, :, :], fs1[:, 6 + i, :].unsqueeze(2).broadcast_to([P, T, P]), ACT.Copy)\
                       .then_inc(fs[name], 1)

            root(0, B + 1)
            ot_out(2 * GROUPS - 1, 1, 1, MISC_BANK)
            act.wait_ge(proj_done, 4 * GROUPS)
            modulate_ffn(0, 0)
            weights_wide(0)
            act.wait_ge(fs["wl_v"], 1)
            act.wait_ge(fs["wl_p"], 1)
            masks_out(0, (0, 1, 2))
            tm_high(0)
            masks_out(0, (3, 4))
            for b in range(B):
                for f in range(FT):
                    m = min(P, F - f * P)
                    i = b * FT + f
                    bank = 2 * (i % 2)
                    for s in range(2):
                        act.wait_ge(fs["h_mm"] if s == 0 else fs["d_mm"], 2 * i + 1)
                        wait(act, fs["p"], 2 * i + s - 1)
                        act.activation(sil[0:m, s, :], ps[0:m, bank, :], ACT.Silu).then_inc(fs["silu"], 1)
                        if b == 0 and f == 1 and s == 0:
                            modulate_ffn(1, 6)
                    if b == 0:
                        if f == 0:
                            root(1, B + 2)
                        if f == 2:
                            weights_wide(1)
                            masks_out(1, (0, 1, 2))
                        if f == 3:
                            tm_high(1)
                        if f == 4:
                            masks_out(1, (3, 4))

        @block.vector
        def _(dve):
            dve.wait_ge(c_exp, 1)
            dve.tensor_scalar(c_e[:, :, :], c_e[:, :, :], 1.0, None, ALU.add).then_inc(c_one, 1)
            dve.wait_ge(c_one, 1)
            dve.reciprocal(c_e[:, :, :], c_e[:, :, :]).then_inc(c_rec, 1)
            dve.wait_ge(c_rec, 1)
            dve.tensor_tensor(c_s[:, :, :], c_sb[:, :, :], c_e[:, :, :], ALU.mult).then_inc(c_silu, 1)

            def row_stats(b, base):
                for t in range(T):
                    i = b * T + t
                    dve.bn_stats(stats[:, i, :], xs[:, i, :]).then_inc(ln_stat, 1)
                for t in range(T):
                    i = b * T + t
                    dve.wait_ge(ln_stat, base * T + i + 1)
                    dve.bn_aggr(mv[:, i, :], stats[:, i, :]).then_inc(ln_aggr, 1)
                dve.wait_ge(ln_aggr, (base + b + 1) * T if base == 0 else (B + b + 1) * T)
                dve.tensor_scalar(ve[:, b * T:(b + 1) * T], mv[:, b * T:(b + 1) * T, 1], EPS, None, ALU.add)\
                   .then_inc(ln_eps, 1)

            def normalise(b, rnd, buf):
                c = slice(b * T, (b + 1) * T)
                k = rnd * B + b + 1
                dve.wait_ge(ln_sqrt, k)
                dve.reciprocal(rstd[:, c], sd[:, c]).then_inc(ln_rec, 1)
                dve.wait_ge(ln_rec, k)
                dve.tensor_tensor(nrt[:, c], rstd[:, c], rstd[:, c], ALU.mult).then_inc(ln_n1, 1)
                dve.wait_ge(ln_n1, 3 * k - 2)
                dve.tensor_tensor(nrt[:, c], nrt[:, c], ve[:, c], ALU.mult).then_inc(ln_n1, 1)
                dve.wait_ge(ln_n1, 3 * k - 1)
                dve.tensor_scalar(nrt[:, c], nrt[:, c], -0.5, 1.5, ALU.mult, ALU.add).then_inc(ln_n1, 1)
                dve.wait_ge(ln_n1, 3 * k)
                dve.tensor_tensor(rstd[:, c], rstd[:, c], nrt[:, c], ALU.mult).then_inc(ln_rstd, 1)
                dve.wait_ge(ln_rstd, k)
                for t in range(T):
                    i = b * T + t
                    dve.tensor_scalar(buf[:, t, :], xs[:, i, :], mv[:, i, 0:1], rstd[:, i:i + 1],
                                      ALU.subtract, ALU.mult).then_inc(xn_ready, 1)

            def modulation_out(i, cols, c):
                dve.wait_ge(mod_mm, 2 * i + 1)
                dve.tensor_copy(modT[:, cols, :].rearrange("p c b -> p (c b)"),
                                ps[:, PV_BANK, 2 * cols.start:2 * cols.stop]).then_inc(mod_sb, 1)
                dve.wait_ge(mod_sb, i + 1)
                dve.tensor_scalar(modT[:, c:c + 2, :], modT[:, c:c + 2, :], 1.0, None, ALU.add).then_inc(mod_add, 1)

            dve.wait_ge(ld_x, 16)
            row_stats(0, 0)
            normalise(0, 0, xn)
            modulation_out(0, slice(0, 4), 2)
            dve.wait_ge(ld_x1, 16)
            row_stats(1, 0)
            normalise(1, 0, xn2)

            def rope(g, par, t, bank):
                wait(dve, v_ready, g - 1)
                wait(dve, vh_ready, g - 1)
                wait(dve, rotk_ready, g - 1)
                wait(dve, rotq_ready, 2 * g - 2)
                dve.wait_ge(proj_done, 4 * g + t + 1)
                for o, table in ((ra, cos_sb), (rb, sin_sb)):
                    dve.tensor_tensor(o[:, par, t, 0:ROT].rearrange("p (h c) -> p h c", c=HD),
                                      ps[:, bank, 0:ROT].rearrange("p (h c) -> p h c", c=HD),
                                      table[:, t, :].unsqueeze(1).broadcast_to([P, G + 1, HD]), ALU.mult)
                dve.tensor_copy(ra[:, par, t, ROT:QKV], ps[:, bank, ROT:QKV]).then_inc(rope_done, 1)

            def rotate(par, items, done):
                hw = HD // 2
                for half in range(2):
                    a = ra[:, par, :, 0:ROT].rearrange("p t (h c) -> p t h c", c=HD)[:, :, items, :]
                    s = rb[:, par, :, :].rearrange("p t (h c) -> p t h c", c=HD)[:, :, items, :]
                    lo, hi = half * hw, (1 - half) * hw
                    ins = dve.tensor_tensor(rot[:, :, items, lo:lo + hw], a[:, :, :, lo:lo + hw], s[:, :, :, hi:hi + hw],
                                            ALU.add)
                ins.then_inc(done, 1)

            def rotate_key(g, par):
                wait(dve, kh_ready, g)
                wait(dve, kl_ready, g)
                dve.wait_ge(rope_done, 4 * g + 4)
                rotate(par, slice(G, G + 1), rotk_ready)

            def rotate_queries(g, par, half):
                wait(dve, qh_ready, 4 * g - 2 + 2 * half)
                wait(dve, ql_ready, 4 * g - 2 + 2 * half)
                dve.wait_ge(rope_done, 4 * g + 4)
                rotate(par, slice(2 * half, 2 * half + 2), rotq_ready)

            def row_max(m, mpar, par, item, between=None):
                for f in range(3):
                    wait_apart(dve, s1_done, 3 * m + f + 1, dve_passed)
                    bank = S1_BANK + (mpar + f) % 2
                    off, at = 0, (0, 512, 896)[f]
                    for qt in ([3], [2], [0, 1])[f]:
                        w = (qt + 1) * P
                        ins = dve.tensor_tensor_reduce(junk[:, at + off:at + off + w], ps[:, bank, off:off + w], causal[:, S - w:S], 1.0,
                                                       -3.0e38, ALU.add, ALU.max, mx[:, mpar, qt:qt + 1])
                        off += w
                    ins.then_inc(maxed, 1)
                    if f == 0 and between:
                        between()
                dve.wait_ge(maxed, 3 * m + 3)
                dve.tensor_scalar(src[:, par, item, :, 1, HD:HD + 1], mx[:, mpar, :].unsqueeze(2), -1.0 / SHIFT_UNIT,
                                  SHIFT_BIAS, ALU.mult, ALU.add).then_inc(m_ready, 1)

            def tb_out(m, mpar):
                dve.wait_ge(tb_done, m + 1)
                dve.tensor_copy(qT[:, mpar, 1, :], ps[:, T_BANK, 0:256].bitcast(F16)).then_inc(tb_evac, 1)

            def norm(n, pair, p, half):
                dve.wait_ge(pv_done, n + 1)
                o = ps[:, PV_BANK, 0:T * (HD + 1)].rearrange("p (t c) -> p t c", c=HD + 1)
                dve.reciprocal(rsum[:, :].unsqueeze(2), o[:, :, HD:HD + 1]).then_inc(rsum_ready, 1)
                dve.wait_ge(rsum_ready, n + 1)
                wait(dve, ot_done, pair - 1)
                dve.tensor_tensor(on[:, p, :, half * HD:(half + 1) * HD], o[:, :, 0:HD],
                                  rsum[:, :].unsqueeze(2).broadcast_to([P, T, HD]), ALU.mult).then_inc(normed, 1)

            def ot_low(pair, par, p, bank):
                dve.wait_ge(ot_evac, pair + 1)
                dve.tensor_tensor(oT_l[:, par, p, :], ps[:, bank, :], oT_h[:, par, p, :].bitcast(F32), ALU.subtract)\
                   .then_inc(ot_low_done, 1)

            def op_add(g, b, t, bank):
                a = acc[:, b * T + t, :]
                dve.wait_ge(op_done, 4 * g + t + 1)
                dve.tensor_tensor(a, ps[:, bank, 0:D], a, ALU.add).then_inc(op_added, 1)

            def w1_low():
                dve.wait_ge(fs["wh"], 2)
                dve.tensor_tensor(w13_l[:, 0, :, :], w13_sb[:, 0, :, :], w13_h[:, 0, :, :].bitcast(F32), ALU.subtract)\
                   .then_inc(fs["wl_v"], 1)

            dve.wait_ge(ld_rope, 32)
            dve.wait_ge(s_const, 1)
            dve.wait_ge(xnT_mm, 2)
            for t in range(T):
                rope(0, 0, t, MISC_BANK + t % 2)
            rotate_key(0, 0)
            rotate_queries(0, 0, 0)
            rope(1, 1, 0, MISC_BANK)
            rotate_queries(0, 0, 1)
            rope(1, 1, 1, MISC_BANK + 1)
            row_max(0, 0, 0, 0)
            rope(1, 1, 2, MISC_BANK)
            tb_out(0, 0)

            def gate_values(i):
                c = (4, 10)[i]
                gsrc = modT[:, c:c + 2, :]
                gs, gab = g_sign[:, 2 * i:2 * i + 2, :], g_abs[:, 2 * i:2 * i + 2, :]
                dve.tensor_scalar(gs, gsrc, 0.0, 2.0, ALU.is_ge, ALU.mult).then_inc(g_s, 1)
                dve.wait_ge(g_s, 2 * i + 1)
                dve.tensor_scalar(gs, gs, -1.0, None, ALU.add).then_inc(g_s, 1)
                dve.wait_ge(g_s, 2 * i + 2)
                dve.tensor_tensor(gab, gs, gsrc, ALU.mult).then_inc(g_a, 1)
                dve.wait_ge(g_a, 2 * i + 1)
                dve.tensor_scalar(gab, gab, 0.25, None, ALU.max).then_inc(g_a, 1)
                dve.wait_ge(g_a, 2 * i + 2)
                dve.tensor_tensor(gab, gab, gs, ALU.mult).then_inc(g_m, 1)
            M0, M1 = MISC_BANK, MISC_BANK + 1

            def group(g, b, odd, known=None):
                gg, par = 2 * g + b, b
                before = known if known is not None else 2
                after = GROUPS - 1 - known if known is not None else 3
                for j in range(G):
                    n, jp = 4 * gg + j, j % 2
                    more1, more2 = after > 0 or j < 3, after > 0 or j < 2
                    par1, item1 = (par, j + 1) if j < 3 else (1 - par, 0)
                    par2, item2 = (par, j + 2) if j < 2 else (1 - par, j - 2)
                    def pair_low():
                        if j == 0 and before > 0:
                            ot_low(2 * gg - 2, 1 - par, 0, M0)
                        if j == 2 and before > 0:
                            ot_low(2 * gg - 1, 1 - par, 1, M1)

                    if more1:
                        row_max(n + 1, 1 - jp, par1, item1, pair_low)
                    if j == 1 and after > 0:
                        rotate_key(gg + 1, 1 - par)
                    if before > 0 or j > 1:
                        norm(n - 2, 2 * gg - 1 + j // 2, 1 - j // 2, jp)
                    if j < 3 and before > 1:
                        op_add(gg - 2, b, j + 1, M1 if j < 2 else M0)
                    if j == 3 and before > 0:
                        op_add(gg - 1, 1 - b, 0 if after else 1, M0)
                    if j > 1 and after == 0:
                        op_add(gg - 1, 1 - b, 2 * j - 4, M1)
                    if more1 and not (j == 2 and after > 0):
                        tb_out(n + 1, 1 - jp)
                    if j == 2 and after > 0:
                        tb_out(n + 1, 1 - jp)
                    if j in (1, 3) and after > 0:
                        rotate_queries(gg + 1, 1 - par, j // 2)
                    if j == 0 and after > 0:
                        rope(gg + 1, 1 - par, 3, M0)
                    if j > 0 and after > 1:
                        rope(gg + 2, par, j - 1, M0 if j == 1 else M1)
                    if j == 3 and after == 0:
                        w1_low()
                    if known == 0 and j == 0:
                        modulation_out(1, slice(4, 12), 8)
                    if known == 0 and j in (1, 3):
                        gate_values(j // 2)

            group(0, 0, 0, 0)
            group(0, 1, 0, 1)
            with dve.Fori(1, KVH - 1, 2) as g:
                for odd in (1, 0):
                    group(g + (1 - odd), 0, odd)
                    group(g + (1 - odd), 1, odd)
            group(KVH - 1, 0, 1, GROUPS - 2)
            group(KVH - 1, 1, 1, GROUPS - 1)
            L = GROUPS - 1

            def residual(b):
                a, xb = acc[:, b * T:(b + 1) * T, :], xs[:, b * T:(b + 1) * T, :]
                dve.tensor_tensor(a, a, gates[:, b, :].unsqueeze(1).broadcast_to([P, T, D]), ALU.mult).then_inc(r_mul, 1)
                dve.wait_ge(r_mul, b + 1)
                dve.tensor_tensor(xb, xb, a, ALU.add).then_inc(r_add, 1)
                dve.wait_ge(r_add, b + 1)

            norm(HEADS - 2, 2 * L + 1, 1, 0)
            ot_low(2 * L, 1, 0, M0)
            op_add(L - 1, 0, 3, M1)
            dve.wait_ge(op_added, 4 * L)
            residual(0)
            row_stats(0, B)
            norm(HEADS - 1, 2 * L + 1, 1, 1)
            normalise(0, 1, xn_f[:, 0])
            ot_low(2 * L + 1, 1, 1, M0)
            for t in range(2):
                op_add(L, 1, t, MISC_BANK + (t + 1) % 2)
            for k in range(DK):
                dve.wait_ge(fs["h2h"], k + 1)
                dve.tensor_tensor(hT_l[:, 0, k, :], hT[:, 0, k, :], hT_h[:, 0, k, :].bitcast(F32), ALU.subtract)\
                   .then_inc(fs["h2l"], 1)

            def one(i):
                return fsm[:, i, :, :]

            def col(i):
                return fs1[:, i, :].unsqueeze(2).broadcast_to([P, T, E])
            revb = rev[:, :].unsqueeze(1).broadcast_to([P, T, E])

            def first_max(k, logits, oh, vmax, names, scratch):
                s_v, s_eq, s_rv, s_fi, s_oh = names
                dve.tensor_reduce(fs1[:, vmax, :], one(logits), AX.X, ALU.max).then_inc(fs[s_v], 1)
                dve.wait_ge(fs[s_v], k)
                dve.tensor_tensor(one(scratch), one(logits), col(vmax), ALU.is_equal).then_inc(fs[s_eq], 1)
                dve.wait_ge(fs[s_eq], k)
                dve.tensor_tensor(one(scratch + 1), one(scratch), revb, ALU.mult).then_inc(fs[s_rv], 1)
                dve.wait_ge(fs[s_rv], k)
                dve.tensor_reduce(fs1[:, vmax + 8, :], one(scratch + 1), AX.X, ALU.max).then_inc(fs[s_fi], 1)
                dve.wait_ge(fs[s_fi], k)
                dve.tensor_tensor(one(oh), one(scratch + 1), col(vmax + 8), ALU.is_equal).then_inc(fs[s_oh], 1)
                dve.wait_ge(fs[s_oh], k)

            def first_choice(b):
                k = b + 1
                dve.wait_ge(fs["gate_mm"], k)
                dve.tensor_copy(one(0).rearrange("p t e -> p (t e)"), ps[:, 4 + 2 * b, 0:T * E]).then_inc(fs["lg"], 1)
                dve.wait_ge(fs["lg"], k)
                first_max(k, 0, 1, 0, ("v1", "eq", "rv", "fi", "oh1"), 4)
                dve.scalar_tensor_tensor(out=one(2), in0=one(1), scalar=-3.0e38, in1=one(0), op0=ALU.mult, op1=ALU.add)\
                   .then_inc(fs["mk2"], 1)
                dve.wait_ge(fs["mk2"], k)

            def second_choice(b):
                k = b + 1
                first_max(k, 2, 3, 1, ("v2", "eq2", "rv2", "fi2", "oh2"), 6)
                dve.tensor_tensor(fs1[:, 3, :], fs1[:, 1, :], fs1[:, 0, :], ALU.subtract).then_inc(fs["dv"], 1)
                if b > 0:
                    dve.wait_ge(fs["mT_mm"], 5)
                for i, oh in enumerate((1, 3)):
                    o = wide[:, i, :, :].rearrange("p t (e r) -> p t e r", r=R)
                    dve.tensor_scalar(o, one(oh).unsqueeze(3).broadcast_to([P, T, E, R]), LORA_SCALE, None, ALU.mult)\
                       .then_inc(fs["wide"], 1)
                dve.wait_ge(fs["wide"], 2 * b + 2)
                dve.tensor_tensor(wide[:, 2, :, :], wide[:, 1, :, :], wide[:, 0, :, :], ALU.subtract).then_inc(fs["dwide"], 1)

            def weights(b):
                k = b + 1
                dve.wait_ge(fs["ex"], k)
                dve.tensor_scalar(fs1[:, 5, :], fs1[:, 4, :], 1.0, None, ALU.add).then_inc(fs["den"], 1)
                dve.wait_ge(fs["den"], 3 * b + 1)
                dve.reciprocal(fs1[:, 6, :], fs1[:, 5, :]).then_inc(fs["den"], 1)
                dve.wait_ge(fs["den"], 3 * b + 2)
                dve.tensor_tensor(fs1[:, 7, :], fs1[:, 4, :], fs1[:, 6, :], ALU.mult).then_inc(fs["den"], 1)

            def mask_inputs(b):
                dve.wait_ge(fs["mT"], 5 * b + 3)
                if b > 0:
                    dve.wait_ge(r_add, B)
                for i in range(4):
                    dve.wait_ge(fs["t_mm"], 2 * b + min(i, 1) + 1)
                    dve.tensor_tensor(tm[b][:, i, :], ps[:, 4 + 2 * b + i % 2, :], maskT[b][:, i - i % 2, :], ALU.mult)\
                       .then_inc(fs["tm"], 1)
                for i in range(2):
                    dve.wait_ge(fs["tmh"], 4 * b + i + 1)
                    dve.tensor_tensor(tm_l[:, b, i, :], tm[b][:, i, :], tm_h[:, b, i, :].bitcast(F32), ALU.subtract)\
                       .then_inc(fs["tml"], 1)

            first_choice(0)
            second_choice(0)
            weights(0)
            for t in (2, 3):
                op_add(L, 1, t, MISC_BANK + (t + 1) % 2)
            mask_inputs(0)
            dve.wait_ge(op_added, 4 * GROUPS)
            residual(1)
            dve.wait_ge(fs["wl_p"], 2)
            dve.wait_ge(fs["mT"], 5)

            def activation_product(b, f, s):
                m, i = min(P, F - f * P), b * FT + f
                bank, q = 2 * (i % 2), 2 * i + s
                dve.wait_ge(fs["silu"], q + 1)
                dve.wait_ge(fs["h_mm"] if s == 0 else fs["d_mm"], 2 * i + 2)
                dve.tensor_tensor(pr[0:m, s, :], ps[0:m, bank + 1, :], sil[0:m, s, :], ALU.mult).then_inc(fs["p"], 1)
                dve.wait_ge(fs["p"], q + 1)
                wait(dve, fs["z_mm"], q - 1)
                if i > 0:
                    dve.wait_ge(fs["g"], i)
                if i == FT:
                    dve.wait_ge(fs["mT"], 10)
                dve.tensor_tensor(av[0:m, s, :], pr[0:m, s, :], maskT[b][0:m, 3 + s, :], ALU.mult).then_inc(fs["a"], 1)

            def store_sum(b):
                gb = gates[:, B + b, :].unsqueeze(1).broadcast_to([P, 2, D])
                for i in range(2):
                    q = 2 * b + i
                    dve.wait_ge(fs["o_mm"], q + 1)
                    y = (y1, y2)[i]
                    dve.tensor_tensor(y, ps[:, 6 + i, :].rearrange("p (t d) -> p t d", t=2), gb, ALU.mult).then_inc(fs["og"], 1)
                    dve.wait_ge(fs["og"], q + 1)
                    xb = xs[:, 2 * q:2 * q + 2, :]
                    dve.tensor_tensor(xb, xb, y, ALU.add).then_inc(fs["o"], 1)

            for b in range(B):
                for f in range(FT):
                    activation_product(b, f, 0)
                    if b == 1 and f == 0:
                        store_sum(0)
                    if b == 0 and f == 2:
                        second_choice(1)
                    activation_product(b, f, 1)
                    if b == 0:
                        if f == 0:
                            row_stats(1, B)
                            normalise(1, 1, xn_f[:, 1])
                        if f == 1:
                            first_choice(1)
                        if f == 2:
                            weights(1)
                        if f == 3:
                            mask_inputs(1)
                dve.wait_ge(fs["z_mm"], 2 * FT * (b + 1))
                if b > 0:
                    dve.wait_ge(fs["o_mm"], 2)
                for s in range(2):
                    dve.tensor_tensor(uT[:, s, :], ps[:, 4 + s, :], maskT[b][:, s, :], ALU.mult).then_inc(fs["zm"], 1)
                dve.wait_ge(fs["zm"], 2 * b + 2)
                dve.tensor_tensor(uT[:, 1, :], uT[:, 1, :], uT[:, 0, :], ALU.add).then_inc(fs["u"], 1)
            store_sum(1)

        @block.gpsimd
        def _(pool):
            k_ones = sem("k_ones")
            pool.memset(ident[:, :], 0.0).then_inc(k_ones, 1)
            pool.memset(ident16[:, :], 0.0).then_inc(k_ones, 1)
            pool.memset(causal[:, :], 0.0).then_inc(k_ones, 1)
            pool.memset(src[:, :, :, :, :, :].rearrange("p a b c d e -> p (a b c d e)").bitcast(F32), 0.0).then_inc(k_ones, 1)
            pool.memset(vh[:, :, :, HD:HD + 1], 1.0).then_inc(k_ones, 1)
            pool.memset(acc[:, :, :], 0.0).then_inc(acc_zero, 1)
            for e in range(E):
                pool.memset(rev[:, e:e + 1], float(E - e)).then_inc(k_ones, 1)
            n_ones = 5 + E
            pool.wait_ge(k_ones, n_ones)
            for m in (ident, ident16):
                pool.affine_select(out=m[:, :], in_=m[:, :], compare_op=ALU.not_equal, fill=1.0, base=0,
                                   pattern=[[-1, P]], channel_multiplier=1).then_inc(k_ones, 1)
            diag = causal[:, S - P:S]
            pool.affine_select(out=diag, in_=diag, compare_op=ALU.is_ge, fill=MASKED, base=0,
                               pattern=[[-1, P]], channel_multiplier=1).then_inc(k_ones, 1)
            pool.memset(src[:, :, G, :, 1, HD:HD + 1], SHIFT_UNIT).then_inc(k_ones, 1)
            pool.wait_ge(k_ones, n_ones + 4)
            pool.wait_ge(acc_zero, 1)
            pool.memset(rsum[:, :], 0.0).then_inc(s_const, 1)

            def v_low(g, par):
                pool.wait_ge(vh_ready, g + 1)
                pool.tensor_tensor(vl[:, par, :, :], ra[:, par, :, ROT:QKV], vh[:, par, :, 0:HD], ALU.subtract)\
                    .then_inc(v_ready, 1)

            def k_low(g, par):
                pool.wait_ge(kh_ready, g + 1)
                pool.tensor_tensor(src[:, par, G, :, 0, HD:P], rot[:, :, G, :], src[:, par, G, :, 0, 0:HD],
                                   ALU.subtract).then_inc(kl_ready, 1)

            def q_low(m, par, item):
                pool.wait_ge(qh_ready, m + 1)
                pool.tensor_tensor(src[:, par, item, :, 1, 0:HD], rot[:, :, item, :], src[:, par, item, :, 0, 0:HD],
                                   ALU.subtract).then_inc(ql_ready, 1)

            def causal_zero(n, npar):
                for off, step, need in ((0, 512, 2), (896, 256, 3)):
                    wait_apart(pool, exp_done, 3 * n + need, pool_passed)
                    if step == 512:
                        v = prob[:, npar, 0:1024].rearrange("p (a c) -> p a c", a=2)[:, :, 0:P]
                    else:
                        v = prob[:, npar, 896:1280].rearrange("p (a c) -> p a c", a=3)[:, 0:3:2, :]
                    ins = pool.affine_select(out=v, in_=v, compare_op=ALU.is_ge, fill=0.0, base=0,
                                             pattern=[[0, 2], [1, P]], channel_multiplier=-1)
                ins.then_inc(sel_done, 1)

            def p_low(n, npar):
                pool.wait_ge(ph_ready, n + 1)
                wait(pool, pv_done, n - 1)
                pool.tensor_tensor(pl[:, npar, :], prob[:, npar, :], ph[:, npar, :], ALU.subtract).then_inc(pl_ready, 1)

            def w_low(lo, w, place, high, g, ready, done):
                pool.wait_ge(ready, g + 1)
                pool.tensor_tensor(lo[:, place, :, :], w[:, :, :], high[:, place, :, :].bitcast(F32), ALU.subtract)\
                    .then_inc(done, 1)

            def wq_low(g, place):
                w_low(wq_l, wq_sb, place, wq_h, g, wqh_ready, wql_ready)

            def wo_low(g, place):
                w_low(wo_l, wo_sb, place, wo_h, g, woh_ready, wol_ready)

            def input_low_first(b):
                pool.wait_ge(hh_ready, b + 1)
                pool.tensor_tensor(hT_l[:, b, :, :], hT[:, b, :, :], hT_h[:, b, :, :].bitcast(F32), ALU.subtract)\
                    .then_inc(hl_ready, 1)

            input_low_first(0)
            k_low(0, 0)
            q_low(0, 0, 0)
            q_low(1, 0, 1)
            input_low_first(1)
            wq_low(0, 0)

            def group(g, b, odd, known=None):
                gg, par = 2 * g + b, b
                after = GROUPS - 1 - known if known is not None else 3
                for j in range(G):
                    n, jp = 4 * gg + j, j % 2
                    par2, item2 = (par, j + 2) if j < 2 else (1 - par, j - 2)
                    causal_zero(n, jp)
                    if j < 2 or after > 0:
                        q_low(n + 2, par2, item2)
                    if j == 0:
                        v_low(gg, par)
                    if j == 1 and after > 0:
                        k_low(gg + 1, 1 - par)
                    if j == 0 and b == 0 and after > 1:
                        wq_low(g + 1, 1 - odd)
                    p_low(n, jp)
                    if j == 2 and b == 0:
                        wo_low(g, odd)

            group(0, 0, 0, 0)
            group(0, 1, 0, 1)
            with pool.Fori(1, KVH - 1, 2) as g:
                for odd in (1, 0):
                    group(g + (1 - odd), 0, odd)
                    group(g + (1 - odd), 1, odd)
            group(KVH - 1, 0, 1, GROUPS - 2)
            group(KVH - 1, 1, 1, GROUPS - 1)
            def low(out, value, high, done):
                pool.tensor_tensor(out, value, high.bitcast(F32), ALU.subtract).then_inc(fs[done], 1)

            def input_low(b):
                for k in range(DK):
                    pool.wait_ge(fs["h2h"], 2 * b + k + 1)
                    low(hT_l[:, b, k, :], hT[:, b, k, :], hT_h[:, b, k, :], "h2l")

            def difference_low(b):
                for i in (2, 3):
                    pool.wait_ge(fs["tmh"], 4 * b + i + 1)
                    low(tm_l[:, b, i, :], tm[b][:, i, :], tm_h[:, b, i, :], "tmd_l")

            pool.wait_ge(fs["wh"], 4)
            low(w13_l[:, 1, :, :], w13_sb[:, 1, :, :], w13_h[:, 1, :, :], "wl_p")
            pool.wait_ge(fs["wh"], 5)
            low(b13_l[:, :, :], b13_sb[:, :, :], b13_h[:, :, :], "wl_p")
            pool.wait_ge(fs["wh"], 6)
            low(a13_l[:, :, :, :], a13_sb[:, :, :, :], a13_h[:, :, :, :], "wl_p")
            difference_low(0)
            for i in range(B * FT):
                f = i % FT
                m = min(P, F - f * P)
                pool.wait_ge(fs["a"], 2 * i + 2)
                if i == 0:
                    pool.wait_ge(fs["tml"], 2)
                    pool.wait_ge(fs["tmh"], 4)
                    pool.wait_ge(fs["tmd_l"], 2)
                elif f == 0:
                    pool.wait_ge(fs["o_mm"], 2)
                pool.tensor_tensor(gsum[0:m, f, :], av[0:m, 0, :], av[0:m, 1, :], ALU.add).then_inc(fs["g"], 1)
                if i == 1:
                    input_low(1)
                if i == 3:
                    difference_low(1)


def kernel(L0_attn_hidden_states, L0_attn_Wq, L0_attn_Wk, L0_attn_Wv, L0_attn_Wo, L0_ffn_gate_w, L0_ffn_w1,
           L0_ffn_w3, L0_ffn_w2, L0_ffn_a1, L0_ffn_b1, L0_ffn_a3, L0_ffn_b3, L0_ffn_a2, L0_ffn_b2, L0_c, L0_wmod):
    import concourse.bacc as bacc
    from concourse.bass_utils import run_bass_kernel_spmd

    def con(a):
        return np.ascontiguousarray(a)

    def by_width(a):
        a = np.asarray(a)
        return con(a.T.reshape(-1, P, a.shape[0]).transpose(1, 0, 2))

    wq = np.asarray(L0_attn_Wq).reshape(KVH, G * HD, D)
    wk = np.asarray(L0_attn_Wk).reshape(KVH, HD, D)
    wv = np.asarray(L0_attn_Wv).reshape(KVH, HD, D)
    wqkv = np.concatenate([wq, wk, wv], axis=1)
    wqkv = con(wqkv.transpose(0, 2, 1).reshape(KVH, DK, P, QKV).transpose(0, 2, 1, 3))
    wo = con(np.asarray(L0_attn_Wo).T.reshape(H // 2, P, D).transpose(1, 0, 2))
    inv = (np.float32(1.0) / np.float32(10000.0) ** (np.arange(0, HD, 2, dtype=np.float32) / np.float32(HD)))
    ang = np.arange(S, dtype=np.float32)[:, None] * inv.astype(np.float32)[None, :]
    c1, s1 = np.cos(ang).astype(np.float32), np.sin(ang).astype(np.float32)
    cos = np.concatenate([c1, c1], 1)
    sin = np.concatenate([s1, -s1], 1)
    by_token = lambda a: con(a.reshape(T, P, -1).transpose(1, 0, 2))
    a1, a3, a2 = (np.asarray(v) for v in (L0_ffn_a1, L0_ffn_a3, L0_ffn_a2))
    b1, b3, b2 = (con(np.asarray(v).transpose(0, 2, 1).reshape(E * R, -1)) for v in (L0_ffn_b1, L0_ffn_b3, L0_ffn_b2))
    arrays = {
        "x": con(L0_attn_hidden_states), "wqkv": wqkv, "wo": wo, "cos": by_token(cos), "sin": by_token(sin),
        "cT": by_width(L0_c), "wmod": con(np.asarray(L0_wmod).reshape(DK, P, 6 * D).transpose(1, 0, 2)),
        "w1T": by_width(L0_ffn_w1), "w3T": by_width(L0_ffn_w3), "w2T": con(np.asarray(L0_ffn_w2).T),
        "gateT": by_width(L0_ffn_gate_w), "a1T": by_width(a1.reshape(E * R, D)), "a3T": by_width(a3.reshape(E * R, D)),
        "b1T": b1, "b3T": b3, "a2T": con(a2.reshape(E * R, F).T), "b2T": b2,
    }
    nc = bacc.Bacc("TRN2", target_bir_lowering=False, num_devices=1)
    args = [nc.dram_tensor(k, a.shape, mybir.dt.from_np(a.dtype), kind="ExternalInput").ap() for k, a in arrays.items()]
    args.append(nc.dram_tensor("out", (B, S, D), F32, kind="ExternalOutput").ap())
    block_kernel(nc, *args)
    r = run_bass_kernel_spmd(nc, [arrays], core_ids=[0])
    return r.results[0]["out"]
```
